# Optimizing a Trainium2 kernel written in Bass

```python
import numpy as np
import jax
import jax.numpy as jnp

def _softmax(x, axis=-1):
    return jax.nn.softmax(x, axis=axis)

def _gelu(x):
    return jax.nn.gelu(x, approximate=True)

def _silu(x):
    return jax.nn.silu(x)

def _sigmoid(x):
    return jax.nn.sigmoid(x)

def _layernorm(x, axis=-1, eps=1e-05):
    m = jnp.mean(x, axis=axis, keepdims=True)
    v = jnp.var(x, axis=axis, keepdims=True)
    return (x - m) / jnp.sqrt(v + eps)

def _scatter_add(tgt, idx, src, axis=0):
    return tgt.at[idx].add(src)

def _segment_sum(src, seg, n):
    return jax.ops.segment_sum(src, seg, n)
kernel_name = 'mk_xattn_ffn_d4_seqx_r4_92dd27'

def setup_inputs(seed: int=0):
    np.random.seed(seed)
    _w = jnp.asarray

    def _rec_inputs():
        import jax
        import jax.numpy as jnp
        _rk = jax.random.key(seed)
        x = -0.0002928 + 1 * jax.random.normal(jax.random.fold_in(_rk, 1), (2, 1024, 256), jnp.float32)
        _lenS = 1024 - jax.random.randint(jax.random.fold_in(_rk, 7), (2,), 0, max(1, 1024 // 4) + 1, jnp.int32)
        _lenS2 = 77 - jax.random.randint(jax.random.fold_in(_rk, 8), (2,), 0, max(1, 77 // 4) + 1, jnp.int32)
        _ctx_768P = jax.random.normal(jax.random.fold_in(_rk, 11), (2, 16, 192), jnp.float32)
        _ctx_768c = jax.random.dirichlet(jax.random.fold_in(_rk, 511), 0.3 * jnp.ones((16,), jnp.float32), (2, 77))
        _ctx_768t = jnp.einsum('bsk,bkd->bsd', _ctx_768c, _ctx_768P)
        _ctx_768t = _ctx_768t * jax.lax.rsqrt(jnp.mean(jnp.square(_ctx_768t)) + 1e-12) * 0.953939
        ctx_768 = 2.09791e-05 + 1.00001 * (_ctx_768t + 0.3 * jax.random.normal(jax.random.fold_in(_rk, 611), (2, 77, 192), jnp.float32))
        _validS = jnp.arange(1024)[None, :] < _lenS[:, None]
        _validS2 = jnp.arange(77)[None, :] < _lenS2[:, None]
        _causal = jnp.tril(jnp.ones((1024, 1024), dtype=bool))
        mask_BxS2_bf1 = jnp.ones((2, 77), dtype=bool)
        mask_BxS_bf1 = jnp.ones((2, 1024), dtype=bool)
        return (x, ctx_768, mask_BxS2_bf1, mask_BxS_bf1)
    x, ctx_768, mask_BxS2_bf1, mask_BxS_bf1 = _rec_inputs()

    def _L0_xattn_setup():
        import jax, jax.numpy as jnp
        import numpy as np
        H = 8
        D = 64
        SCALE = D ** (-0.5)
        key = jax.random.key(seed)
        ks = jax.random.split(key, 7)
        B, Nq, Nkv = (2, 512, 512)
        Cq, Ck, I = (256, 192, H * D)
        return {'x': jax.random.normal(ks[0], (B, Nq, Cq), jnp.float32), 'context': jax.random.normal(ks[1], (B, Nkv, Ck), jnp.float32), 'Wq': jax.random.normal(ks[2], (Cq, I), jnp.float32) * Cq ** (-0.5), 'Wk': jax.random.normal(ks[3], (Ck, I), jnp.float32) * Ck ** (-0.5), 'Wv': jax.random.normal(ks[4], (Ck, I), jnp.float32) * Ck ** (-0.5), 'Wo': jax.random.normal(ks[5], (I, Cq), jnp.float32) * I ** (-0.5), 'bo': jnp.zeros((Cq,), jnp.float32)}
    _L0_xattn_all = _L0_xattn_setup()
    _L0_xattn_in = {k: v for k, v in _L0_xattn_all.items() if k in ('Wq', 'Wk', 'Wv', 'Wo', 'bo')}
    del _L0_xattn_all

    def _L0_ffn_setup():
        import jax, jax.numpy as jnp
        import numpy as np
        HIDDEN = 256
        N_EXPERTS = 32
        MOE_I = 128
        N_GROUP = 4
        TOPK_GROUP = 2
        TOP_K = 6
        N_LOCAL_GROUPS = 16
        ANCHOR_I = 64
        SHARED_I = 128
        ROUTED_SCALE = 0.2
        ANCHOR_ALPHA = 0.1
        BATCH, SEQ = (1, 256)

        def _moe_forward(hidden_states, gate_weight, gate_bias, w_gate, w_up, w_down, shared_w_gate, shared_w_up, shared_w_down, anchor_w_gate, anchor_w_up, anchor_w_down):
            B, S, H = hidden_states.shape
            x = hidden_states.reshape(-1, H)
            T = x.shape[0]
            E = gate_weight.shape[0]
            L = anchor_w_gate.shape[0]
            logits = x @ gate_weight.T
            scores = jax.nn.sigmoid(logits)
            sc = scores + gate_bias
            grp = sc.reshape(T, N_GROUP, E // N_GROUP)
            group_scores = jax.lax.top_k(grp, 2)[0].sum(-1)
            _, gidx = jax.lax.top_k(group_scores, TOPK_GROUP)
            gmask = jax.nn.one_hot(gidx, N_GROUP, dtype=sc.dtype).sum(1)
            emask = jnp.repeat(gmask, E // N_GROUP, axis=1)
            masked = jnp.where(emask > 0, sc, -jnp.inf)
            _, topidx = jax.lax.top_k(masked, TOP_K)
            tw = jnp.take_along_axis(scores, topidx, axis=-1)
            tw = tw / (tw.sum(-1, keepdims=True) + 1e-20) * ROUTED_SCALE
            g = jnp.einsum('th,ehi->tei', x, w_gate)
            u = jnp.einsum('th,ehi->tei', x, w_up)
            eo = jnp.einsum('tei,eih->teh', jax.nn.silu(g) * u, w_down)
            cw = (jax.nn.one_hot(topidx, E, dtype=x.dtype) * tw[..., None]).sum(1)
            routed = jnp.einsum('te,teh->th', cw, eo)
            shared = jax.nn.silu(x @ shared_w_gate) * (x @ shared_w_up) @ shared_w_down
            lg = topidx[:, 0] // (E // L)
            ag = jnp.einsum('th,lhi->tli', x, anchor_w_gate)
            au = jnp.einsum('th,lhi->tli', x, anchor_w_up)
            ao = jnp.einsum('tli,lih->tlh', jax.nn.silu(ag) * au, anchor_w_down)
            acw = jax.nn.one_hot(lg, L, dtype=x.dtype)
            anchor = jnp.einsum('tl,tlh->th', acw, ao)
            out = routed + shared + ANCHOR_ALPHA * anchor
            return out.reshape(B, S, H)
        key = jax.random.key(seed)
        ks = jax.random.split(key, 13)
        s = 0.02
        return {'hidden_states': jax.random.normal(ks[0], (BATCH, SEQ, HIDDEN), jnp.float32), 'gate_weight': s * jax.random.normal(ks[1], (N_EXPERTS, HIDDEN), jnp.float32), 'gate_bias': s * jax.random.normal(ks[2], (N_EXPERTS,), jnp.float32), 'w_gate': s * jax.random.normal(ks[3], (N_EXPERTS, HIDDEN, MOE_I), jnp.float32), 'w_up': s * jax.random.normal(ks[4], (N_EXPERTS, HIDDEN, MOE_I), jnp.float32), 'w_down': s * jax.random.normal(ks[5], (N_EXPERTS, MOE_I, HIDDEN), jnp.float32), 'shared_w_gate': s * jax.random.normal(ks[6], (HIDDEN, SHARED_I), jnp.float32), 'shared_w_up': s * jax.random.normal(ks[7], (HIDDEN, SHARED_I), jnp.float32), 'shared_w_down': s * jax.random.normal(ks[8], (SHARED_I, HIDDEN), jnp.float32), 'anchor_w_gate': s * jax.random.normal(ks[9], (N_LOCAL_GROUPS, HIDDEN, ANCHOR_I), jnp.float32), 'anchor_w_up': s * jax.random.normal(ks[10], (N_LOCAL_GROUPS, HIDDEN, ANCHOR_I), jnp.float32), 'anchor_w_down': s * jax.random.normal(ks[11], (N_LOCAL_GROUPS, ANCHOR_I, HIDDEN), jnp.float32)}
    _L0_ffn_all = _L0_ffn_setup()
    _L0_ffn_in = {k: v for k, v in _L0_ffn_all.items() if k in ('gate_weight', 'gate_bias', 'w_gate', 'w_up', 'w_down', 'shared_w_gate', 'shared_w_up', 'shared_w_down', 'anchor_w_gate', 'anchor_w_up', 'anchor_w_down')}
    del _L0_ffn_all

    def _L1_xattn_setup():
        import jax, jax.numpy as jnp
        import numpy as np
        DIM = 256
        CTX_DIM = 192
        HEADS = 16
        key = jax.random.key(seed)
        ks = jax.random.split(key, 7)
        B, N, M = (4, 1024, 64)
        x = jax.random.normal(ks[0], (B, N, DIM), dtype=jnp.float32)
        context = jax.random.normal(ks[1], (B, M, CTX_DIM), dtype=jnp.float32)
        context_mask = jnp.ones((B, M), dtype=bool)
        s_d = 1.0 / np.sqrt(DIM)
        s_c = 1.0 / np.sqrt(CTX_DIM)
        Wq = jax.random.normal(ks[2], (DIM, DIM), dtype=jnp.float32) * s_d
        Wk = jax.random.normal(ks[3], (CTX_DIM, DIM), dtype=jnp.float32) * s_c
        Wv = jax.random.normal(ks[4], (CTX_DIM, DIM), dtype=jnp.float32) * s_c
        Wo = jax.random.normal(ks[5], (DIM, DIM), dtype=jnp.float32) * s_d
        return {'x': x, 'context': context, 'context_mask': context_mask, 'Wq': Wq, 'Wk': Wk, 'Wv': Wv, 'Wo': Wo}
    _L1_xattn_all = _L1_xattn_setup()
    _L1_xattn_in = {k: v for k, v in _L1_xattn_all.items() if k in ('Wq', 'Wk', 'Wv', 'Wo')}
    del _L1_xattn_all

    def _L1_ffn_setup():
        import jax, jax.numpy as jnp
        import numpy as np
        H = 8
        KD = 128
        TOPK = 8
        NUM_KEYS = 64
        N_EXPERTS = NUM_KEYS * NUM_KEYS
        N_DIM = 256
        BN_EPS = 1e-05

        def gelu_new(x):
            c = jnp.sqrt(jnp.asarray(2.0 / jnp.pi, x.dtype))
            return 0.5 * x * (1.0 + jnp.tanh(c * (x + 0.044715 * x * x * x)))
        key = jax.random.key(seed)
        ks = jax.random.split(key, 5)
        b, s = (2, 256)
        x = jax.random.normal(ks[0], (b, s, N_DIM), dtype=jnp.float32)
        w_q = jax.random.normal(ks[1], (N_DIM, 2 * H * KD), dtype=jnp.float32) * 0.02
        bn_gamma = jnp.ones((2 * H * KD,), dtype=jnp.float32)
        bn_beta = jnp.zeros((2 * H * KD,), dtype=jnp.float32)
        keys = jax.random.normal(ks[2], (H, NUM_KEYS, 2, KD), dtype=jnp.float32) * 0.02
        down_embed = jax.random.normal(ks[3], (N_EXPERTS, N_DIM), dtype=jnp.float32) * 0.02
        up_embed = jax.random.normal(ks[4], (N_EXPERTS, N_DIM), dtype=jnp.float32) * 0.02
        return {'x': x, 'w_q': w_q, 'bn_gamma': bn_gamma, 'bn_beta': bn_beta, 'keys': keys, 'down_embed': down_embed, 'up_embed': up_embed}
    _L1_ffn_all = _L1_ffn_setup()
    _L1_ffn_in = {k: v for k, v in _L1_ffn_all.items() if k in ('w_q', 'bn_gamma', 'bn_beta', 'keys', 'down_embed', 'up_embed')}
    del _L1_ffn_all

    def _L2_xattn_setup():
        import jax, jax.numpy as jnp
        import numpy as np
        B, T, DT, G, DV = (16, 128, 256, 144, 192)
        H, DH = (4, 32)
        INNER = H * DH
        HID = 4 * DT
        N_STATE = 64
        K_TOP = 32

        def layernorm(x, g, b, eps=1e-05):
            m = x.mean(-1, keepdims=True)
            v = x.var(-1, keepdims=True)
            return (x - m) * jax.lax.rsqrt(v + eps) * g + b

        def s4d(x, log_dt, A_re, A_im, C_re, C_im, D_skip):
            Bb, L, D = x.shape
            dt = jnp.exp(log_dt)
            A = A_re + 1j * A_im
            C = C_re + 1j * C_im
            dtA = dt[:, None] * A
            dC = C * (jnp.exp(dtA) - 1.0) / A
            powers = jnp.exp(dtA[:, :, None] * jnp.arange(L))
            K = 2.0 * jnp.einsum('dn,dnl->dl', dC, powers).real
            n = 2 * L
            Kf = jnp.fft.rfft(K, n=n, axis=-1)
            xf = jnp.fft.rfft(x, n=n, axis=1)
            y = jnp.fft.irfft(xf * Kf.T[None], n=n, axis=1)[:, :L]
            return y + x * D_skip
        key = jax.random.key(seed)
        ks = jax.random.split(key, 16)
        s = 0.02
        inp = {'x_text': jax.random.normal(ks[0], (B, T, DT), jnp.float32), 'x_vision': jax.random.normal(ks[1], (B, G, DV), jnp.float32), 'text_mask': jnp.ones((B, T), bool), 'vision_mask': jnp.ones((B, G), bool), 'Wq': jax.random.normal(ks[2], (DT, INNER), jnp.float32) * s, 'Wk': jax.random.normal(ks[3], (DV, INNER), jnp.float32) * s, 'Wv': jax.random.normal(ks[4], (DV, DT), jnp.float32) * s, 'W_film_in': jax.random.normal(ks[5], (DT, 2 * DT), jnp.float32) * s, 'b_film_in': jnp.zeros((2 * DT,), jnp.float32), 'W_film_out': jax.random.normal(ks[6], (DT, 2 * DT), jnp.float32) * s, 'b_film_out': jnp.zeros((2 * DT,), jnp.float32), 'g_norm_in': jnp.ones((DT,), jnp.float32), 'b_norm_in': jnp.zeros((DT,), jnp.float32), 'g_norm_out': jnp.ones((DT,), jnp.float32), 'b_norm_out': jnp.zeros((DT,), jnp.float32), 'g_ffn': jnp.ones((DT,), jnp.float32), 'b_ffn': jnp.zeros((DT,), jnp.float32), 'W1': jax.random.normal(ks[7], (DT, HID), jnp.float32) * s, 'b1': jnp.zeros((HID,), jnp.float32), 'W2': jax.random.normal(ks[8], (HID, DT), jnp.float32) * s, 'b2': jnp.zeros((DT,), jnp.float32), 'log_dt': jnp.log(0.001) + jax.random.uniform(ks[9], (DT,), jnp.float32) * (jnp.log(0.1) - jnp.log(0.001)), 'A_re': -0.5 * jnp.ones((DT, N_STATE), jnp.float32), 'A_im': jnp.tile(jnp.pi * jnp.arange(N_STATE, dtype=jnp.float32), (DT, 1)), 'C_re': jax.random.normal(ks[10], (DT, N_STATE), jnp.float32) * 0.5 ** 0.5, 'C_im': jax.random.normal(ks[11], (DT, N_STATE), jnp.float32) * 0.5 ** 0.5, 'D_skip': jax.random.normal(ks[12], (DT,), jnp.float32), 'mod_gate': jnp.array(0.5, jnp.float32)}
        return inp
    _L2_xattn_all = _L2_xattn_setup()
    _L2_xattn_in = {k: v for k, v in _L2_xattn_all.items() if k in ('Wq', 'Wk', 'Wv', 'W_film_in', 'b_film_in', 'W_film_out', 'b_film_out', 'g_norm_in', 'b_norm_in', 'g_norm_out', 'b_norm_out', 'g_ffn', 'b_ffn', 'W1', 'b1', 'W2', 'b2', 'log_dt', 'A_re', 'A_im', 'C_re', 'C_im', 'D_skip', 'mod_gate')}
    del _L2_xattn_all

    def _L2_ffn_setup():
        import jax, jax.numpy as jnp
        import numpy as np
        QB = 127.0
        EPS = 1e-05

        def _ste(x, q):
            return x + jax.lax.stop_gradient(q - x)

        def bitlinear(x, W, b):
            w_scale = jnp.clip(jnp.mean(jnp.abs(W)), EPS, None)
            Wq = _ste(W, jnp.clip(jnp.round(W / w_scale), -1.0, 1.0) * w_scale)
            x_scale = jnp.clip(jnp.max(jnp.abs(x), axis=-1, keepdims=True), EPS, None)
            xq = _ste(x, jnp.clip(jnp.round(x * (QB / x_scale)), -QB - 1.0, QB) * (x_scale / QB))
            return jnp.einsum('bnd,hd->bnh', xq, Wq) + b
        key = jax.random.key(seed)
        k0, k1, k2 = jax.random.split(key, 3)
        B, N, D = (8, 1024, 256)
        H = int(D * 4.0)
        x = jax.random.normal(k0, (B, N, D), dtype=jnp.float32)
        W1 = jax.random.normal(k1, (H, D), dtype=jnp.float32) * 0.02
        b1 = jnp.zeros((H,), dtype=jnp.float32)
        W2 = jax.random.normal(k2, (D, H), dtype=jnp.float32) * 0.02
        b2 = jnp.zeros((D,), dtype=jnp.float32)
        return {'x': x, 'W1': W1, 'b1': b1, 'W2': W2, 'b2': b2}
    _L2_ffn_all = _L2_ffn_setup()
    _L2_ffn_in = {k: v for k, v in _L2_ffn_all.items() if k in ('W1', 'b1', 'W2', 'b2')}
    del _L2_ffn_all

    def _L3_xattn_setup():
        import jax, jax.numpy as jnp
        import numpy as np
        B, LQ, LK = (4, 512, 512)
        D1, D2, H = (256, 192, 256)
        key = jax.random.key(seed)
        ks = jax.random.split(key, 9)
        s1, s2, sh = (1.0 / np.sqrt(D1), 1.0 / np.sqrt(D2), 1.0 / np.sqrt(H))
        return {'query': jax.random.normal(ks[0], (B, LQ, D1), jnp.float32), 'key': jax.random.normal(ks[1], (B, LK, D2), jnp.float32), 'value': jax.random.normal(ks[2], (B, LK, D2), jnp.float32), 'Wq': jax.random.normal(ks[3], (D1, H), jnp.float32) * s1, 'bq': jax.random.normal(ks[4], (H,), jnp.float32) * s1, 'Wk': jax.random.normal(ks[5], (D2, H), jnp.float32) * s2, 'bk': jax.random.normal(ks[6], (H,), jnp.float32) * s2, 'Wv': jax.random.normal(ks[7], (D2, H), jnp.float32) * s2, 'bv': jax.random.normal(ks[8], (H,), jnp.float32) * s2}
    _L3_xattn_all = _L3_xattn_setup()
    _L3_xattn_in = {k: v for k, v in _L3_xattn_all.items() if k in ('Wq', 'bq', 'Wk', 'bk', 'Wv', 'bv')}
    del _L3_xattn_all

    def _L3_ffn_setup():
        import jax, jax.numpy as jnp
        import numpy as np
        B, S, H, F, G = (8, 512, 256, 1024, 128)
        EPS = 1e-05

        def _dequant(q, scales, g):
            K, N = q.shape
            w = (q.astype(jnp.float32) - 128.0).reshape(K // g, g, N) * scales[:, None, :]
            return w.reshape(K, N)
        key = jax.random.key(seed)
        ks = jax.random.split(key, 8)
        x = jax.random.normal(ks[0], (B, S, H), dtype=jnp.float32)
        ln_gamma = jnp.ones((H,), jnp.float32)
        ln_beta = jnp.zeros((H,), jnp.float32)
        fc1_q = jax.random.randint(ks[1], (H, F), 0, 64, dtype=jnp.int32)
        fc2_q = jax.random.randint(ks[2], (F, H), 0, 64, dtype=jnp.int32)
        fc1_scales = jax.random.uniform(ks[3], (H // G, F), jnp.float32) * 0.02 + 0.001
        fc2_scales = jax.random.uniform(ks[4], (F // G, H), jnp.float32) * 0.02 + 0.001
        fc1_bias = jax.random.normal(ks[5], (F,), jnp.float32) * 0.02
        fc2_bias = jax.random.normal(ks[6], (H,), jnp.float32) * 0.02
        return {'x': x, 'ln_gamma': ln_gamma, 'ln_beta': ln_beta, 'fc1_q': fc1_q, 'fc1_scales': fc1_scales, 'fc1_bias': fc1_bias, 'fc2_q': fc2_q, 'fc2_scales': fc2_scales, 'fc2_bias': fc2_bias}
    _L3_ffn_all = _L3_ffn_setup()
    _L3_ffn_in = {k: v for k, v in _L3_ffn_all.items() if k in ('ln_gamma', 'ln_beta', 'fc1_q', 'fc1_scales', 'fc1_bias', 'fc2_q', 'fc2_scales', 'fc2_bias')}
    del _L3_ffn_all
    return {'x': x, 'ctx_768': ctx_768, 'mask_BxS2_bf1': mask_BxS2_bf1, 'mask_BxS_bf1': mask_BxS_bf1, 'L0_xattn_Wq': _L0_xattn_in['Wq'], 'L0_xattn_Wk': _L0_xattn_in['Wk'], 'L0_xattn_Wv': _L0_xattn_in['Wv'], 'L0_xattn_Wo': _L0_xattn_in['Wo'], 'L0_xattn_bo': _L0_xattn_in['bo'], 'L0_ffn_gate_weight': _L0_ffn_in['gate_weight'], 'L0_ffn_gate_bias': _L0_ffn_in['gate_bias'], 'L0_ffn_w_gate': _L0_ffn_in['w_gate'], 'L0_ffn_w_up': _L0_ffn_in['w_up'], 'L0_ffn_w_down': _L0_ffn_in['w_down'], 'L0_ffn_shared_w_gate': _L0_ffn_in['shared_w_gate'], 'L0_ffn_shared_w_up': _L0_ffn_in['shared_w_up'], 'L0_ffn_shared_w_down': _L0_ffn_in['shared_w_down'], 'L0_ffn_anchor_w_gate': _L0_ffn_in['anchor_w_gate'], 'L0_ffn_anchor_w_up': _L0_ffn_in['anchor_w_up'], 'L0_ffn_anchor_w_down': _L0_ffn_in['anchor_w_down'], 'L1_xattn_Wq': _L1_xattn_in['Wq'], 'L1_xattn_Wk': _L1_xattn_in['Wk'], 'L1_xattn_Wv': _L1_xattn_in['Wv'], 'L1_xattn_Wo': _L1_xattn_in['Wo'], 'L1_ffn_w_q': _L1_ffn_in['w_q'], 'L1_ffn_bn_gamma': _L1_ffn_in['bn_gamma'], 'L1_ffn_bn_beta': _L1_ffn_in['bn_beta'], 'L1_ffn_keys': _L1_ffn_in['keys'], 'L1_ffn_down_embed': _L1_ffn_in['down_embed'], 'L1_ffn_up_embed': _L1_ffn_in['up_embed'], 'L2_xattn_Wq': _L2_xattn_in['Wq'], 'L2_xattn_Wk': _L2_xattn_in['Wk'], 'L2_xattn_Wv': _L2_xattn_in['Wv'], 'L2_xattn_W_film_in': _L2_xattn_in['W_film_in'], 'L2_xattn_b_film_in': _L2_xattn_in['b_film_in'], 'L2_xattn_W_film_out': _L2_xattn_in['W_film_out'], 'L2_xattn_b_film_out': _L2_xattn_in['b_film_out'], 'L2_xattn_g_norm_in': _L2_xattn_in['g_norm_in'], 'L2_xattn_b_norm_in': _L2_xattn_in['b_norm_in'], 'L2_xattn_g_norm_out': _L2_xattn_in['g_norm_out'], 'L2_xattn_b_norm_out': _L2_xattn_in['b_norm_out'], 'L2_xattn_g_ffn': _L2_xattn_in['g_ffn'], 'L2_xattn_b_ffn': _L2_xattn_in['b_ffn'], 'L2_xattn_W1': _L2_xattn_in['W1'], 'L2_xattn_b1': _L2_xattn_in['b1'], 'L2_xattn_W2': _L2_xattn_in['W2'], 'L2_xattn_b2': _L2_xattn_in['b2'], 'L2_xattn_log_dt': _L2_xattn_in['log_dt'], 'L2_xattn_A_re': _L2_xattn_in['A_re'], 'L2_xattn_A_im': _L2_xattn_in['A_im'], 'L2_xattn_C_re': _L2_xattn_in['C_re'], 'L2_xattn_C_im': _L2_xattn_in['C_im'], 'L2_xattn_D_skip': _L2_xattn_in['D_skip'], 'L2_xattn_mod_gate': _L2_xattn_in['mod_gate'], 'L2_ffn_W1': _L2_ffn_in['W1'], 'L2_ffn_b1': _L2_ffn_in['b1'], 'L2_ffn_W2': _L2_ffn_in['W2'], 'L2_ffn_b2': _L2_ffn_in['b2'], 'L3_xattn_Wq': _L3_xattn_in['Wq'], 'L3_xattn_bq': _L3_xattn_in['bq'], 'L3_xattn_Wk': _L3_xattn_in['Wk'], 'L3_xattn_bk': _L3_xattn_in['bk'], 'L3_xattn_Wv': _L3_xattn_in['Wv'], 'L3_xattn_bv': _L3_xattn_in['bv'], 'L3_ffn_ln_gamma': _L3_ffn_in['ln_gamma'], 'L3_ffn_ln_beta': _L3_ffn_in['ln_beta'], 'L3_ffn_fc1_q': _L3_ffn_in['fc1_q'], 'L3_ffn_fc1_scales': _L3_ffn_in['fc1_scales'], 'L3_ffn_fc1_bias': _L3_ffn_in['fc1_bias'], 'L3_ffn_fc2_q': _L3_ffn_in['fc2_q'], 'L3_ffn_fc2_scales': _L3_ffn_in['fc2_scales'], 'L3_ffn_fc2_bias': _L3_ffn_in['fc2_bias']}

def reference(x, ctx_768, mask_BxS2_bf1, mask_BxS_bf1, L0_xattn_Wq, L0_xattn_Wk, L0_xattn_Wv, L0_xattn_Wo, L0_xattn_bo, L0_ffn_gate_weight, L0_ffn_gate_bias, L0_ffn_w_gate, L0_ffn_w_up, L0_ffn_w_down, L0_ffn_shared_w_gate, L0_ffn_shared_w_up, L0_ffn_shared_w_down, L0_ffn_anchor_w_gate, L0_ffn_anchor_w_up, L0_ffn_anchor_w_down, L1_xattn_Wq, L1_xattn_Wk, L1_xattn_Wv, L1_xattn_Wo, L1_ffn_w_q, L1_ffn_bn_gamma, L1_ffn_bn_beta, L1_ffn_keys, L1_ffn_down_embed, L1_ffn_up_embed, L2_xattn_Wq, L2_xattn_Wk, L2_xattn_Wv, L2_xattn_W_film_in, L2_xattn_b_film_in, L2_xattn_W_film_out, L2_xattn_b_film_out, L2_xattn_g_norm_in, L2_xattn_b_norm_in, L2_xattn_g_norm_out, L2_xattn_b_norm_out, L2_xattn_g_ffn, L2_xattn_b_ffn, L2_xattn_W1, L2_xattn_b1, L2_xattn_W2, L2_xattn_b2, L2_xattn_log_dt, L2_xattn_A_re, L2_xattn_A_im, L2_xattn_C_re, L2_xattn_C_im, L2_xattn_D_skip, L2_xattn_mod_gate, L2_ffn_W1, L2_ffn_b1, L2_ffn_W2, L2_ffn_b2, L3_xattn_Wq, L3_xattn_bq, L3_xattn_Wk, L3_xattn_bk, L3_xattn_Wv, L3_xattn_bv, L3_ffn_ln_gamma, L3_ffn_ln_beta, L3_ffn_fc1_q, L3_ffn_fc1_scales, L3_ffn_fc1_bias, L3_ffn_fc2_q, L3_ffn_fc2_scales, L3_ffn_fc2_bias):
    import jax
    import jax.numpy as jnp

    def _L0_xattn_ref(x, context, Wq, Wk, Wv, Wo, bo):
        import jax, jax.numpy as jnp
        import numpy as np
        H = 8
        D = 64
        SCALE = D ** (-0.5)
        B, Nq, _ = x.shape
        Nkv = context.shape[1]
        q = (x @ Wq).reshape(B, Nq, H, D)
        k = (context @ Wk).reshape(B, Nkv, H, D)
        v = (context @ Wv).reshape(B, Nkv, H, D)
        sim = jnp.einsum('bihd,bjhd->bhij', q, k) * SCALE
        attn = jax.nn.softmax(sim, axis=-1)
        out = jnp.einsum('bhij,bjhd->bihd', attn, v).reshape(B, Nq, H * D)
        return out @ Wo + bo

    def _L0_ffn_ref(hidden_states, gate_weight, gate_bias, w_gate, w_up, w_down, shared_w_gate, shared_w_up, shared_w_down, anchor_w_gate, anchor_w_up, anchor_w_down):
        import jax, jax.numpy as jnp
        import numpy as np
        HIDDEN = 256
        N_EXPERTS = 32
        MOE_I = 128
        N_GROUP = 4
        TOPK_GROUP = 2
        TOP_K = 6
        N_LOCAL_GROUPS = 16
        ANCHOR_I = 64
        SHARED_I = 128
        ROUTED_SCALE = 0.2
        ANCHOR_ALPHA = 0.1
        BATCH, SEQ = (1, 256)

        def _moe_forward(hidden_states, gate_weight, gate_bias, w_gate, w_up, w_down, shared_w_gate, shared_w_up, shared_w_down, anchor_w_gate, anchor_w_up, anchor_w_down):
            B, S, H = hidden_states.shape
            x = hidden_states.reshape(-1, H)
            T = x.shape[0]
            E = gate_weight.shape[0]
            L = anchor_w_gate.shape[0]
            logits = x @ gate_weight.T
            scores = jax.nn.sigmoid(logits)
            sc = scores + gate_bias
            grp = sc.reshape(T, N_GROUP, E // N_GROUP)
            group_scores = jax.lax.top_k(grp, 2)[0].sum(-1)
            _, gidx = jax.lax.top_k(group_scores, TOPK_GROUP)
            gmask = jax.nn.one_hot(gidx, N_GROUP, dtype=sc.dtype).sum(1)
            emask = jnp.repeat(gmask, E // N_GROUP, axis=1)
            masked = jnp.where(emask > 0, sc, -jnp.inf)
            _, topidx = jax.lax.top_k(masked, TOP_K)
            tw = jnp.take_along_axis(scores, topidx, axis=-1)
            tw = tw / (tw.sum(-1, keepdims=True) + 1e-20) * ROUTED_SCALE
            g = jnp.einsum('th,ehi->tei', x, w_gate)
            u = jnp.einsum('th,ehi->tei', x, w_up)
            eo = jnp.einsum('tei,eih->teh', jax.nn.silu(g) * u, w_down)
            cw = (jax.nn.one_hot(topidx, E, dtype=x.dtype) * tw[..., None]).sum(1)
            routed = jnp.einsum('te,teh->th', cw, eo)
            shared = jax.nn.silu(x @ shared_w_gate) * (x @ shared_w_up) @ shared_w_down
            lg = topidx[:, 0] // (E // L)
            ag = jnp.einsum('th,lhi->tli', x, anchor_w_gate)
            au = jnp.einsum('th,lhi->tli', x, anchor_w_up)
            ao = jnp.einsum('tli,lih->tlh', jax.nn.silu(ag) * au, anchor_w_down)
            acw = jax.nn.one_hot(lg, L, dtype=x.dtype)
            anchor = jnp.einsum('tl,tlh->th', acw, ao)
            out = routed + shared + ANCHOR_ALPHA * anchor
            return out.reshape(B, S, H)
        return _moe_forward(hidden_states, gate_weight, gate_bias, w_gate, w_up, w_down, shared_w_gate, shared_w_up, shared_w_down, anchor_w_gate, anchor_w_up, anchor_w_down)

    def _L1_xattn_ref(x, context, context_mask, Wq, Wk, Wv, Wo):
        import jax, jax.numpy as jnp
        import numpy as np
        DIM = 256
        CTX_DIM = 192
        HEADS = 16
        B, N, _ = x.shape
        M = context.shape[1]
        hd = DIM // HEADS
        scale = hd ** (-0.5)
        q = (x @ Wq).reshape(B, N, HEADS, hd).transpose(0, 2, 1, 3)
        k = (context @ Wk).reshape(B, M, HEADS, hd).transpose(0, 2, 1, 3)
        v = (context @ Wv).reshape(B, M, HEADS, hd).transpose(0, 2, 1, 3)
        scores = jnp.einsum('bhid,bhjd->bhij', q, k) * scale
        max_neg = -jnp.finfo(scores.dtype).max
        scores = jnp.where(context_mask[:, None, None, :], scores, max_neg)
        attn = jax.nn.softmax(scores, axis=-1)
        out = jnp.einsum('bhij,bhjd->bhid', attn, v)
        out = out.transpose(0, 2, 1, 3).reshape(B, N, DIM)
        return out @ Wo

    def _L1_ffn_ref(x, w_q, bn_gamma, bn_beta, keys, down_embed, up_embed):
        import jax, jax.numpy as jnp
        import numpy as np
        H = 8
        KD = 128
        TOPK = 8
        NUM_KEYS = 64
        N_EXPERTS = NUM_KEYS * NUM_KEYS
        N_DIM = 256
        BN_EPS = 1e-05

        def gelu_new(x):
            c = jnp.sqrt(jnp.asarray(2.0 / jnp.pi, x.dtype))
            return 0.5 * x * (1.0 + jnp.tanh(c * (x + 0.044715 * x * x * x)))
        b, n, d = x.shape
        q = jnp.einsum('bnd,de->bne', x, w_q)
        mean = jnp.mean(q, axis=(0, 1))
        var = jnp.var(q, axis=(0, 1))
        q = (q - mean) * jax.lax.rsqrt(var + BN_EPS) * bn_gamma + bn_beta
        q = q.reshape(b, n, 2, H, KD).transpose(2, 0, 1, 3, 4)
        sim = jnp.einsum('pbnhd,hkpd->pbnhk', q, keys)
        sx, ix = jax.lax.top_k(sim[0], TOPK)
        sy, iy = jax.lax.top_k(sim[1], TOPK)
        all_scores = (sx[..., :, None] + sy[..., None, :]).reshape(b, n, H, TOPK * TOPK)
        all_indices = (ix[..., :, None] * NUM_KEYS + iy[..., None, :]).reshape(b, n, H, TOPK * TOPK)
        scores, pk = jax.lax.top_k(all_scores, TOPK)
        indices = jnp.take_along_axis(all_indices, pk, axis=-1)
        wd = down_embed[indices]
        wu = up_embed[indices]
        h = jnp.einsum('bnd,bnhkd->bnhk', x, wd)
        h = gelu_new(h)
        h = jax.nn.softmax(scores, axis=-1) * h
        out = jnp.einsum('bnhk,bnhkd->bnd', h, wu)
        return out

    def _L2_xattn_ref(x_text, x_vision, text_mask, vision_mask, Wq, Wk, Wv, W_film_in, b_film_in, W_film_out, b_film_out, g_norm_in, b_norm_in, g_norm_out, b_norm_out, g_ffn, b_ffn, W1, b1, W2, b2, log_dt, A_re, A_im, C_re, C_im, D_skip, mod_gate):
        import jax, jax.numpy as jnp
        import numpy as np
        B, T, DT, G, DV = (16, 128, 256, 144, 192)
        H, DH = (4, 32)
        INNER = H * DH
        HID = 4 * DT
        N_STATE = 64
        K_TOP = 32

        def layernorm(x, g, b, eps=1e-05):
            m = x.mean(-1, keepdims=True)
            v = x.var(-1, keepdims=True)
            return (x - m) * jax.lax.rsqrt(v + eps) * g + b

        def s4d(x, log_dt, A_re, A_im, C_re, C_im, D_skip):
            Bb, L, D = x.shape
            dt = jnp.exp(log_dt)
            A = A_re + 1j * A_im
            C = C_re + 1j * C_im
            dtA = dt[:, None] * A
            dC = C * (jnp.exp(dtA) - 1.0) / A
            powers = jnp.exp(dtA[:, :, None] * jnp.arange(L))
            K = 2.0 * jnp.einsum('dn,dnl->dl', dC, powers).real
            n = 2 * L
            Kf = jnp.fft.rfft(K, n=n, axis=-1)
            xf = jnp.fft.rfft(x, n=n, axis=1)
            y = jnp.fft.irfft(xf * Kf.T[None], n=n, axis=1)[:, :L]
            return y + x * D_skip
        Bb, Tt, D = x_text.shape
        Gg = x_vision.shape[1]
        Q = (x_text @ Wq).reshape(Bb, Tt, H, DH)
        K = (x_vision @ Wk).reshape(Bb, Gg, H, DH)
        scores = jnp.einsum('bthd,bghd->bhtg', Q, K) / np.sqrt(DH).astype(np.float32)
        scores = jnp.where(vision_mask[:, None, None, :], scores, -jnp.inf)
        topv, topi = jax.lax.top_k(scores, K_TOP)
        probs = jax.nn.softmax(topv, axis=-1)
        bi = jnp.arange(Bb)[:, None, None, None]
        hi = jnp.arange(H)[None, :, None, None]
        ti = jnp.arange(Tt)[None, None, :, None]
        attn = jnp.zeros_like(scores).at[bi, hi, ti, topi].set(probs)
        attn_mean = attn.mean(axis=1)
        V = x_vision @ Wv
        c_t = jnp.einsum('btg,bgd->btd', attn_mean, V)
        c_t = c_t * text_mask[..., None]
        x = layernorm(x_text, g_norm_in, b_norm_in)
        scale_in, shift_in = jnp.split(c_t @ W_film_in + b_film_in, 2, axis=-1)
        x = x * (1.0 + mod_gate * scale_in) + mod_gate * shift_in
        y = s4d(x, log_dt, A_re, A_im, C_re, C_im, D_skip)
        scale_out, shift_out = jnp.split(c_t @ W_film_out + b_film_out, 2, axis=-1)
        y = y * (1.0 + mod_gate * scale_out) + mod_gate * shift_out
        xt = x_text + y
        h = layernorm(xt, g_ffn, b_ffn)
        h = jax.nn.gelu(h @ W1 + b1, approximate=False) @ W2 + b2
        xt = xt + h
        return layernorm(xt, g_norm_out, b_norm_out)

    def _L2_ffn_ref(x, W1, b1, W2, b2):
        import jax, jax.numpy as jnp
        import numpy as np
        QB = 127.0
        EPS = 1e-05

        def _ste(x, q):
            return x + jax.lax.stop_gradient(q - x)

        def bitlinear(x, W, b):
            w_scale = jnp.clip(jnp.mean(jnp.abs(W)), EPS, None)
            Wq = _ste(W, jnp.clip(jnp.round(W / w_scale), -1.0, 1.0) * w_scale)
            x_scale = jnp.clip(jnp.max(jnp.abs(x), axis=-1, keepdims=True), EPS, None)
            xq = _ste(x, jnp.clip(jnp.round(x * (QB / x_scale)), -QB - 1.0, QB) * (x_scale / QB))
            return jnp.einsum('bnd,hd->bnh', xq, Wq) + b
        h = bitlinear(x, W1, b1)
        h = jax.nn.gelu(h, approximate=False)
        return bitlinear(h, W2, b2)

    def _L3_xattn_ref(query, key, value, Wq, bq, Wk, bk, Wv, bv):
        import jax, jax.numpy as jnp
        import numpy as np
        B, LQ, LK = (4, 512, 512)
        D1, D2, H = (256, 192, 256)
        q = jnp.einsum('bqd,dh->bqh', query, Wq) + bq
        k = jnp.einsum('bkd,dh->bkh', key, Wk) + bk
        v = jnp.einsum('bkd,dh->bkh', value, Wv) + bv
        scores = jnp.einsum('bqh,bkh->bqk', q, k)
        weights = jax.nn.softmax(scores, axis=-1)
        return jnp.einsum('bqk,bkh->bqh', weights, v)

    def _L3_ffn_ref(x, ln_gamma, ln_beta, fc1_q, fc1_scales, fc1_bias, fc2_q, fc2_scales, fc2_bias):
        import jax, jax.numpy as jnp
        import numpy as np
        B, S, H, F, G = (8, 512, 256, 1024, 128)
        EPS = 1e-05

        def _dequant(q, scales, g):
            K, N = q.shape
            w = (q.astype(jnp.float32) - 128.0).reshape(K // g, g, N) * scales[:, None, :]
            return w.reshape(K, N)
        residual = x
        mu = jnp.mean(x, axis=-1, keepdims=True)
        var = jnp.mean(jnp.square(x - mu), axis=-1, keepdims=True)
        h = (x - mu) * jax.lax.rsqrt(var + EPS) * ln_gamma + ln_beta
        hf = h.reshape(-1, H)
        w1 = _dequant(fc1_q, fc1_scales, G)
        y = hf @ w1 + fc1_bias
        y = jax.nn.silu(y)
        w2 = _dequant(fc2_q, fc2_scales, G)
        z = y @ w2 + fc2_bias
        return residual + 0.5 * z.reshape(residual.shape)
    x = x + _L0_xattn_ref(_layernorm(x, axis=-1), ctx_768, L0_xattn_Wq, L0_xattn_Wk, L0_xattn_Wv, L0_xattn_Wo, L0_xattn_bo)
    x = x + _L0_ffn_ref(_layernorm(x, axis=-1), L0_ffn_gate_weight, L0_ffn_gate_bias, L0_ffn_w_gate, L0_ffn_w_up, L0_ffn_w_down, L0_ffn_shared_w_gate, L0_ffn_shared_w_up, L0_ffn_shared_w_down, L0_ffn_anchor_w_gate, L0_ffn_anchor_w_up, L0_ffn_anchor_w_down)
    x = x + _L1_xattn_ref(_layernorm(x, axis=-1), ctx_768, mask_BxS2_bf1, L1_xattn_Wq, L1_xattn_Wk, L1_xattn_Wv, L1_xattn_Wo)
    x = x + _L1_ffn_ref(_layernorm(x, axis=-1), L1_ffn_w_q, L1_ffn_bn_gamma, L1_ffn_bn_beta, L1_ffn_keys, L1_ffn_down_embed, L1_ffn_up_embed)
    x = x + _L2_xattn_ref(_layernorm(x, axis=-1), ctx_768, mask_BxS_bf1, mask_BxS2_bf1, L2_xattn_Wq, L2_xattn_Wk, L2_xattn_Wv, L2_xattn_W_film_in, L2_xattn_b_film_in, L2_xattn_W_film_out, L2_xattn_b_film_out, L2_xattn_g_norm_in, L2_xattn_b_norm_in, L2_xattn_g_norm_out, L2_xattn_b_norm_out, L2_xattn_g_ffn, L2_xattn_b_ffn, L2_xattn_W1, L2_xattn_b1, L2_xattn_W2, L2_xattn_b2, L2_xattn_log_dt, L2_xattn_A_re, L2_xattn_A_im, L2_xattn_C_re, L2_xattn_C_im, L2_xattn_D_skip, L2_xattn_mod_gate)
    x = x + _L2_ffn_ref(_layernorm(x, axis=-1), L2_ffn_W1, L2_ffn_b1, L2_ffn_W2, L2_ffn_b2)
    x = x + _L3_xattn_ref(_layernorm(x, axis=-1), ctx_768, ctx_768, L3_xattn_Wq, L3_xattn_bq, L3_xattn_Wk, L3_xattn_bk, L3_xattn_Wv, L3_xattn_bv)
    x = x + _L3_ffn_ref(_layernorm(x, axis=-1), L3_ffn_ln_gamma, L3_ffn_ln_beta, L3_ffn_fc1_q, L3_ffn_fc1_scales, L3_ffn_fc1_bias, L3_ffn_fc2_q, L3_ffn_fc2_scales, L3_ffn_fc2_bias)
    return x

_drawn_inputs = setup_inputs


def setup_inputs(seed=0):
    import zlib

    import numpy as np

    out = dict(_drawn_inputs(seed))
    spreads = {'L0_xattn_bo': (0.0, 0.1),
     'L1_ffn_bn_gamma': (1.0, 0.6),
     'L1_ffn_bn_beta': (0.0, 0.8),
     'L2_xattn_b_film_in': (0.0, 0.557),
     'L2_xattn_b_film_out': (0.0, 1.015),
     'L2_xattn_g_norm_in': (1.0, 0.544),
     'L2_xattn_b_norm_in': (0.0, 0.303),
     'L2_xattn_g_norm_out': (1.0, 0.2),
     'L2_xattn_b_norm_out': (0.0, 0.268),
     'L2_xattn_g_ffn': (1.0, 0.6),
     'L2_xattn_b_ffn': (0.0, 2.0),
     'L2_xattn_b1': (0.0, 2.0),
     'L2_xattn_b2': (0.0, 0.783),
     'L2_xattn_A_re': (-0.5, 0.6),
     'L2_ffn_b1': (0.0, 0.8),
     'L2_ffn_b2': (0.0, 0.1),
     'L3_ffn_ln_gamma': (1.0, 0.2),
     'L3_ffn_ln_beta': (0.0, 0.1)}
    factors = {'L0_ffn_gate_weight': 8.0,
     'L0_ffn_gate_bias': 8.0,
     'L0_ffn_w_gate': 8.0,
     'L0_ffn_w_up': 8.0,
     'L0_ffn_w_down': 8.0,
     'L0_ffn_shared_w_gate': 5.69,
     'L0_ffn_shared_w_up': 5.332,
     'L0_ffn_shared_w_down': 5.681,
     'L0_ffn_anchor_w_gate': 8.0,
     'L0_ffn_anchor_w_up': 8.0,
     'L0_ffn_anchor_w_down': 8.0,
     'L1_ffn_w_q': 8.0,
     'L1_ffn_keys': 8.0,
     'L1_ffn_down_embed': 8.0,
     'L1_ffn_up_embed': 8.0,
     'L2_xattn_Wq': 8.0,
     'L2_xattn_Wk': 8.0,
     'L2_xattn_Wv': 2.705,
     'L2_xattn_W_film_in': 4.409,
     'L2_xattn_W_film_out': 5.041,
     'L3_xattn_bk': 200.0,
     'L3_ffn_fc1_bias': 200.0,
     'L3_ffn_fc2_bias': 200.0,
     'L2_ffn_W1': 4.112,
     'L3_xattn_bv': 3.306}
    for name, (base, spread) in spreads.items():
        noise = np.random.default_rng([zlib.crc32(name.encode()), seed]).standard_normal(out[name].shape)
        drawn = base * np.exp(spread * noise) if base else spread * noise
        out[name] = jnp.asarray(drawn.astype(out[name].dtype))
    for name, factor in factors.items():
        out[name] = (out[name] * factor).astype(out[name].dtype)
    return out
```

```python
import numpy as np
import math
from contextlib import ExitStack

import concourse.bass as bass
from concourse import mybir

ALU = mybir.AluOpType
ACT = mybir.ActivationFunctionType
AX = mybir.AxisListType
F32 = mybir.dt.float32
BF16 = mybir.dt.bfloat16
I32 = mybir.dt.int32
U8 = mybir.dt.uint8
F16 = mybir.dt.float16

T = 2048
NT = 16
B = 2
D = 256
S2 = 77
MAGIC = 12582912.0
NEG = -1.0e30
WS = 4096.0


class Queues:

    def __init__(self, nc, ctx):
        self.nc, self.ctx = nc, ctx
        self.q = {k: [] for k in ("pe", "act", "dve", "pool", "sp")}
        self.sem = {k: ctx.enter_context(nc.semaphore("s_" + k)) for k in ("pe", "act", "dve", "pool")}
        self.n = {k: 0 for k in self.sem}
        self.groups = []

    def op(self, eng, fn, after, sig=True, chain=False):
        waits = [t for t in after if t is not None]
        if chain and self.n[eng]:
            waits.append((self.sem[eng], self.n[eng]))
        if sig:
            self.n[eng] += 1
        self.q[eng].append((waits, fn, (self.sem[eng], 1) if sig else None))
        return (self.sem[eng], self.n[eng]) if sig else None

    def V(self, fn, *after):
        return self.op("dve", fn, after, chain=True)

    def Vn(self, fn, *after):
        return self.op("dve", fn, after)

    def A(self, fn, *after):
        return self.op("act", fn, after)

    def G(self, fn, *after):
        return self.op("pool", fn, after)

    def mm(self, out, lhsT, rhs, start, stop, *after, sig=False):
        return self.op("pe", lambda e: e.matmul(out, lhsT, rhs, start=start, stop=stop,
                                                skip_group_check=True), after, sig)

    def tr(self, out, in_, ident, *after, sig=False):
        return self.op("pe", lambda e: e.transpose(out, in_, ident), after, sig)

    def group(self, name):
        g = Group(self, self.ctx.enter_context(self.nc.semaphore(name)))
        self.groups.append(g)
        return g

    def emit(self):
        done = {}

        def run(key, eng):
            seen = {}
            for waits, fn, inc in self.q[key]:
                for s, v in waits:
                    if seen.get(s.name, 0) < v:
                        eng.wait_ge(s, v)
                        seen[s.name] = v
                ins = fn(eng)
                if inc is not None:
                    ins.then_inc(*inc)
            done[key] = True

        block = self.ctx.enter_context(self.nc.Block())

        @block.sync
        def _(eng):
            run("sp", eng)
            for g in self.groups:
                if g.n:
                    eng.wait_ge(g.sem, 16 * g.n)

        @block.gpsimd
        def _(eng):
            run("pool", eng)

        @block.scalar
        def _(eng):
            run("act", eng)

        @block.tensor
        def _(eng):
            run("pe", eng)

        @block.vector
        def _(eng):
            run("dve", eng)


class Group:

    def __init__(self, K, sem):
        self.K, self.sem, self.n = K, sem, 0

    def load(self, out, in_, *after, eng="sp"):
        self.n += 1
        self.K.q[eng].append(([t for t in after if t is not None], lambda e: e.dma_start(out, in_), (self.sem, 16)))
        return (self.sem, 16 * self.n)

    def tok(self):
        return (self.sem, 16 * self.n)


class Arena:

    def __init__(self, mem, size):
        self.mem, self.size, self.at, self.peak = mem, size, 0, 0

    def get(self, *shape, dt=F32, parts=128):
        n = 1
        for s in shape:
            n *= s
        w = n if dt in (F32, I32) else (n + 1) // 2 if dt in (BF16, F16) else (n + 3) // 4
        w = (w + 7) // 8 * 8
        a = self.mem[0:parts, self.at:self.at + w]
        self.at += w
        self.peak = max(self.peak, self.at)
        assert self.at <= self.size, (self.at, self.size)
        if dt != F32:
            a = a.bitcast(dt)
        a = a[:, 0:n]
        if len(shape) > 1:
            names = "abcdef"[:len(shape)]
            a = a.rearrange(f"p ({' '.join(names)}) -> p {' '.join(names)}",
                            **{c: s for c, s in zip(names, shape)})
        return a


def bc(ap, axis, shape):
    return ap.unsqueeze(axis).to_broadcast(list(shape))


def program(nc, d, out):
    ctx = ExitStack()
    with ctx:
        K = Queues(nc, ctx)
        V, Vn, A, G, mm, tr = K.V, K.Vn, K.A, K.G, K.mm, K.tr
        SIZE = 53208
        mem = ctx.enter_context(nc.sbuf_tensor("mem", [128, SIZE], F32))
        PS = ctx.enter_context(nc.psum_tensor("PS", [128, 8, 512], F32))
        ar = Arena(mem, SIZE)
        free = {}
        scr = {n: nc.dram_tensor("scr_" + n, s, F32, kind="Internal").ap() for n, s in {"cw": (48, T)}.items()}

        def fr(*keys):
            return [t for k in keys for t in free.get(k, ())]

        X = ar.get(NT, D)
        HT = ar.get(2, T)
        ident = ar.get(128)
        ones = ar.get(128)
        ctxT = ar.get(2, 2 * S2, parts=96)
        st6 = ar.get(NT, 6)
        mv = ar.get(NT, 2)
        rstd = ar.get(NT)
        colc = ar.get(4)
        m8 = ar.get(B * S2, dt=U8, parts=1)
        g0 = K.group("g0")
        g0.load(X, d["x"].rearrange("b (t p) c -> p (b t) c", p=128))
        g0.load(ident, d["c_ident"])
        g0.load(ctxT, d["ctxT"].rearrange("(c p) n -> p c n", p=96))
        g0.load(colc, d["c_col"])
        g0.load(m8, d["mask2"].rearrange("(a b) k -> a (b k)", a=1))
        L0 = g0.tok()
        t_ones = V(lambda e: e.memset(ones, 1.0))

        def mask_row():
            mrow = ar.get(B, 4 * S2, parts=1)
            V(lambda e: e.tensor_copy(mrow[:, :, 0:S2], m8.rearrange("p (b k) -> p b k", b=B)), L0)
            V(lambda e: e.tensor_scalar(mrow[:, :, 0:S2], mrow[:, :, 0:S2], -1.0, -NEG, ALU.add, ALU.mult))
            for h in range(1, 4):
                t = V(lambda e, h=h: e.tensor_copy(mrow[:, :, h * S2:(h + 1) * S2], mrow[:, :, 0:S2]))
            return mrow, t

        BASE = ar.at
        barrier_tokens = []

        def phase():
            toks = [(K.sem[k], K.n[k]) for k in K.sem if K.n[k]]
            for key in K.q:
                K.q[key].append((list(toks), lambda e: None, None))
            free.clear()
            ar.at = BASE

        def ln_stats(src, after=()):
            for t in range(NT):
                (Vn if t else V)(lambda e, t=t: e.bn_stats(st6[:, t, :], src[:, t, :]), *after)
            for t in range(NT):
                (Vn if t else V)(lambda e, t=t: e.bn_aggr(mv[:, t, :], st6[:, t, :]))
            a = V(lambda e: e.tensor_scalar(rstd, mv[:, :, 1], 1e-5, None, ALU.add))
            a = A(lambda e: e.activation(rstd, rstd, ACT.Sqrt), a)
            r = V(lambda e: e.reciprocal(rstd, rstd), a)
            free["rstd"] = [r]
            return r

        def ln_tile(dst, src, t, *after):
            return Vn(lambda e: e.tensor_scalar(dst, src[:, t, :], mv[:, t, 0:1], rstd[:, t:t + 1],
                                               ALU.subtract, ALU.mult), *after, *fr("rstd"))

        evn = [0]

        def evac(out_ap, in_ap, *after):
            evn[0] += 1
            if evn[0] % 2:
                return A(lambda e: e.activation(out_ap, in_ap, ACT.Copy), *after)
            return Vn(lambda e: e.tensor_copy(out_ap, in_ap), *after)

        def transpose_tile(Hs, t, ready, bank, dst=None):
            dst = HT if dst is None else dst
            k = ("ps", bank)
            tr(PS[:, bank, 0:128], Hs[:, 0:128], ident, ready, *fr(k))
            p = tr(PS[:, bank, 128:256], Hs[:, 128:256], ident, sig=True)
            e = evac(dst[:, :, t * 128:(t + 1) * 128],
                     PS[:, bank, 0:256].rearrange("p (c n) -> p c n", c=2), p)
            free[k] = [e]
            return p, e

        def layernorm_T(src, after=()):
            r = ln_stats(src, after)
            Hb = ar.get(4, D)
            done = []
            for t in range(NT):
                a = ln_tile(Hb[:, t % 4, :], src, t, *fr(("hb", t % 4)))
                p, e = transpose_tile(Hb[:, t % 4, :], t, a, 4 + t % 4)
                free[("hb", t % 4)] = [p]
                done.append(e)
            return done

        def small_proj(dst, W, hd, ns, ready, bias=None):
            toks = []
            for s in range(ns):
                k = ("ps", s % 4)
                o = PS[0:hd, s % 4, 0:2 * S2]
                mm(o, W[:, 0, s * hd:(s + 1) * hd], ctxT[:, 0, :], True, False, ready, L0, *fr(k))
                p = mm(o, W[:, 1, s * hd:(s + 1) * hd], ctxT[:, 1, :], False, True, sig=True)
                if bias is None:
                    e = evac(dst[:, s, :], o, p)
                else:
                    e = V(lambda e, s=s, o=o: e.tensor_scalar(dst[:, s, :], o, bias[:, s:s + 1], None, ALU.add), p)
                free[k] = [e]
                toks.append(e)
            return toks

        def build_M(M, WqT, KT, hd, H, nch, kt, ready):
            toks = []
            i = 0
            for h in range(H):
                for kc in range(2):
                    bk = i % 4
                    i += 1
                    k = ("ps", bk)
                    o = PS[:, bk, 0:2 * S2]
                    for c in range(nch):
                        s = h * nch + c
                        p = mm(o, WqT[:, s, kc * 128:(kc + 1) * 128], KT[:, s, :], c == 0, c == nch - 1,
                               ready, kt[s], *fr(k), sig=(c == nch - 1))
                    e = evac(M[:, kc, :, h * S2:(h + 1) * S2], o.rearrange("p (b j) -> p b j", b=2), p)
                    free[k] = [e]
                    toks.append(e)
            return toks

        def attention(H, M, mtoks, rowb, rowt, scale, Z, ztoks, borow, bot, htoks):
            W = H * S2
            NG = (H + 3) // 4
            E = ar.get(2, W)
            ET = ar.get(2, H, 128, parts=S2)
            mx = ar.get(2, H)
            sm = ar.get(2, H)
            tokE, tokT, tokN = {}, {}, {}

            def sa(t):
                b, u = t // 8, t % 2
                for g in range(NG):
                    n = min(4, H - 4 * g)
                    k = ("ps", g)
                    o = PS[:, g, 0:n * S2]
                    for c in range(2):
                        p = mm(o, HT[:, c, t * 128:(t + 1) * 128], M[:, c, b, g * 4 * S2:g * 4 * S2 + n * S2],
                               c == 0, c == 1 and rowb is None, htoks[t], *mtoks, *fr(k),
                               sig=(c == 1 and rowb is None))
                    if rowb is not None:
                        p = mm(o, ones[0:1, :], rowb[:, b, 0:n * S2], False, True,
                               rowt, t_ones, sig=True)
                    o3 = o.rearrange("p (h j) -> p h j", h=n)
                    V(lambda e, g=g, n=n, o3=o3: e.tensor_reduce(mx[:, u, 4 * g:4 * g + n], o3, AX.X, ALU.max), p)
                    v = V(lambda e, g=g, n=n, o3=o3: e.tensor_tensor(
                        E[:, u, g * 4 * S2:g * 4 * S2 + n * S2].rearrange("p (h j) -> p h j", h=n), o3,
                        bc(mx[:, u, 4 * g:4 * g + n], 2, (128, n, S2)), ALU.subtract), *fr(("E", u)))
                    free[k] = [v]
                tokE[t] = A(lambda e: e.activation(E[:, u, :], E[:, u, :], ACT.Exp, scale=scale), v)

            def sb(t):
                u = t % 2
                E3 = E[:, u, :].rearrange("p (h j) -> p h j", h=H)
                V(lambda e: e.tensor_reduce(sm[:, u, :], E3, AX.X, ALU.add), tokE[t])
                V(lambda e: e.reciprocal(sm[:, u, :], sm[:, u, :]))
                tokN[t] = V(lambda e: e.tensor_tensor(E3, E3, bc(sm[:, u, :], 2, (128, H, S2)), ALU.mult))
                tt = []
                for g in range(NG):
                    n = min(4, H - 4 * g)
                    bk = 4 + (t * NG + g) % 2
                    k = ("ps", bk)
                    for j in range(n):
                        h = 4 * g + j
                        p = tr(PS[0:S2, bk, j * 128:(j + 1) * 128], E[:, u, h * S2:(h + 1) * S2], ident,
                               tokN[t], *fr(k), sig=(j == n - 1))
                    e = A(lambda e, g=g, n=n, bk=bk: e.activation(
                        ET[:, u, 4 * g:4 * g + n, :],
                        PS[0:S2, bk, 0:n * 128].rearrange("p (h j) -> p h j", h=n), ACT.Copy),
                        p, *fr(("ET", u)))
                    free[k] = [e]
                    tt.append(e)
                free[("E", u)] = [p]
                tokT[t] = tt

            def sc(t):
                b, u = t // 8, t % 2
                k = ("ps", 6 + u)
                o = PS[:, 6 + u, 0:256]
                for h in range(H):
                    last = h == H - 1 and borow is None
                    p = mm(o, ET[:, u, h, :], Z[:, h, b, :], h == 0, last, *tokT[t], *ztoks, *fr(k), sig=last)
                if borow is not None:
                    p = mm(o, ones[0:1, :], borow, False, True, bot, t_ones, sig=True)
                free[("ET", u)] = [p]
                free[k] = [V(lambda e: e.tensor_tensor(X[:, t, :], X[:, t, :], o, ALU.add), p)]

            for i in range(NT + 2):
                if i < NT:
                    sa(i)
                if 1 <= i <= NT:
                    sb(i - 1)
                if i >= 2:
                    sc(i - 2)

        def xattn_heads(L, H, hd, scale, masked, bo):
            phase()
            g = K.group("gx" + L)
            WK = ar.get(2, H * hd, parts=96)
            WV = ar.get(2, H * hd, parts=96)
            WQ = ar.get(H, D, parts=hd)
            WO = ar.get(H, D, parts=hd)
            g.load(WK, d[L + "Wk"].rearrange("(c p) n -> p c n", p=96), *barrier_tokens)
            g.load(WV, d[L + "Wv"].rearrange("(c p) n -> p c n", p=96))
            g.load(WQ, d[L + "WqT"].rearrange("(h p) n -> p h n", p=hd))
            g.load(WO, d[L + "Wo"].rearrange("(h p) n -> p h n", p=hd))
            bor = None
            if bo:
                bor = ar.get(D, parts=1)
                g.load(bor, d[L + "bo"])
            w = g.tok()
            KT = ar.get(H, 2 * S2, parts=hd)
            VT = ar.get(H, 2 * S2, parts=hd)
            M = ar.get(2, 2, H * S2)
            Z = ar.get(H, 2, D, parts=S2)
            ht = layernorm_T(X, (L0,))
            kt = small_proj(KT, WK, hd, H, w)
            vt = small_proj(VT, WV, hd, H, w)
            mt = build_M(M, WQ, KT, hd, H, 1, kt, w)
            zt = []
            for h in range(H):
                k = ("ps", h % 4)
                for b in range(2):
                    p = mm(PS[0:S2, h % 4, b * 256:(b + 1) * 256], VT[:, h, b * S2:(b + 1) * S2], WO[:, h, :],
                           True, True, vt[h], w, *fr(k), sig=(b == 1))
                e = evac(Z[:, h, :, :], PS[0:S2, h % 4, :].rearrange("p (b n) -> p b n", b=2), p)
                free[k] = [e]
                zt.append(e)
            mrow, t_mrow = mask_row() if masked else (None, None)
            attention(H, M, mt[-2:], mrow, t_mrow, scale, Z, zt[-2:], bor, w, ht)

        xattn_heads("L0_xattn_", 8, 64, 0.125, False, True)

        def moe():
            phase()
            NU = 41
            g = K.group("gmw")
            gm = K.group("gmm")
            WGU = ar.get(2, 2, NU, 128)
            WD = ar.get(NU, D)
            GW = ar.get(2, 32)
            gb = ar.get(32)
            gm.load(GW, d["gwT"].rearrange("(c p) n -> p c n", p=128))
            gm.load(gb, d["gate_bias"].partition_broadcast(128).rearrange("p a n -> p (a n)"))
            wl = []
            for s0, s1 in ((0, 4), (4, 16), (16, 28), (28, 41)):
                gg = K.group(f"gmw{s0}")
                gg.load(WGU[:, 0, :, s0:s1, :], d["moe_g"].rearrange("p (c e n) -> p c e n", c=2, e=NU)[:, :, s0:s1, :])
                gg.load(WGU[:, 1, :, s0:s1, :], d["moe_u"].rearrange("p (c e n) -> p c e n", c=2, e=NU)[:, :, s0:s1, :])
                gg.load(WD[:, s0:s1, :], d["moe_d"].rearrange("p (e n) -> p e n", e=NU)[:, s0:s1, :])
                wl += [gg.tok()] * (s1 - s0)
            ht = layernorm_T(X)
            s0 = ar.at
            sc = ar.get(NT, 32)
            sb_ = ar.get(NT, 32)
            gs = ar.get(NT, 8)
            tops = ar.get(NT, 4, 8)
            t8 = ar.get(NT, 8)
            sel = ar.get(NT, 32)
            cw = ar.get(NT, 48)
            wsum = ar.get(NT)
            for t in range(NT):
                for c in range(2):
                    p = mm(PS[:, 0, t * 32:(t + 1) * 32], HT[:, c, t * 128:(t + 1) * 128], GW[:, c, :],
                           c == 0, c == 1, ht[t], gm.tok(), sig=(c == 1))
            a = A(lambda e: e.activation(sc, PS[:, 0, :].rearrange("p (t n) -> p t n", t=NT), ACT.Sigmoid), p)
            V(lambda e: e.tensor_tensor(sb_, sc, bc(gb, 1, (128, NT, 32)), ALU.add), a)
            for t in range(NT):
                for q in range(4):
                    V(lambda e, t=t, q=q: e.max(tops[:, t, q, :], sb_[:, t, q * 8:(q + 1) * 8]))
            V(lambda e: e.memset(gs, NEG))
            V(lambda e: e.tensor_tensor(gs[:, :, 0:4], tops[:, :, :, 0], tops[:, :, :, 1], ALU.add))
            for t in range(NT):
                V(lambda e, t=t: e.max(t8[:, t, :], gs[:, t, :]))
            V(lambda e: e.tensor_tensor(gs[:, :, 0:4], gs[:, :, 0:4], bc(t8[:, :, 1], 2, (128, NT, 4)), ALU.is_ge))
            V(lambda e: e.tensor_scalar(gs[:, :, 0:4], gs[:, :, 0:4], -1.0, -NEG, ALU.add, ALU.mult))
            for q in range(4):
                V(lambda e, q=q: e.tensor_tensor(sb_[:, :, q * 8:(q + 1) * 8], sb_[:, :, q * 8:(q + 1) * 8],
                                                 bc(gs[:, :, q], 2, (128, NT, 8)), ALU.add))
            for t in range(NT):
                V(lambda e, t=t: e.max(t8[:, t, :], sb_[:, t, :]))
            V(lambda e: e.tensor_tensor(sel, sb_, bc(t8[:, :, 5], 2, (128, NT, 32)), ALU.is_ge))
            V(lambda e: e.tensor_tensor(sel, sel, sc, ALU.mult))
            V(lambda e: e.tensor_reduce(wsum, sel, AX.X, ALU.add))
            V(lambda e: e.tensor_scalar(wsum, wsum, 1e-20, None, ALU.add))
            V(lambda e: e.reciprocal(wsum, wsum))
            V(lambda e: e.tensor_scalar(wsum, wsum, 0.2, None, ALU.mult))
            V(lambda e: e.tensor_tensor(cw[:, :, 0:32], sel, bc(wsum, 2, (128, NT, 32)), ALU.mult))
            V(lambda e: e.tensor_tensor(sel, sb_, bc(t8[:, :, 0], 2, (128, NT, 32)), ALU.is_ge))
            s4 = sel.rearrange("p t (l r) -> p t l r", r=2)
            V(lambda e: e.tensor_tensor(cw[:, :, 32:48], s4[:, :, :, 0], s4[:, :, :, 1], ALU.max))
            a = V(lambda e: e.tensor_scalar(cw[:, :, 32:48], cw[:, :, 32:48], 0.1, None, ALU.mult))
            cwT = ar.get(T, parts=48)
            gc = K.group("gcw")
            for i in range(4):
                for j in range(4):
                    t = 4 * i + j
                    p = tr(PS[0:48, 1 + i % 2, j * 128:(j + 1) * 128], cw[:, t, :], ident, a,
                           *fr(("cwt", i % 2)), sig=(j == 3))
                e = A(lambda e, i=i: e.activation(cwT[:, i * 512:(i + 1) * 512], PS[0:48, 1 + i % 2, :], ACT.Copy), p)
                free[("cwt", i % 2)] = [e]
            gc.load(scr["cw"], cwT, e)
            wrote = gc.tok()
            pend = [(K.sem["dve"], K.n["dve"]), (K.sem["pe"], K.n["pe"]), wrote, (K.sem["act"], K.n["act"])]
            ar.at = s0
            NB_ = 4
            CB = ar.get(NB_, 512)
            SG = ar.get(2, 512)
            UU = ar.get(2, 512)
            AC = ar.get(2, 512)
            gcb = [K.group(f"gcb{i}") for i in range(NB_)]
            free_cb = {}
            free[("ps", 0)] = pend
            units = [(e, g4) for g4 in range(4) for e in range(NU)]
            actt = {}

            def up(i):
                e_, g4 = units[i]
                tk = slice(g4 * 512, (g4 + 1) * 512)
                u = i % 2
                if e_ < 40:
                    slot = i % NB_
                    G_ = gcb[slot]
                    deps = pend if i < NB_ else [wrote]
                    if e_ < 32:
                        G_.load(CB[:, slot, :], scr["cw"][e_:e_ + 1, tk].partition_broadcast(128)
                                .rearrange("p a n -> p (a n)"), *deps, *free_cb.get(slot, ()))
                    else:
                        l = 32 + 2 * (e_ - 32)
                        G_.load(CB[0:64, slot, :], scr["cw"][l:l + 1, tk].partition_broadcast(64)
                                .rearrange("p a n -> p (a n)"), *deps, *free_cb.get(slot, ()))
                        G_.load(CB[64:128, slot, :], scr["cw"][l + 1:l + 2, tk].partition_broadcast(64)
                                .rearrange("p a n -> p (a n)"))
                    ct = G_.tok()
                for m in range(2):
                    bk = 2 * u + m
                    for c in range(2):
                        p = mm(PS[:, bk, :], WGU[:, m, c, e_, :], HT[:, c, tk], c == 0, c == 1, wl[e_],
                               *(pend if i < 2 else ()), *ht[4 * g4:4 * g4 + 4], *fr(("ps", bk)), sig=(c == 1))
                    if m == 0:
                        s = A(lambda e, bk=bk, u=u: e.activation(SG[:, u, :], PS[:, bk, :], ACT.Silu), p,
                              *fr(("SG", u)), *(pend if i < 2 else ()))
                        free[("ps", bk)] = [s]
                if e_ < 40:
                    v1 = V(lambda e, bk=bk, u=u, slot=slot: e.tensor_tensor(UU[:, u, :], PS[:, bk, :], CB[:, slot, :], ALU.mult),
                           p, ct, *fr(("UU", u)))
                    free[("ps", bk)] = [v1]
                    free_cb[slot] = [v1]
                    a_ = G(lambda e, u=u: e.tensor_tensor(AC[:, u, :], UU[:, u, :], SG[:, u, :], ALU.mult), v1, s,
                           *fr(("AC", u)))
                    free[("UU", u)] = [a_]
                else:
                    a_ = V(lambda e, bk=bk, u=u: e.tensor_tensor(AC[:, u, :], PS[:, bk, :], SG[:, u, :], ALU.mult),
                           p, s, *fr(("AC", u)))
                    free[("ps", bk)] = [a_]
                free[("SG", u)] = [a_]
                actt[i] = a_

            def down(i):
                e_, g4 = units[i]
                u = i % 2
                for j in range(4):
                    bk = 4 + 2 * (g4 % 2) + j // 2
                    p = mm(PS[:, bk, (j % 2) * 256:(j % 2) * 256 + 256], AC[:, u, j * 128:(j + 1) * 128], WD[:, e_, :],
                           e_ == 0 and j % 2 == 0, e_ == NU - 1, actt[i], *fr(("ps", bk)), sig=(j == 3))
                free[("AC", u)] = [p]
                if e_ == NU - 1:
                    for q in range(2):
                        bk = 4 + 2 * (g4 % 2) + q
                        t = 4 * g4 + 2 * q
                        v = V(lambda e, bk=bk, t=t: e.tensor_tensor(
                            X[:, t:t + 2, :], X[:, t:t + 2, :],
                            PS[:, bk, :].rearrange("p (a n) -> p a n", a=2), ALU.add), p)
                        free[("ps", bk)] = [v]

            for i in range(len(units) + 1):
                if i < len(units):
                    up(i)
                if i:
                    down(i - 1)

        if True:
            moe()
        if True:
            xattn_heads("L1_xattn_", 16, 16, 0.25, True, False)

        def peer():
            phase()
            H = 8
            RW = ar.get(16, 64, parts=1)
            Mk = ar.get(2, 1024)
            s1 = ar.at
            Hn = ar.get(NT, D)
            gw = K.group("gpw")
            Wq = ar.get(2, 2048)
            WqT = ar.get(16, D)
            KY = ar.get(16, 64)
            gam = ar.get(16)
            bet = ar.get(16)
            gw.load(Wq, d["peer_wq"].rearrange("(c p) n -> p c n", p=128))
            gw.load(WqT, d["peer_wqT"].rearrange("(s p) n -> p s n", p=128))
            gw.load(KY, d["peer_keysT"])
            gw.load(gam, d["bn_gamma"])
            gw.load(bet, d["bn_beta"])
            w = gw.tok()
            ln_stats(X)
            ht = []
            for t in range(NT):
                a = ln_tile(Hn[:, t, :], X, t)
                ht.append(transpose_tile(Hn[:, t, :], t, a, 4 + t % 4)[1])
                for kc in range(2):
                    mm(PS[:, kc, 0:256], Hn[:, t, kc * 128:(kc + 1) * 128], Hn[:, t, :], t == 0, False)
                p = mm(PS[0:1, 2, 0:256], ones[:, 0:1], Hn[:, t, :], t == 0, t == NT - 1, t_ones, sig=True)
                for kc in range(2):
                    p = mm(PS[:, 3, 8 * kc:8 * kc + 1], Hn[:, t, kc * 128:(kc + 1) * 128], ones[:, 0:1],
                           t == 0 and kc == 0, t == NT - 1, sig=True)
            srow = ar.get(2, D, parts=1)
            mcol = ar.get(2)
            V(lambda e: e.tensor_copy(srow[:, 0, :], PS[0:1, 2, 0:256]), p)
            V(lambda e: e.tensor_scalar(srow[:, 1, :], PS[0:1, 2, 0:256], -1.0 / T, None, ALU.mult))
            a = V(lambda e: e.tensor_scalar(mcol, PS[:, 3, 0:16].rearrange("p (c n) -> p c n", c=2)[:, :, 0], 1.0 / T, None, ALU.mult))
            for kc in range(2):
                p = mm(PS[:, kc, 0:256], srow[:, 1, kc * 128:(kc + 1) * 128], srow[:, 0, :], False, True, a, sig=True)
            C = ar.get(2, D)
            a = A(lambda e: e.activation(C, PS[:, 0:2, 0:256], ACT.Copy), p)
            Gm = ar.get(2, 2048)
            for kc in range(2):
                for q in range(4):
                    bk = (kc * 4 + q) % 4
                    sl = slice(q * 512, (q + 1) * 512)
                    for c in range(2):
                        p = mm(PS[:, bk, :], C[:, c, kc * 128:(kc + 1) * 128], Wq[:, c, sl], c == 0, c == 1,
                               a, w, *fr(("ps", bk)), sig=(c == 1))
                    v = V(lambda e, kc=kc, sl=sl, bk=bk: e.tensor_tensor(Gm[:, kc, sl], PS[:, bk, :], Wq[:, kc, sl], ALU.mult), p)
                    free[("ps", bk)] = [v]
            for s in range(16):
                for c in range(2):
                    mm(PS[:, 4, s:s + 1], Gm[:, c, s * 128:(s + 1) * 128], ones[:, 0:1], s == 0 and c == 0,
                       c == 1, v, *fr(("ps", 4)))
            for s in range(16):
                for c in range(2):
                    p = mm(PS[:, 5, s:s + 1], Wq[:, c, s * 128:(s + 1) * 128], mcol[:, c:c + 1],
                           s == 0 and c == 0, c == 1, *fr(("ps", 5)), sig=(s == 15 and c == 1))
            av = ar.get(16)
            bv = ar.get(16)
            a = V(lambda e: e.tensor_scalar(av, PS[:, 4, 0:16], 1.0 / T, 1e-5, ALU.mult, ALU.add), p)
            a = A(lambda e: e.activation(av, av, ACT.Sqrt), a)
            V(lambda e: e.reciprocal(av, av), a)
            V(lambda e: e.tensor_tensor(av, av, gam, ALU.mult), w)
            V(lambda e: e.tensor_tensor(bv, PS[:, 5, 0:16], av, ALU.mult))
            V(lambda e: e.tensor_tensor(bv, bet, bv, ALU.subtract))
            KA = ar.get(16, 64)
            a = V(lambda e: e.tensor_tensor(KA, KY, bc(av, 2, (128, 16, 64)), ALU.mult))
            for kc in range(2):
                for s in range(16):
                    bk = 2 * kc + s // 8
                    p = mm(PS[:, bk, (s % 8) * 64:(s % 8) * 64 + 64], WqT[:, s, kc * 128:(kc + 1) * 128], KA[:, s, :],
                           True, True, a, *fr(("ps", bk)), sig=(s == 15))
                A(lambda e, kc=kc: e.activation(Mk[:, kc, :].rearrange("p (a n) -> p a n", a=2),
                                                PS[:, 2 * kc:2 * kc + 2, :], ACT.Copy), p)
            for s in range(16):
                p = mm(PS[0:1, 4 + s // 8, (s % 8) * 64:(s % 8) * 64 + 64], bv[:, s:s + 1], KY[:, s, :], True, True,
                       sig=(s == 15))
            A(lambda e: e.activation(RW.rearrange("p (a s) n -> p a (s n)", a=2), PS[0:1, 4:6, :], ACT.Copy), p)
            for key in K.q:
                K.q[key].append(([(K.sem[k], K.n[k]) for k in K.sem], lambda e: None, None))
            free.clear()
            ar.at = s1
            gd = K.group("gpd")
            DT_ = ar.get(2, 4096)
            UP = ar.get(32, D)
            gd.load(DT_, d["downT"].rearrange("(c p) n -> p c n", p=128))
            gd.load(UP, d["up_embed"].rearrange("(c p) n -> p c n", p=128))
            wd = gd.tok()
            iota = ar.get(128)
            gd.load(iota, d["c_iota"].partition_broadcast(128).rearrange("p a n -> p (a n)"))
            ti = wd = gd.tok()
            U32 = mybir.dt.uint32
            SXY = ar.get(2, 16, 64)
            GG = ar.get(2, 32, 256)
            OR = 2
            O = ar.get(OR, 128, 16, dt=F16)
            R = ar.get(OR, 32, 16, dt=F16)
            IDX = ar.get(4, 3, 128, dt=F16)
            IR = ar.get(128, 16, dt=F16)
            w1h = ar.get(64, dt=F16)
            tir = V(lambda e: e.tensor_copy(IR, bc(iota, 2, (128, 128, 16))), ti)
            sm_ = ar.get(16, 8)
            ixu = ar.get(16, 8, dt=I32).bitcast(U32)
            cand = ar.get(8, 64)
            top = ar.get(8, 8)
            pku = ar.get(8, 8, dt=I32).bitcast(U32)
            abu = ar.get(2, 64, dt=I32).bitcast(U32)
            EQ = cand.rearrange("p h (a b) -> p h a b", a=8)
            ij = ar.get(2, 64)
            w12 = ij[:, 0, :]
            rz = ar.get(8)
            e8 = ar.get(8, 8)
            TRS = ar.get(3, 2, 64)

            def sims(t):
                u = t % 2
                for q in range(2):
                    for c in range(2):
                        mm(PS[:, 0, :], HT[:, c, t * 128:(t + 1) * 128], Mk[:, c, q * 512:(q + 1) * 512], c == 0,
                           False, ht[t], *fr(("ps", 0)))
                    p = mm(PS[:, 0, :], ones[0:1, :], RW.rearrange("p (a s) n -> p a (s n)", a=2)[:, q, :],
                           False, True, sig=True)
                    e = A(lambda e, q=q: e.activation(
                        SXY[:, u, :, :].rearrange("p (a s) n -> p a (s n)", a=2)[:, q, :], PS[:, 0, :], ACT.Copy),
                        p, *fr(("SXY", u)))
                    free[("ps", 0)] = [e]
                return e

            def prep(t, st):
                u = t % 2
                for s in range(16):
                    (Vn if s else V)(lambda e, s=s: e.max(sm_[:, s, :], SXY[:, u, s, :]), st)
                for s in range(16):
                    v = (Vn if s else V)(lambda e, s=s: e.max_index(ixu[:, s, :], sm_[:, s, :], SXY[:, u, s, :]))
                free[("SXY", u)] = [v]
                V(lambda e: e.tensor_tensor(cand.rearrange("p h (a b) -> p h a b", a=8),
                                            sm_[:, 0:8, :].unsqueeze(3).to_broadcast([128, 8, 8, 8]),
                                            sm_[:, 8:16, :].unsqueeze(2).to_broadcast([128, 8, 8, 8]), ALU.add))
                for h in range(8):
                    (Vn if h else V)(lambda e, h=h: e.max(top[:, h, :], cand[:, h, :]))
                for h in range(8):
                    (Vn if h else V)(lambda e, h=h: e.max_index(pku[:, h, :], top[:, h, :], cand[:, h, :]))
                a = V(lambda e: e.tensor_tensor(e8, top, bc(top[:, :, 0], 2, (128, 8, 8)), ALU.subtract))
                a = A(lambda e: e.activation(e8, e8, ACT.Exp), a)
                pf = pku.rearrange("p h k -> p (h k)")
                V(lambda e: e.tensor_scalar(abu[:, 0, :], pf, 3, None, ALU.logical_shift_right))
                V(lambda e: e.tensor_scalar(abu[:, 1, :], pf, 7, None, ALU.bitwise_and))
                for m in range(2):
                    V(lambda e, m=m: e.tensor_tensor(
                        EQ, abu[:, m, :].rearrange("p (h k) -> p h k", h=8).unsqueeze(3).to_broadcast([128, 8, 8, 8]),
                        iota[:, 0:8].unsqueeze(1).unsqueeze(1).to_broadcast([128, 8, 8, 8]), ALU.is_equal), ti)
                    V(lambda e, m=m: e.tensor_tensor(
                        EQ, EQ, ixu[:, 8 * m:8 * m + 8, :].unsqueeze(2).to_broadcast([128, 8, 8, 8]), ALU.mult))
                    V(lambda e, m=m: e.tensor_reduce(ij[:, m, :].rearrange("p (h k) -> p h k", h=8), EQ, AX.X, ALU.add))
                V(lambda e: e.scalar_tensor_tensor(abu[:, 0, :], ij[:, 0, :], 64.0, ij[:, 1, :], ALU.mult, ALU.add))
                V(lambda e: e.tensor_scalar(abu[:, 1, :], abu[:, 0, :], 7, None, ALU.logical_shift_right))
                V(lambda e: e.tensor_scalar(abu[:, 0, :], abu[:, 0, :], 127, None, ALU.bitwise_and))
                V(lambda e: e.tensor_copy(TRS[:, 0:2, :, :], abu.unsqueeze(2).to_broadcast([128, 2, 2, 64])),
                  *fr("TRS"))
                V(lambda e: e.tensor_reduce(rz, e8, AX.X, ALU.add), a)
                V(lambda e: e.reciprocal(rz, rz))
                V(lambda e: e.tensor_scalar(rz, rz, WS, None, ALU.mult))
                V(lambda e: e.tensor_tensor(w12.rearrange("p (h k) -> p h k", h=8), e8, bc(rz, 2, (128, 8, 8)), ALU.mult))
                V(lambda e: e.tensor_copy(w1h, w12))
                V(lambda e: e.tensor_copy(TRS[:, 2, 0, :], w1h))
                return V(lambda e: e.tensor_tensor(TRS[:, 2, 1, :], w12, w1h, ALU.subtract))

            def turn(t, v):
                for m in range(3):
                    p = tr(PS[:, 0, m * 128:(m + 1) * 128], TRS[:, m, :, :].rearrange("p a b -> p (a b)"), ident, v,
                           *fr(("ps", 0)), sig=(m == 2))
                free["TRS"] = [p]
                e = A(lambda e: e.activation(IDX[:, t % 4, :, :], PS[:, 0, 0:384].rearrange("p (m n) -> p m n", m=3),
                                             ACT.Copy), p, *fr(("IDX", t % 4)))
                free[("ps", 0)] = [e]
                return e

            def scatter(t, it, gt, between, n_between=1):
                g2 = GG[:, (t // 2) % 2, :, :]
                ix = IDX[:, t % 4, :, :]
                for q in range(8):
                    r_ = q % OR
                    ts_ = slice(q * 16, q * 16 + 16)
                    ov = Vn(lambda e, r_=r_, ts_=ts_: e.tensor_tensor(O[:, r_, :, :], bc(ix[:, 0, ts_], 1, (128, 128, 16)),
                                                                IR, ALU.is_equal), it, tir, *fr(("O", r_)))
                    rv = Vn(lambda e, r_=r_, ts_=ts_: e.tensor_tensor(R[:, r_, :, :], bc(ix[:, 1, ts_], 1, (128, 32, 16)),
                                                                IR[:, 0:32, :], ALU.is_equal), it, tir, *fr(("O", r_)))
                    v = G(lambda e, r_=r_, ts_=ts_: e.tensor_tensor(R[:, r_, :, :], R[:, r_, :, :],
                                                                    bc(ix[:, 2, ts_], 1, (128, 32, 16)), ALU.mult), rv)
                    bk = 4 + q % 4
                    for i in range(16):
                        p = mm(PS[:, bk, i * 32:(i + 1) * 32], O[:, r_, :, i], R[:, r_, :, i], True, True, v, ov,
                               *fr(("ps", bk)), sig=(i == 15))
                    free[("O", r_)] = [p]
                    k = (t % 2) * 128 + q * 16
                    pv.append((g2[:, :, k:k + 16].rearrange("p c n -> p n c"), bk, p, gt))
                    for f in range(n_between):
                        if between:
                            between.pop(0)()
                    if len(pv) > 1:
                        apply_()
                free[("IDX", t % 4)] = [v, ov]

            pv = []
            last = {}

            def apply_():
                gv, bk, p, gt = pv.pop(0)
                w_ = Vn(lambda e: e.tensor_tensor(gv, gv, PS[:, bk, :].rearrange("p (n c) -> p n c", n=16),
                                                 ALU.mult), p, gt)
                free[("ps", bk)] = [w_]
                last["v"] = w_

            ghid = {}

            def hidden_steps(g_):
                u = g_ % 2

                def step(c2):
                    bk = 2 + c2 % 2
                    for h in range(2):
                        c = 2 * c2 + h
                        for kc in range(2):
                            p = mm(PS[:, bk, h * 256:(h + 1) * 256], DT_[:, kc, c * 128:(c + 1) * 128],
                                   HT[:, kc, g_ * 256:(g_ + 1) * 256], kc == 0, kc == 1, wd, ht[2 * g_], ht[2 * g_ + 1],
                                   *fr(("ps", bk)), sig=(h == 1 and kc == 1))
                    a = A(lambda e, bk=bk, c2=c2, u=u: e.activation(
                        GG[:, u, 2 * c2:2 * c2 + 2, :].rearrange("p a n -> p (a n)"), PS[:, bk, :],
                        ACT.Gelu_apprx_tanh), p, *fr(("GG", u)))
                    free[("ps", bk)] = [a]
                    ghid[g_] = a
                return [lambda c2=c2: step(c2) for c2 in range(16)]

            def outp(g_):
                u = g_ % 2
                for tl in range(2):
                    for c in range(32):
                        p = mm(PS[:, 1, tl * 256:(tl + 1) * 256], GG[:, u, c, tl * 128:(tl + 1) * 128], UP[:, c, :],
                               c == 0, c == 31, last["v"], *fr(("ps", 1)), sig=(c == 31))
                free[("GG", u)] = [p]
                return p

            def addx(g_, p):
                free[("ps", 1)] = [V(lambda e: e.scalar_tensor_tensor(
                    X[:, 2 * g_:2 * g_ + 2, :], PS[:, 1, :].rearrange("p (a n) -> p a n", a=2), 1.0 / WS,
                    X[:, 2 * g_:2 * g_ + 2, :], ALU.mult, ALU.add), p)]

            st = [sims(0), sims(1)]
            it = {}
            v0 = prep(0, st[0])
            for f in hidden_steps(0):
                f()
            it[0] = turn(0, v0)
            it[1] = turn(1, prep(1, st[1]))
            for g_ in range(8):
                nx = g_ + 1 < 8
                steps = hidden_steps(g_ + 1) if nx else []
                if nx:
                    st = [sims(2 * g_ + 2), sims(2 * g_ + 3)]
                for t in (2 * g_, 2 * g_ + 1):
                    scatter(t, it[t], ghid[g_], steps)
                apply_()
                for f in steps:
                    f()
                po = outp(g_)
                if nx:
                    for t in (2 * g_ + 2, 2 * g_ + 3):
                        it[t] = turn(t, prep(t, st[t % 2]))
                addx(g_, po)

        if True:
            peer()

        def l2x():
            phase()
            gw = K.group("gl2")
            XT0 = ar.get(NT, D)
            X1 = ar.get(NT, D)
            AT = ar.get(T, parts=S2)
            ZF = ar.get(2, 1024, parts=S2)
            FB = ar.get(1024, parts=1)
            gin = ar.get(D)
            bin_ = ar.get(D)
            dsk = ar.get(D)
            mg = ar.get(1)
            K128 = ar.get(8, D)
            for o_, n_ in ((gin, "g_norm_in"), (bin_, "b_norm_in"), (dsk, "D_skip"), (mg, "mod_gate")):
                gw.load(o_, d["L2_" + n_].partition_broadcast(128).rearrange("p a n -> p (a n)"))
            gw.load(FB[:, 0:512], d["L2_b_film_in"])
            gw.load(FB[:, 512:1024], d["L2_b_film_out"])
            s1 = ar.at
            WK = ar.get(2, 128, parts=96)
            WV = ar.get(2, 256, parts=96)
            WQ = ar.get(4, D, parts=32)
            WF = ar.get(2, 1024)
            tm8 = ar.get(NT, dt=U8)
            tmf = ar.get(NT)
            gw.load(WK, d["L2_Wk"].rearrange("(c p) n -> p c n", p=96))
            gw.load(WV, d["L2_Wv"].rearrange("(c p) n -> p c n", p=96))
            gw.load(WQ, d["L2_WqT"].rearrange("(h p) n -> p h n", p=32))
            gw.load(WF[:, :, 0:512], d["L2_W_film_in"].rearrange("(c p) n -> p c n", p=128))
            gw.load(WF[:, :, 512:1024], d["L2_W_film_out"].rearrange("(c p) n -> p c n", p=128))
            gw.load(tm8, d["mask1T"])
            w = gw.tok()
            V(lambda e: e.tensor_copy(tmf, tm8), w)
            V(lambda e: e.tensor_scalar(tmf, tmf, 0.25, None, ALU.mult))
            ln_stats(X)
            ht = []
            for t in range(NT):
                a = ln_tile(XT0[:, t, :], X, t)
                ht.append(transpose_tile(XT0[:, t, :], t, a, 4 + t % 4)[1])
            KT = ar.get(4, 2 * S2, parts=32)
            VT = ar.get(2, 2 * S2)
            M = ar.get(2, 2, 4 * S2)
            kt = small_proj(KT, WK, 32, 4, w)
            vt = small_proj(VT, WV, 128, 2, w)
            mt = build_M(M, WQ, KT, 32, 4, 1, kt, w)
            for b in range(2):
                for q in range(2):
                    bk = 2 * b + q
                    for c in range(2):
                        p = mm(PS[0:S2, bk, :], VT[:, c, b * S2:(b + 1) * S2], WF[:, c, q * 512:(q + 1) * 512], c == 0,
                               c == 1, *vt, *fr(("ps", bk)), sig=(c == 1))
                    v = V(lambda e, b=b, q=q, bk=bk: e.tensor_scalar(ZF[:, b, q * 512:(q + 1) * 512], PS[0:S2, bk, :],
                                                                     mg[0:S2, 0:1], None, ALU.mult), p)
                    free[("ps", bk)] = [v]
            V(lambda e: e.tensor_scalar(FB, FB, mg[0:1, 0:1], None, ALU.mult))
            for o_ in (0, 512):
                zt = V(lambda e, o_=o_: e.tensor_scalar(FB[:, o_:o_ + 256], FB[:, o_:o_ + 256], 1.0, None, ALU.add))
            W = 4 * S2
            mrow, t_mrow = mask_row()
            SS = ar.get(2, W)
            SR = ar.get(W)
            EE = ar.get(2, W)
            mx = ar.get(2, 4, 8)
            t8 = ar.get(4, 8)
            sm = ar.get(4)
            AM = ar.get(2, S2)
            for t in range(NT):
                b, u = t // 8, t % 2
                k = ("ps", u)
                o = PS[:, u, 0:W]
                for c in range(2):
                    mm(o, HT[:, c, t * 128:(t + 1) * 128], M[:, c, b, :], c == 0, False, ht[t], *mt[-2:], *fr(k))
                p = mm(o, ones[0:1, :], mrow[:, b, 0:W], False, True, t_mrow, sig=True)
                a = A(lambda e, u=u, o=o: e.activation(SS[:, u, :], o, ACT.Copy), p, *fr(("SS", u)))
                free[k] = [a]
                for h in range(4):
                    hs = slice(h * S2, (h + 1) * S2)
                    V(lambda e, h=h, u=u, hs=hs: e.max(mx[:, u, h, :], SS[:, u, hs]), a)
                    V(lambda e, h=h, u=u, hs=hs: e.match_replace(SR[:, hs], mx[:, u, h, :], SS[:, u, hs], -3.0e38))
                    V(lambda e, h=h, hs=hs: e.max(t8[:, h, :], SR[:, hs]))
                    for r in range(2):
                        V(lambda e, h=h, hs=hs: e.match_replace(SR[:, hs], t8[:, h, :], SR[:, hs], -3.0e38))
                        V(lambda e, h=h, hs=hs: e.max(t8[:, h, :], SR[:, hs]))
                v = V(lambda e, u=u: e.tensor_tensor(
                    EE[:, u, :].rearrange("p (h j) -> p h j", h=4), SS[:, u, :].rearrange("p (h j) -> p h j", h=4),
                    bc(mx[:, u, :, 0], 2, (128, 4, S2)), ALU.subtract))
                a = A(lambda e, u=u: e.activation(EE[:, u, :], EE[:, u, :], ACT.Exp, scale=32.0 ** -0.5), v)
                for h in range(4):
                    hs = slice(h * S2, (h + 1) * S2)
                    v = V(lambda e, h=h, u=u, hs=hs: e.scalar_tensor_tensor(
                        EE[:, u, hs], SS[:, u, hs], t8[:, h, 7:8], EE[:, u, hs], ALU.is_ge, ALU.mult), a)
                free[("SS", u)] = [v]
                V(lambda e, u=u: e.tensor_reduce(sm, EE[:, u, :].rearrange("p (h j) -> p h j", h=4), AX.X, ALU.add))
                V(lambda e: e.reciprocal(sm, sm))
                V(lambda e, t=t: e.tensor_scalar(sm, sm, tmf[:, t:t + 1], None, ALU.mult))
                V(lambda e, u=u: e.tensor_scalar(AM[:, u, :], EE[:, u, 0:S2], sm[:, 0:1], None, ALU.mult), *fr(("AM", u)))
                for h in range(1, 4):
                    hs = slice(h * S2, (h + 1) * S2)
                    v = V(lambda e, h=h, u=u, hs=hs: e.scalar_tensor_tensor(
                        AM[:, u, :], EE[:, u, hs], sm[:, h:h + 1], AM[:, u, :], ALU.mult, ALU.add))
                p = tr(PS[0:S2, 2 + u, 0:128], AM[:, u, :], ident, v, *fr(("ps", 2 + u)), sig=True)
                free[("AM", u)] = [p]
                e_ = A(lambda e, t=t, u=u: e.activation(AT[:, t * 128:(t + 1) * 128], PS[0:S2, 2 + u, 0:128], ACT.Copy), p)
                free[("ps", 2 + u)] = [e_]
            ln_stats(XT0)
            for t in range(NT):
                b, u = t // 8, t % 2
                ln_tile(X1[:, t, :], XT0, t)
                V(lambda e, t=t: e.tensor_tensor(X1[:, t, :], X1[:, t, :], gin, ALU.mult))
                V(lambda e, t=t: e.tensor_tensor(X1[:, t, :], X1[:, t, :], bin_, ALU.add))
                k = ("ps", 4 + u)
                mm(PS[:, 4 + u, :], AT[:, t * 128:(t + 1) * 128], ZF[:, b, 0:512], True, False, e_, zt, *fr(k))
                p = mm(PS[:, 4 + u, :], ones[0:1, :], FB[:, 0:512], False, True, sig=True)
                V(lambda e, t=t, u=u: e.tensor_tensor(X1[:, t, :], X1[:, t, :], PS[:, 4 + u, 0:256], ALU.mult), p)
                v = V(lambda e, t=t, u=u: e.tensor_tensor(X1[:, t, :], X1[:, t, :], PS[:, 4 + u, 256:512], ALU.add))
                free[k] = [v]
            x1t = v
            all_ = [(K.sem[k], K.n[k]) for k in K.sem if K.n[k]]
            for key in K.q:
                K.q[key].append((list(all_), lambda e: None, None))
            free.clear()
            ar.at = s1
            gk = K.group("gk")
            PI2 = 2 * math.pi
            C1 = 6.28125
            C2 = float(np.float32(PI2 - C1))
            C3 = PI2 - C1 - C2
            s2 = ar.at
            dta = ar.get(D)
            Are = ar.get(D)
            Aim = ar.get(D)
            Cre = ar.get(D)
            Cim = ar.get(D)
            l32 = ar.get(2, 32)
            for n_, o_ in (("A_re", Are), ("A_im", Aim), ("C_re", Cre), ("C_im", Cim)):
                gk.load(o_[0:64], d["L2_" + n_ + "T"])
                gk.load(o_[64:128], d["L2_" + n_ + "T"])
            gk.load(dta, d["L2_log_dt"].partition_broadcast(128).rearrange("p a n -> p (a n)"))
            gk.load(l32, d["c_l32"].partition_broadcast(128).rearrange("p a (c n) -> p (a c) n", c=2))
            wk = gk.tok()
            dt_ = ar.get(D)
            ei = ar.get(D, dt=I32)
            tmp = [ar.get(D) for _ in range(8)]

            def ts(o, i, s0, s1=None, op0=ALU.mult, op1=None, *after):
                if s1 is None:
                    return V(lambda e: e.tensor_scalar(o, i, s0, None, op0), *after)
                return V(lambda e: e.tensor_scalar(o, i, s0, s1, op0, op1), *after)

            def tt(o, a_, b_, op, *after):
                return V(lambda e: e.tensor_tensor(o, a_, b_, op), *after)

            def stt(o, a_, s_, b_, op0, op1, *after):
                return V(lambda e: e.scalar_tensor_tensor(o, a_, s_, b_, op0, op1), *after)

            def pexp(o, x_, kf, r, *after):
                ts(kf, x_, 1.4426950408889634, MAGIC, ALU.mult, ALU.add, *after)
                ts(kf, kf, -MAGIC, None, ALU.add)
                stt(r, kf, -0.693359375, x_, ALU.mult, ALU.add)
                stt(r, kf, 2.12194440e-4, r, ALU.mult, ALU.add)
                ts(kf, kf, 127.0, None, ALU.add)
                ts(kf, kf, 0.0, 254.0, ALU.max, ALU.min)
                V(lambda e: e.tensor_copy(ei, kf))
                V(lambda e: e.tensor_scalar(ei, ei, 23, None, ALU.logical_shift_left))
                ts(o, r, 1.0 / 5040)
                for c in (1 / 720, 1 / 120, 1 / 24, 1 / 6, 0.5, 1.0):
                    stt(o, o, c, r, ALU.add, ALU.mult)
                ts(o, o, 1.0, None, ALU.add)
                return tt(o, o, ei.bitcast(F32), ALU.mult)

            def reduce2pi(r, kf, x_, *after):
                ts(kf, x_, 1.0 / PI2, MAGIC, ALU.mult, ALU.add, *after)
                ts(kf, kf, -MAGIC, None, ALU.add)
                stt(r, kf, -C1, x_, ALU.mult, ALU.add)
                stt(r, kf, -C2, r, ALU.mult, ALU.add)
                return stt(r, kf, -C3, r, ALU.mult, ALU.add)

            def wrap(y, m, r, c_, pc):
                ts(m, r, pc, -PI2, ALU.is_gt, ALU.mult)
                return stt(y, r, c_, m, ALU.add, ALU.add)

            SH = 0.9999995
            pexp(dt_, dta, tmp[0], tmp[1], wk)
            dre, dim = tmp[2], tmp[3]
            tt(dre, dt_, Are, ALU.mult)
            tt(dim, dt_, Aim, ALU.mult)
            er = tmp[4]
            pexp(er, dre, tmp[0], tmp[1])
            reduce2pi(tmp[5], tmp[0], dim)
            v = wrap(tmp[6], tmp[0], tmp[5], math.pi / 2, math.pi / 2)
            a = A(lambda e: e.activation(tmp[7], tmp[5], ACT.Sin, scale=SH), v)
            a = A(lambda e: e.activation(tmp[6], tmp[6], ACT.Sin, scale=SH))
            tt(tmp[6], tmp[6], er, ALU.mult, a)
            ts(tmp[6], tmp[6], -1.0, None, ALU.add)
            tt(tmp[7], tmp[7], er, ALU.mult)
            cr, ci = tmp[0], tmp[1]
            tt(cr, tmp[6], Cre, ALU.mult)
            tt(tmp[4], tmp[7], Cim, ALU.mult)
            tt(cr, cr, tmp[4], ALU.subtract)
            tt(ci, tmp[6], Cim, ALU.mult)
            tt(tmp[4], tmp[7], Cre, ALU.mult)
            tt(ci, ci, tmp[4], ALU.add)
            tt(tmp[4], Are, Are, ALU.mult)
            tt(tmp[5], Aim, Aim, ALU.mult)
            tt(tmp[4], tmp[4], tmp[5], ALU.add)
            V(lambda e: e.reciprocal(tmp[4], tmp[4]))
            ts(tmp[4], tmp[4], 2.0)
            tt(tmp[5], cr, Are, ALU.mult)
            tt(tmp[6], ci, Aim, ALU.mult)
            tt(tmp[5], tmp[5], tmp[6], ALU.add)
            tt(ci, ci, Are, ALU.mult)
            tt(tmp[6], cr, Aim, ALU.mult)
            tt(ci, ci, tmp[6], ALU.subtract)
            tt(ci, ci, tmp[4], ALU.mult)
            tt(cr, tmp[5], tmp[4], ALU.mult)
            ND = 64
            big = [ar.get(ND, 32) for _ in range(6)]
            Kt = ar.get(32, D, parts=32)
            sh3 = (128, ND, 32)
            for blk in range(D // ND):
                ds = slice(blk * ND, (blk + 1) * ND)
                R, Q, C_, S_, EXP, U = big
                la = bc(l32[:, 0, :], 1, sh3)
                lb = bc(l32[:, 1, :], 1, sh3)
                tt(R, bc(dim[:, ds], 2, sh3), la, ALU.mult, *fr("mmUV"))
                reduce2pi(C_, Q, R)
                wrap(S_, Q, C_, colc[:, 0:1], colc[:, 1:2])
                wrap(C_, Q, C_, colc[:, 2:3], colc[:, 3:4])
                v = tt(EXP, bc(dre[:, ds], 2, sh3), la, ALU.mult)
                A(lambda e, S_=S_: e.activation(S_, S_, ACT.Sin, scale=SH), v)
                A(lambda e, C_=C_: e.activation(C_, C_, ACT.Sin, scale=SH))
                a = A(lambda e, EXP=EXP: e.activation(EXP, EXP, ACT.Exp))
                tt(C_, C_, bc(cr[:, ds], 2, sh3), ALU.mult, a)
                tt(S_, S_, bc(ci[:, ds], 2, sh3), ALU.mult)
                tt(C_, C_, S_, ALU.subtract)
                tt(U, C_, EXP, ALU.mult)
                tt(R, bc(dim[:, ds], 2, sh3), lb, ALU.mult)
                reduce2pi(C_, Q, R)
                V(lambda e, C_=C_: e.tensor_scalar(C_, C_, colc[:, 0:1], None, ALU.subtract))
                wrap(C_, Q, C_, math.pi / 2, math.pi / 2)
                v = tt(EXP, bc(dre[:, ds], 2, sh3), lb, ALU.mult)
                A(lambda e, C_=C_: e.activation(C_, C_, ACT.Sin, scale=SH), v)
                a = A(lambda e, EXP=EXP: e.activation(EXP, EXP, ACT.Exp))
                v = tt(R, C_, EXP, ALU.mult, a)
                for q in range(ND // 16):
                    bk = q % 4
                    for j in range(16):
                        dd = q * 16 + j
                        p = mm(PS[0:32, bk, j * 32:(j + 1) * 32], R[:, dd, :], U[:, dd, :], True, True, v,
                               *fr(("ps", bk)), sig=(j == 15))
                    d0 = blk * ND + q * 16
                    e_ = evac(Kt[:, :, d0:d0 + 16].rearrange("p a d -> p d a"),
                              PS[0:32, bk, :].rearrange("p (d a) -> p d a", d=16), p)
                    free[("ps", bk)] = [e_]
                free["mmUV"] = [p]
            gm_ = K.group("gkm")
            for q in range(4):
                gm_.load(K128[32 * q:32 * (q + 1), :, :], Kt.rearrange("p (l q) d -> p l q d", q=4)[:, :, q, :],
                         (K.sem["act"], K.n["act"]), (K.sem["dve"], K.n["dve"]))
            kt128 = gm_.tok()
            for key in K.q:
                K.q[key].append(([(K.sem[k], K.n[k]) for k in K.sem] + [kt128], lambda e: None, None))
            ar.at = s2
            Y = ar.get(8, 2, 512)
            FF = ar.get(2, 8, 2, 128)
            KF = ar.get(2, 2, D)
            TP = ar.get(4, 512)
            gf = [K.group("gf0"), K.group("gf1")]
            bcx = lambda a_: a_.unsqueeze(1).to_broadcast([128, 2, D])
            r2 = lambda a_: a_.rearrange("p (b n) -> p b n", b=2)
            for j in range(8):
                u = j % 2
                gf[u].load(FF[:, u, :, :, :], d["c_fwd"][j].rearrange("p (l r n) -> p l r n", l=8, r=2), *fr(("FF", u)))
                ff = gf[u].tok()
                for r in range(2):
                    k = ("ps", 2 * u + r)
                    for lt in range(8):
                        p = mm(PS[:, 2 * u + r, :], FF[:, u, lt, r, :],
                               X1.rearrange("p (b l) n -> p b l n", b=2)[:, :, lt, :],
                               lt == 0, lt == 7, ff, x1t, *fr(k), sig=(lt == 7))
                for r in range(2):
                    for lt in range(8):
                        p = mm(PS[:, 4 + u, r * 256:(r + 1) * 256], FF[:, u, lt, r, :], K128[:, lt, :],
                               lt == 0, lt == 7, kt128, *fr(("ps", 4 + u)), sig=(lt == 7))
                free[("FF", u)] = [p]
                a = A(lambda e, u=u: e.activation(KF[:, u, :, :], r2(PS[:, 4 + u, :]), ACT.Copy), p, *fr(("KF", u)))
                free[("ps", 4 + u)] = [a]
                xr, xi = r2(PS[:, 2 * u, :]), r2(PS[:, 2 * u + 1, :])
                kr, ki = bcx(KF[:, u, 0, :]), bcx(KF[:, u, 1, :])
                tt(r2(TP[:, 0, :]), xr, kr, ALU.mult, a, *fr("TP"))
                tt(r2(TP[:, 1, :]), xi, ki, ALU.mult)
                tt(r2(TP[:, 2, :]), xr, ki, ALU.mult)
                v = tt(r2(TP[:, 3, :]), xi, kr, ALU.mult)
                free[("ps", 2 * u)] = [v]
                free[("ps", 2 * u + 1)] = [v]
                free[("KF", u)] = [v]
                G(lambda e, j=j: e.tensor_tensor(Y[:, j, 0, :], TP[:, 0, :], TP[:, 1, :], ALU.subtract), v)
                g_ = G(lambda e, j=j: e.tensor_tensor(Y[:, j, 1, :], TP[:, 2, :], TP[:, 3, :], ALU.add))
                free["TP"] = [g_]
            yt = g_
            tmpb = ar.get(2, D)
            gi = [K.group("gi0"), K.group("gi1")]
            for lt in range(8):
                u = lt % 2
                FI = FF[:, u, :, :, :]
                gi[u].load(FI, d["c_inv"][lt].rearrange("p (l r n) -> p l r n", l=8, r=2), *fr(("FF", u)))
                k = ("ps", u)
                for j in range(8):
                    for r in range(2):
                        p = mm(PS[:, u, :], FI[:, j, r, :], Y[:, j, r, :], j == 0 and r == 0, j == 7 and r == 1,
                               gi[u].tok(), yt, *fr(k), sig=(j == 7 and r == 1))
                free[("FF", u)] = [p]
                pc = p
                for b in range(2):
                    t = b * 8 + lt
                    k2 = ("ps", 4 + b)
                    mm(PS[:, 4 + b, :], AT[:, t * 128:(t + 1) * 128], ZF[:, b, 512:1024], True, False, *fr(k2))
                    p = mm(PS[:, 4 + b, :], ones[0:1, :], FB[:, 512:1024], False, True, sig=True)
                    tb = tmpb[:, b, :]
                    tt(tb, X1[:, t, :], dsk, ALU.mult, pc)
                    v0 = tt(tb, tb, PS[:, u, b * 256:(b + 1) * 256], ALU.add)
                    tt(tb, tb, PS[:, 4 + b, 0:256], ALU.mult, p)
                    v1 = tt(tb, tb, PS[:, 4 + b, 256:512], ALU.add)
                    free[k2] = [v1]
                    tt(XT0[:, t, :], XT0[:, t, :], tb, ALU.add)
                free[k] = [v0]
            for key in K.q:
                K.q[key].append(([(K.sem[k], K.n[k]) for k in K.sem], lambda e: None, None))
            free.clear()
            ar.at = s1
            gn = K.group("gn")
            vec = ar.get(4, D)
            W1 = ar.get(2, 1024)
            b1c = ar.get(8)
            W2 = ar.get(8, D)
            b2r = ar.get(D, parts=1)
            for i, n_ in enumerate(("g_ffn", "b_ffn", "g_norm_out", "b_norm_out")):
                gn.load(vec[:, i, :], d["L2_" + n_].partition_broadcast(128).rearrange("p a n -> p (a n)"))
            gn.load(W1, d["L2_W1"].rearrange("(c p) n -> p c n", p=128))
            gn.load(W2, d["L2_W2"].rearrange("(c p) n -> p c n", p=128))
            gn.load(b1c, d["L2_b1"])
            gn.load(b2r, d["L2_b2"])
            wn = gn.tok()
            ln_stats(XT0)
            Hb = ar.get(4, D)
            ht = []
            for t in range(NT):
                u = t % 4
                ln_tile(Hb[:, u, :], XT0, t, *fr(("hb", u)))
                tt(Hb[:, u, :], Hb[:, u, :], vec[:, 0, :], ALU.mult, wn)
                a = tt(Hb[:, u, :], Hb[:, u, :], vec[:, 1, :], ALU.add)
                p, e = transpose_tile(Hb[:, u, :], t, a, 4 + t % 4)
                free[("hb", u)] = [p]
                ht.append(e)
            ffn(W1, b1c, W2, b2r, wn, ht, ACT.Gelu,
                lambda t, n, ps, p: tt(XT0[:, t:t + n, :], XT0[:, t:t + n, :], ps, ALU.add, p))
            ln_stats(XT0)
            for t in range(NT):
                u = t % 4
                ln_tile(Hb[:, u, :], XT0, t, *fr(("hb", u)))
                tt(Hb[:, u, :], Hb[:, u, :], vec[:, 2, :], ALU.mult)
                tt(Hb[:, u, :], Hb[:, u, :], vec[:, 3, :], ALU.add)
                free[("hb", u)] = [tt(X[:, t, :], X[:, t, :], Hb[:, u, :], ALU.add)]

        def ffn(W1, b1c, W2, b2r, ready, ht, func, add):
            AT_ = ar.get(2, 8, 512)
            at = {}

            def up(g4):
                u = g4 % 2
                for f in range(8):
                    bk = f % 4
                    for c in range(2):
                        p = mm(PS[:, bk, :], W1[:, c, f * 128:(f + 1) * 128], HT[:, c, g4 * 512:(g4 + 1) * 512], c == 0,
                               c == 1, ready, *ht[4 * g4:4 * g4 + 4], *fr(("ps", bk)), sig=(c == 1))
                    a = A(lambda e, f=f, bk=bk, u=u: e.activation(AT_[:, u, f, :], PS[:, bk, :], func, bias=b1c[:, f:f + 1]),
                          p, *fr(("AT_", u)))
                    free[("ps", bk)] = [a]
                at[g4] = a

            def down(g4):
                u = g4 % 2
                for q in range(2):
                    bk = 4 + 2 * u + q
                    for j in range(2):
                        tl = 2 * q + j
                        o = PS[:, bk, j * 256:(j + 1) * 256]
                        for f in range(8):
                            mm(o, AT_[:, u, f, tl * 128:(tl + 1) * 128], W2[:, f, :], f == 0, False, at[g4],
                               *fr(("ps", bk)))
                        p = mm(o, ones[0:1, :], b2r, False, True, sig=True)
                    t = 4 * g4 + 2 * q
                    v = add(t, 2, PS[:, bk, :].rearrange("p (a n) -> p a n", a=2), p)
                    free[("ps", bk)] = [v]
                free[("AT_", u)] = [p]

            for i in range(5):
                if i < 4:
                    up(i)
                if i:
                    down(i - 1)

        if True:
            l2x()

        def bitffn():
            phase()
            g = K.group("gbf")
            Wf = [ar.get(2, 1024), ar.get(8, D)]
            Wq = [ar.get(2, 1024, dt=BF16), ar.get(8, D, dt=BF16)]
            b1b = ar.get(1024)
            b2b = ar.get(D)
            idb = ar.get(128, dt=BF16)
            g.load(Wf[0], d["L2f_W1T"].rearrange("(c p) n -> p c n", p=128))
            g.load(Wf[1], d["L2f_W2T"].rearrange("(c p) n -> p c n", p=128))
            g.load(b1b, d["L2f_b1"].partition_broadcast(128).rearrange("p a n -> p (a n)"))
            g.load(b2b, d["L2f_b2"].partition_broadcast(128).rearrange("p a n -> p (a n)"))
            w = g.tok()
            V(lambda e: e.tensor_copy(idb, ident))
            red = ar.get(2)
            ws = ar.get(2)
            wi = ar.get(2)
            for i in range(2):
                a = V(lambda e, i=i: e.tensor_reduce(red[:, i:i + 1], Wf[i].rearrange("p a b -> p (a b)"), AX.X, ALU.add,
                                                     apply_absolute_value=True), w)
            onesq = ones
            p = mm(PS[:, 0, 0:2], onesq, red, True, True, a, sig=True)
            V(lambda e: e.tensor_scalar(ws, PS[:, 0, 0:2], 1.0 / (D * 1024), 1e-5, ALU.mult, ALU.max), p)
            V(lambda e: e.reciprocal(wi, ws))
            V(lambda e: e.tensor_scalar(ws, ws, 1.0 / 127.0, None, ALU.mult))
            for i in range(2):
                fl = Wf[i].rearrange("p a b -> p (a b)")
                V(lambda e, i=i, fl=fl: e.tensor_scalar(fl, fl, wi[:, i:i + 1], MAGIC, ALU.mult, ALU.add))
                V(lambda e, fl=fl: e.tensor_scalar(fl, fl, -MAGIC, 1.0, ALU.add, ALU.min))
                wq = V(lambda e, i=i, fl=fl: e.tensor_scalar(Wq[i].rearrange("p a b -> p (a b)"), fl, -1.0, None, ALU.max))
            ln_stats(X)
            Hb = ar.get(2, D)
            am = ar.get(2, 4)
            Qb = ar.get(2, D, dt=BF16)
            QT = ar.get(2, 2, 128, dt=BF16)
            G1 = ar.get(2, 1024)
            am2 = ar.get(2, 4)
            Q2 = ar.get(2, 1024, dt=BF16)
            QT2 = ar.get(2, 8, 128, dt=BF16)
            tq = {}

            def quant(dst, src, m, n):
                V(lambda e: e.tensor_reduce(m[:, 0:1], src, AX.X, ALU.max, apply_absolute_value=True))
                V(lambda e: e.tensor_scalar(m[:, 2:3], m[:, 0:1], 1e-5, None, ALU.max))
                V(lambda e: e.reciprocal(m[:, 3:4], m[:, 2:3]))
                V(lambda e: e.tensor_scalar(m[:, 3:4], m[:, 3:4], 127.0, None, ALU.mult))
                V(lambda e: e.tensor_scalar(src, src, m[:, 3:4], MAGIC, ALU.mult, ALU.add))
                return V(lambda e: e.tensor_scalar(dst, src, -MAGIC, None, ALU.add))

            def first(t):
                u = t % 2
                ln_tile(Hb[:, u, :], X, t, *fr(("hb", u)))
                a = quant(Qb[:, u, :], Hb[:, u, :], am[:, u, :], D)
                k = ("ps", 4 + u)
                pb_ = PS[:, 4 + u, 0:128].bitcast(BF16)
                for c in range(2):
                    p = tr(pb_[:, c * 128:(c + 1) * 128], Qb[:, u, c * 128:(c + 1) * 128], idb, a, *fr(k), sig=(c == 1))
                e = A(lambda e, u=u, pb_=pb_: e.activation(QT[:, u, :, :].rearrange("p c n -> p (c n)"), pb_, ACT.Copy), p,
                      *fr(("QT", u)))
                free[k] = [e]
                a = V(lambda e, u=u: e.tensor_tensor(am[:, u, 1:2], am[:, u, 2:3], ws[:, 0:1], ALU.mult))
                for q in range(2):
                    k = ("ps", 2 * u + q)
                    for c in range(2):
                        p = mm(PS[:, 2 * u + q, :], QT[:, u, c, :], Wq[0][:, c, q * 512:(q + 1) * 512], c == 0, c == 1,
                               e, wq, *fr(k), sig=(c == 1))
                    v = V(lambda e, u=u, q=q: e.scalar_tensor_tensor(
                        G1[:, u, q * 512:(q + 1) * 512], PS[:, 2 * u + q, :], am[:, u, 1:2],
                        b1b[:, q * 512:(q + 1) * 512], ALU.mult, ALU.add), p, w)
                    free[k] = [v]
                free[("QT", u)] = [p]
                tq[t] = A(lambda e, u=u: e.activation(G1[:, u, :], G1[:, u, :], ACT.Gelu), v)

            def second(t):
                u = t % 2
                V(lambda e: e.tensor_copy(am2[:, u, 0:1], am[:, u, 0:1]), tq[t])
                a = quant(Q2[:, u, :], G1[:, u, :], am2[:, u, :], 1024)
                V(lambda e: e.tensor_tensor(am2[:, u, 1:2], am2[:, u, 2:3], ws[:, 1:2], ALU.mult))
                k = ("ps", 6)
                pb_ = PS[:, 6, :].bitcast(BF16)
                for f in range(8):
                    p = tr(pb_[:, f * 128:(f + 1) * 128], Q2[:, u, f * 128:(f + 1) * 128], idb, a, *fr(k), sig=(f == 7))
                e = A(lambda e, u=u, pb_=pb_: e.activation(QT2[:, u, :, :].rearrange("p c n -> p (c n)"), pb_, ACT.Copy), p,
                      *fr(("QT2", u)))
                free[k] = [e]
                k = ("ps", 7)
                for f in range(8):
                    p = mm(PS[:, 7, 0:256], QT2[:, u, f, :], Wq[1][:, f, :], f == 0, f == 7, e, *fr(k), sig=(f == 7))
                free[("QT2", u)] = [p]
                v = V(lambda e, u=u: e.scalar_tensor_tensor(Hb[:, u, :], PS[:, 7, 0:256], am2[:, u, 1:2], b2b,
                                                            ALU.mult, ALU.add), p)
                free[k] = [v]
                free[("hb", u)] = [V(lambda e, t=t, u=u: e.tensor_tensor(X[:, t, :], X[:, t, :], Hb[:, u, :], ALU.add))]

            for i in range(NT + 1):
                if i < NT:
                    first(i)
                if i:
                    second(i - 1)

        if True:
            bitffn()

        def l3x():
            phase()
            g = K.group("gl3")
            WK = ar.get(2, D, parts=96)
            WV = ar.get(2, D, parts=96)
            WQ = ar.get(2, D)
            bkc = ar.get(2)
            bqc = ar.get(2)
            bvr = ar.get(D, parts=1)
            g.load(WK, d["L3_Wk"].rearrange("(c p) n -> p c n", p=96))
            g.load(WV, d["L3_Wv"].rearrange("(c p) n -> p c n", p=96))
            g.load(WQ, d["L3_WqT"].rearrange("(h p) n -> p h n", p=128))
            g.load(bkc, d["L3_bk"])
            g.load(bqc, d["L3_bq"])
            g.load(bvr, d["L3_bv"])
            w = g.tok()
            KT = ar.get(2, 2 * S2)
            M = ar.get(2, 2, S2)
            Z = ar.get(1, 2, D, parts=S2)
            rb = ar.get(2, S2, parts=1)
            ht = layernorm_T(X)
            V(lambda e: e.memset(rb, 0.0), w)
            kt = small_proj(KT, WK, 128, 2, w, bias=bkc)
            mt = build_M(M, WQ, KT, 128, 1, 2, kt, w)
            for c in range(2):
                p = mm(PS[0:1, 2, 0:2 * S2], bqc[:, c:c + 1], KT[:, c, :], c == 0, c == 1, *kt, *fr(("ps", 2)), sig=(c == 1))
            rt = V(lambda e: e.tensor_copy(rb.rearrange("p b n -> p (b n)"), PS[0:1, 2, 0:2 * S2]), p)
            free[("ps", 2)] = [rt]
            for b in range(2):
                o = PS[0:S2, 3, b * 256:(b + 1) * 256]
                for c in range(2):
                    mm(o, ctxT[:, c, b * S2:(b + 1) * S2], WV[:, c, :], c == 0, False, w, *fr(("ps", 3)))
                p = mm(o, ones[0:1, 0:S2], bvr, False, True, sig=True)
            zt = V(lambda e: e.tensor_copy(Z[:, 0, :, :], PS[0:S2, 3, :].rearrange("p (b n) -> p b n", b=2)), p)
            free[("ps", 3)] = [zt]
            attention(1, M, mt, rb, rt, 1.0, Z, [zt], None, None, ht)

        if True:
            l3x()

        def l3f():
            phase()
            g = K.group("gl3f")
            q1 = ar.get(2, 1024, dt=I32)
            q2 = ar.get(8, D, dt=I32)
            sc1 = ar.get(2, 1024)
            sc2 = ar.get(8, D)
            W1 = ar.get(2, 1024)
            W2 = ar.get(8, D)
            b1c = ar.get(8)
            b2r = ar.get(D, parts=1)
            vec = ar.get(2, D)
            R = ar.get(NT, D)
            g.load(q1, d["fc1_q"].rearrange("(c p) n -> p c n", p=128))
            g.load(q2, d["fc2_q"].rearrange("(c p) n -> p c n", p=128))
            for c in range(2):
                g.load(sc1[:, c, :], d["fc1_scales"][c:c + 1, :].partition_broadcast(128).rearrange("p a n -> p (a n)"))
            for c in range(8):
                g.load(sc2[:, c, :], d["fc2_scales"][c:c + 1, :].partition_broadcast(128).rearrange("p a n -> p (a n)"))
            g.load(b1c, d["fc1_bias"])
            g.load(b2r, d["fc2_bias"])
            g.load(vec[:, 0, :], d["ln_gamma"].partition_broadcast(128).rearrange("p a n -> p (a n)"))
            g.load(vec[:, 1, :], d["ln_beta"].partition_broadcast(128).rearrange("p a n -> p (a n)"))
            w = g.tok()
            f2 = lambda a_: a_.rearrange("p a b -> p (a b)")
            V(lambda e: e.scalar_tensor_tensor(f2(W1), f2(q1), -128.0, f2(sc1), ALU.add, ALU.mult), w)
            V(lambda e: e.scalar_tensor_tensor(f2(W2), f2(q2), -128.0, f2(sc2), ALU.add, ALU.mult))
            wt = (K.sem["dve"], K.n["dve"])
            ln_stats(X)
            for t in range(NT):
                ln_tile(R[:, t, :], X, t)
            ln_stats(R)
            Hb = ar.get(4, D)
            ht = []
            for t in range(NT):
                u = t % 4
                ln_tile(Hb[:, u, :], R, t, *fr(("hb", u)))
                V(lambda e, u=u: e.tensor_tensor(Hb[:, u, :], Hb[:, u, :], vec[:, 0, :], ALU.mult))
                a = V(lambda e, u=u: e.tensor_tensor(Hb[:, u, :], Hb[:, u, :], vec[:, 1, :], ALU.add))
                p, e = transpose_tile(Hb[:, u, :], t, a, 4 + t % 4)
                free[("hb", u)] = [p]
                ht.append(e)
            gb_out = K.group("gout")

            def add(t, n, ps, p):
                v0 = V(lambda e: e.scalar_tensor_tensor(R[:, t:t + n, :], ps, 0.5, R[:, t:t + n, :], ALU.mult, ALU.add), p)
                v = V(lambda e: e.tensor_tensor(X[:, t:t + n, :], X[:, t:t + n, :], R[:, t:t + n, :], ALU.add))
                gb_out.load(out.rearrange("b (t p) c -> p (b t) c", p=128)[:, t:t + n, :], X[:, t:t + n, :], v)
                return v0

            ffn(W1, b1c, W2, b2r, wt, ht, ACT.Silu, add)

        if True:
            l3f()
        else:
            phase()
            go = K.group("gout")
            go.load(out.rearrange("b (t p) c -> p (b t) c", p=128), X)
        K.emit()


def constants():
    f = np.arange(1024)
    l = np.arange(1024)
    th = 2 * np.pi * ((2 * f[None, :] + 1) * l[:, None] % 4096) / 4096.0
    co, si = np.cos(th), np.sin(th)
    fw = np.stack([co, -si], 0).reshape(2, 8, 128, 8, 128)
    iv = np.stack([co, -si], 0).transpose(0, 2, 1).reshape(2, 8, 128, 8, 128) * (2.0 / 2048)
    c = {}
    c["c_fwd"] = fw.transpose(3, 2, 1, 0, 4).reshape(8, 128, 2048).astype(np.float32)
    c["c_inv"] = iv.transpose(3, 2, 1, 0, 4).reshape(8, 128, 2048).astype(np.float32)
    c["c_iota"] = np.arange(128, dtype=np.float32)[None, :]
    c["c_ident"] = np.eye(128, dtype=np.float32)
    o = np.where(np.arange(128) < 64, 0.0, np.pi / 2)
    c["c_col"] = np.stack([o, np.pi - o, o + np.pi / 2, np.pi / 2 - o], 1).astype(np.float32)
    c["c_l32"] = np.concatenate([32.0 * np.arange(32), np.arange(32)])[None, :].astype(np.float32)
    return c


def layout(i):
    a = {}
    row = lambda v: v.reshape(1, -1)
    col = lambda v: np.ascontiguousarray(v.reshape(-1, 128).T)
    a["x"] = i["x"]
    a["ctxT"] = i["ctx_768"].transpose(2, 0, 1).reshape(192, 154)
    a["mask2"] = i["mask_BxS2_bf1"].view(np.uint8)
    a["mask1T"] = i["mask_BxS_bf1"].view(np.uint8).reshape(16, 128).T
    for L in ("L0_xattn_", "L1_xattn_"):
        a[L + "Wk"] = i[L + "Wk"]
        a[L + "Wv"] = i[L + "Wv"]
        a[L + "WqT"] = i[L + "Wq"].T
        a[L + "Wo"] = i[L + "Wo"]
    a["L0_xattn_bo"] = row(i["L0_xattn_bo"])
    a["gwT"] = i["L0_ffn_gate_weight"].T
    a["gate_bias"] = row(i["L0_ffn_gate_bias"])

    def up(w, s, n):
        w = w.transpose(1, 0, 2).reshape(256, 32, 128)
        n = n.transpose(1, 0, 2).reshape(256, 8, 128)
        w = np.concatenate([w, n, s.reshape(256, 1, 128)], 1)
        return w.reshape(2, 128, 41 * 128).transpose(1, 0, 2).reshape(128, -1)

    a["moe_g"] = up(i["L0_ffn_w_gate"], i["L0_ffn_shared_w_gate"], i["L0_ffn_anchor_w_gate"])
    a["moe_u"] = up(i["L0_ffn_w_up"], i["L0_ffn_shared_w_up"], i["L0_ffn_anchor_w_up"])
    dn = np.concatenate([i["L0_ffn_w_down"], i["L0_ffn_anchor_w_down"].reshape(8, 128, 256),
                         i["L0_ffn_shared_w_down"][None]], 0)
    a["moe_d"] = dn.transpose(1, 0, 2).reshape(128, -1)
    a["peer_wq"] = i["L1_ffn_w_q"]
    a["peer_wqT"] = i["L1_ffn_w_q"].T
    k = i["L1_ffn_keys"]
    a["peer_keysT"] = k.transpose(3, 2, 0, 1).reshape(128, 16, 64)
    a["bn_gamma"] = col(i["L1_ffn_bn_gamma"])
    a["bn_beta"] = col(i["L1_ffn_bn_beta"])
    a["downT"] = i["L1_ffn_down_embed"].T
    a["up_embed"] = i["L1_ffn_up_embed"]
    X = "L2_xattn_"
    for n in ("Wk", "Wv", "W_film_in", "W_film_out", "W1", "W2"):
        a["L2_" + n] = i[X + n]
    a["L2_WqT"] = i[X + "Wq"].T
    for n in ("g_norm_in", "b_norm_in", "D_skip", "mod_gate", "b_film_in", "b_film_out", "g_norm_out", "b_norm_out",
              "g_ffn", "b_ffn", "log_dt", "b2"):
        a["L2_" + n] = row(i[X + n])
    a["L2_b1"] = col(i[X + "b1"])
    for n in ("A_re", "A_im", "C_re", "C_im"):
        a["L2_" + n + "T"] = i[X + n].T
    a["L2f_W1T"] = i["L2_ffn_W1"].T
    a["L2f_W2T"] = i["L2_ffn_W2"].T
    a["L2f_b1"] = row(i["L2_ffn_b1"])
    a["L2f_b2"] = row(i["L2_ffn_b2"])
    X = "L3_xattn_"
    a["L3_Wk"] = i[X + "Wk"]
    a["L3_Wv"] = i[X + "Wv"]
    a["L3_WqT"] = i[X + "Wq"].T
    a["L3_bk"] = col(i[X + "bk"])
    a["L3_bq"] = col(i[X + "bq"])
    a["L3_bv"] = row(i[X + "bv"])
    X = "L3_ffn_"
    for n in ("fc1_q", "fc2_q", "fc1_scales", "fc2_scales"):
        a[n] = i[X + n]
    a["fc1_bias"] = col(i[X + "fc1_bias"])
    a["fc2_bias"] = row(i[X + "fc2_bias"])
    a["ln_gamma"] = row(i[X + "ln_gamma"])
    a["ln_beta"] = row(i[X + "ln_beta"])
    return a


def kernel(**inputs):
    import concourse.bacc as _bacc
    from concourse import mybir as _mybir
    from concourse.bass_utils import run_bass_kernel_spmd as _run

    nc = _bacc.Bacc("TRN2", target_bir_lowering=False, num_devices=1)
    arrays, aps = {}, {}
    data = layout({k: np.asarray(v) for k, v in inputs.items()})
    data.update(constants())
    for name, a in data.items():
        a = np.ascontiguousarray(a)
        arrays["in_" + name] = a
        aps[name] = nc.dram_tensor("in_" + name, a.shape, _mybir.dt.from_np(a.dtype), kind="ExternalInput").ap()
    o = nc.dram_tensor("out_0_dram", (2, 1024, 256), _mybir.dt.float32, kind="ExternalOutput").ap()
    program(nc, aps, o)
    r = _run(nc, [arrays], core_ids=[0])
    return r.results[0]["out_0_dram"]
```

```python
import numpy as np
import math
from contextlib import ExitStack

import concourse.bass as bass
from concourse import mybir

ALU = mybir.AluOpType
ACT = mybir.ActivationFunctionType
AX = mybir.AxisListType
F32 = mybir.dt.float32
BF16 = mybir.dt.bfloat16
I32 = mybir.dt.int32
U8 = mybir.dt.uint8
F16 = mybir.dt.float16

T = 2048
NT = 16
B = 2
D = 256
S2 = 77
MAGIC = 12582912.0
NEG = -1.0e30
WS = 4096.0


class Queues:

    def __init__(self, nc, ctx):
        self.nc, self.ctx = nc, ctx
        self.q = {k: [] for k in ("pe", "act", "dve", "pool", "sp")}
        self.sem = {k: ctx.enter_context(nc.semaphore("s_" + k)) for k in ("pe", "act", "dve", "pool")}
        self.n = {k: 0 for k in self.sem}
        self.groups = []

    def op(self, eng, fn, after, sig=True, chain=False):
        waits = [t for t in after if t is not None]
        if chain and self.n[eng]:
            waits.append((self.sem[eng], self.n[eng]))
        if sig:
            self.n[eng] += 1
        self.q[eng].append((waits, fn, (self.sem[eng], 1) if sig else None))
        return (self.sem[eng], self.n[eng]) if sig else None

    def V(self, fn, *after):
        return self.op("dve", fn, after, chain=True)

    def Vn(self, fn, *after):
        return self.op("dve", fn, after)

    def A(self, fn, *after):
        return self.op("act", fn, after)

    def G(self, fn, *after):
        return self.op("pool", fn, after)

    def mm(self, out, lhsT, rhs, start, stop, *after, sig=False):
        return self.op("pe", lambda e: e.matmul(out, lhsT, rhs, start=start, stop=stop,
                                                skip_group_check=True), after, sig)

    def tr(self, out, in_, ident, *after, sig=False):
        return self.op("pe", lambda e: e.transpose(out, in_, ident), after, sig)

    def group(self, name):
        g = Group(self, self.ctx.enter_context(self.nc.semaphore(name)))
        self.groups.append(g)
        return g

    def emit(self):
        done = {}

        def run(key, eng):
            seen = {}
            for waits, fn, inc in self.q[key]:
                for s, v in waits:
                    if seen.get(s.name, 0) < v:
                        eng.wait_ge(s, v)
                        seen[s.name] = v
                ins = fn(eng)
                if inc is not None:
                    ins.then_inc(*inc)
            done[key] = True

        block = self.ctx.enter_context(self.nc.Block())

        @block.sync
        def _(eng):
            run("sp", eng)
            for g in self.groups:
                if g.n:
                    eng.wait_ge(g.sem, 16 * g.n)

        @block.gpsimd
        def _(eng):
            run("pool", eng)

        @block.scalar
        def _(eng):
            run("act", eng)

        @block.tensor
        def _(eng):
            run("pe", eng)

        @block.vector
        def _(eng):
            run("dve", eng)


class Group:

    def __init__(self, K, sem):
        self.K, self.sem, self.n = K, sem, 0

    def load(self, out, in_, *after, eng="sp"):
        self.n += 1
        self.K.q[eng].append(([t for t in after if t is not None], lambda e: e.dma_start(out, in_), (self.sem, 16)))
        return (self.sem, 16 * self.n)

    def tok(self):
        return (self.sem, 16 * self.n)


class Arena:

    def __init__(self, mem, size):
        self.mem, self.size, self.at, self.peak = mem, size, 0, 0

    def get(self, *shape, dt=F32, parts=128):
        n = 1
        for s in shape:
            n *= s
        w = n if dt in (F32, I32) else (n + 1) // 2 if dt in (BF16, F16) else (n + 3) // 4
        w = (w + 7) // 8 * 8
        a = self.mem[0:parts, self.at:self.at + w]
        self.at += w
        self.peak = max(self.peak, self.at)
        assert self.at <= self.size, (self.at, self.size)
        if dt != F32:
            a = a.bitcast(dt)
        a = a[:, 0:n]
        if len(shape) > 1:
            names = "abcdef"[:len(shape)]
            a = a.rearrange(f"p ({' '.join(names)}) -> p {' '.join(names)}",
                            **{c: s for c, s in zip(names, shape)})
        return a


def bc(ap, axis, shape):
    return ap.unsqueeze(axis).to_broadcast(list(shape))


def program(nc, d, out):
    ctx = ExitStack()
    with ctx:
        K = Queues(nc, ctx)
        V, Vn, A, G, mm, tr = K.V, K.Vn, K.A, K.G, K.mm, K.tr
        SIZE = 53208
        mem = ctx.enter_context(nc.sbuf_tensor("mem", [128, SIZE], F32))
        PS = ctx.enter_context(nc.psum_tensor("PS", [128, 8, 512], F32))
        ar = Arena(mem, SIZE)
        free = {}
        scr = {n: nc.dram_tensor("scr_" + n, s, F32, kind="Internal").ap() for n, s in {"cw": (48, T), "K": (1024, D)}.items()}

        def fr(*keys):
            return [t for k in keys for t in free.get(k, ())]

        X = ar.get(NT, D)
        HT = ar.get(2, T)
        ident = ar.get(128)
        ones = ar.get(128)
        ctxT = ar.get(2, 2 * S2, parts=96)
        st6 = ar.get(NT, 6)
        mv = ar.get(NT, 2)
        rstd = ar.get(NT)
        colc = ar.get(6)
        m8 = ar.get(B * S2, dt=U8, parts=1)
        g0 = K.group("g0")
        g0.load(X, d["x"].rearrange("b (t p) c -> p (b t) c", p=128))
        g0.load(ident, d["c_ident"])
        g0.load(ctxT, d["ctxT"].rearrange("(c p) n -> p c n", p=96))
        g0.load(colc, d["c_col"])
        g0.load(m8, d["mask2"].rearrange("(a b) k -> a (b k)", a=1))
        L0 = g0.tok()
        t_ones = V(lambda e: e.memset(ones, 1.0))

        def mask_row():
            mrow = ar.get(B, 4 * S2, parts=1)
            V(lambda e: e.tensor_copy(mrow[:, :, 0:S2], m8.rearrange("p (b k) -> p b k", b=B)), L0)
            V(lambda e: e.tensor_scalar(mrow[:, :, 0:S2], mrow[:, :, 0:S2], -1.0, -NEG, ALU.add, ALU.mult))
            for h in range(1, 4):
                t = V(lambda e, h=h: e.tensor_copy(mrow[:, :, h * S2:(h + 1) * S2], mrow[:, :, 0:S2]))
            return mrow, t

        BASE = ar.at
        barrier_tokens = []

        def phase():
            toks = [(K.sem[k], K.n[k]) for k in K.sem if K.n[k]]
            for key in K.q:
                K.q[key].append((list(toks), lambda e: None, None))
            free.clear()
            ar.at = BASE

        def ln_stats(src, after=()):
            for t in range(NT):
                (Vn if t else V)(lambda e, t=t: e.bn_stats(st6[:, t, :], src[:, t, :]), *after)
            for t in range(NT):
                (Vn if t else V)(lambda e, t=t: e.bn_aggr(mv[:, t, :], st6[:, t, :]))
            a = V(lambda e: e.tensor_scalar(rstd, mv[:, :, 1], 1e-5, None, ALU.add))
            a = A(lambda e: e.activation(rstd, rstd, ACT.Sqrt), a)
            r = V(lambda e: e.reciprocal(rstd, rstd), a)
            free["rstd"] = [r]
            return r

        def ln_tile(dst, src, t, *after):
            return Vn(lambda e: e.tensor_scalar(dst, src[:, t, :], mv[:, t, 0:1], rstd[:, t:t + 1],
                                               ALU.subtract, ALU.mult), *after, *fr("rstd"))

        evn = [0]

        def evac(out_ap, in_ap, *after):
            evn[0] += 1
            if evn[0] % 2:
                return A(lambda e: e.activation(out_ap, in_ap, ACT.Copy), *after)
            return Vn(lambda e: e.tensor_copy(out_ap, in_ap), *after)

        def transpose_tile(Hs, t, ready, bank, dst=None):
            dst = HT if dst is None else dst
            k = ("ps", bank)
            tr(PS[:, bank, 0:128], Hs[:, 0:128], ident, ready, *fr(k))
            p = tr(PS[:, bank, 128:256], Hs[:, 128:256], ident, sig=True)
            e = evac(dst[:, :, t * 128:(t + 1) * 128],
                     PS[:, bank, 0:256].rearrange("p (c n) -> p c n", c=2), p)
            free[k] = [e]
            return p, e

        def layernorm_T(src, after=()):
            r = ln_stats(src, after)
            Hb = ar.get(4, D)
            done = []
            for t in range(NT):
                a = ln_tile(Hb[:, t % 4, :], src, t, *fr(("hb", t % 4)))
                p, e = transpose_tile(Hb[:, t % 4, :], t, a, 4 + t % 4)
                free[("hb", t % 4)] = [p]
                done.append(e)
            return done

        def small_proj(dst, W, hd, ns, ready, bias=None):
            toks = []
            for s in range(ns):
                k = ("ps", s % 4)
                o = PS[0:hd, s % 4, 0:2 * S2]
                mm(o, W[:, 0, s * hd:(s + 1) * hd], ctxT[:, 0, :], True, False, ready, L0, *fr(k))
                p = mm(o, W[:, 1, s * hd:(s + 1) * hd], ctxT[:, 1, :], False, True, sig=True)
                if bias is None:
                    e = evac(dst[:, s, :], o, p)
                else:
                    e = V(lambda e, s=s, o=o: e.tensor_scalar(dst[:, s, :], o, bias[:, s:s + 1], None, ALU.add), p)
                free[k] = [e]
                toks.append(e)
            return toks

        def build_M(M, WqT, KT, hd, H, nch, kt, ready):
            toks = []
            i = 0
            for h in range(H):
                for kc in range(2):
                    bk = i % 4
                    i += 1
                    k = ("ps", bk)
                    o = PS[:, bk, 0:2 * S2]
                    for c in range(nch):
                        s = h * nch + c
                        p = mm(o, WqT[:, s, kc * 128:(kc + 1) * 128], KT[:, s, :], c == 0, c == nch - 1,
                               ready, kt[s], *fr(k), sig=(c == nch - 1))
                    e = evac(M[:, kc, :, h * S2:(h + 1) * S2], o.rearrange("p (b j) -> p b j", b=2), p)
                    free[k] = [e]
                    toks.append(e)
            return toks

        def chunks(H):
            W = H * S2
            return [(c, min(128, W - 128 * c)) for c in range((W + 127) // 128)]

        def pack_rows(g, Zp, Zs, H, ready):
            for h in range(H):
                a = 0
                while a < S2:
                    r = h * S2 + a
                    n = min(S2 - a, 128 - r % 128)
                    g.load(Zp[r % 128:r % 128 + n, r // 128, :, :], Zs[a:a + n, h, :, :], ready[h])
                    a += n
            return g.tok()

        def attention(H, M, mtoks, rowb, rowt, scale, Z, ztoks, borow, bot, htoks, early=(), bg=None):
            W = H * S2
            NG = (H + 3) // 4
            CH = chunks(H)
            E = ar.get(2, W)
            ET = ar.get(2, len(CH), 128)
            mx = ar.get(2, H)
            sm = ar.get(2, H)
            free[("E", 0)] = free[("E", 1)] = free[("ET", 0)] = free[("ET", 1)] = list(early)
            tokE, tokT, tokN = {}, {}, {}
            bg = bg or (lambda n: None)

            def sa(t):
                b, u = t // 8, t % 2
                ps_ = []
                for g in range(NG):
                    n = min(4, H - 4 * g)
                    k = ("ps", g)
                    o = PS[:, g, 0:n * S2]
                    for c in range(2):
                        p = mm(o, HT[:, c, t * 128:(t + 1) * 128], M[:, c, b, g * 4 * S2:g * 4 * S2 + n * S2],
                               c == 0, c == 1 and rowb is None, htoks[t], *mtoks, *fr(k),
                               sig=(c == 1 and rowb is None))
                    if rowb is not None:
                        p = mm(o, ones[0:1, :], rowb[:, b, 0:n * S2], False, True,
                               rowt, t_ones, sig=True)
                    ps_.append((g, n, o.rearrange("p (h j) -> p h j", h=n), p))
                for g, n, o3, p in ps_:
                    (Vn if g else V)(lambda e, g=g, n=n, o3=o3: e.tensor_reduce(
                        mx[:, u, 4 * g:4 * g + n], o3, AX.X, ALU.max), p, *(early if t < 2 else ()))
                for g, n, o3, p in ps_:
                    v = (Vn if g else V)(lambda e, g=g, n=n, o3=o3: e.tensor_tensor(
                        E[:, u, g * 4 * S2:g * 4 * S2 + n * S2].rearrange("p (h j) -> p h j", h=n), o3,
                        bc(mx[:, u, 4 * g:4 * g + n], 2, (128, n, S2)), ALU.subtract), *fr(("E", u)))
                    free[("ps", g)] = [v]
                tokE[t] = A(lambda e: e.activation(E[:, u, :], E[:, u, :], ACT.Exp, scale=scale), v)

            def sb(t):
                u = t % 2
                E3 = E[:, u, :].rearrange("p (h j) -> p h j", h=H)
                V(lambda e: e.tensor_reduce(sm[:, u, :], E3, AX.X, ALU.add), tokE[t])
                V(lambda e: e.reciprocal(sm[:, u, :], sm[:, u, :]))
                tokN[t] = V(lambda e: e.tensor_tensor(E3, E3, bc(sm[:, u, :], 2, (128, H, S2)), ALU.mult))

            def sc(t):
                u = t % 2
                tt = []
                for q in range(0, len(CH), 4):
                    part = CH[q:q + 4]
                    bk = 4 + (q // 4) % 2
                    k = ("ps", bk)
                    for c, n in part:
                        p = tr(PS[0:n, bk, (c - q) * 128:(c - q + 1) * 128], E[:, u, c * 128:c * 128 + n], ident,
                               tokN[t], *fr(k), sig=(c == part[-1][0]))
                    free[k] = []
                    for n in sorted({n for _, n in part}, reverse=True):
                        cs = [c for c, m in part if m == n]
                        e = A(lambda e, cs=cs, n=n, q=q, bk=bk: e.activation(
                            ET[0:n, u, cs[0]:cs[-1] + 1, :],
                            PS[0:n, bk, (cs[0] - q) * 128:(cs[-1] - q + 1) * 128].rearrange("p (h j) -> p h j", h=len(cs)),
                            ACT.Copy), p, *fr(("ET", u)))
                        free[k] = [e]
                    tt.append(e)
                free[("E", u)] = [p]
                tokT[t] = tt

            def sd(t):
                b, u = t // 8, t % 2
                k = ("ps", 7)
                o = PS[:, 7, 0:256]
                for c, n in CH:
                    last = c == CH[-1][0] and borow is None
                    p = mm(o, ET[0:n, u, c, :], Z[0:n, c, b, :], c == 0, last, *tokT[t], *ztoks, *fr(k), sig=last)
                if borow is not None:
                    p = mm(o, ones[0:1, :], borow, False, True, bot, t_ones, sig=True)
                free[("ET", u)] = [p]
                return p

            def se(t, p):
                free[("ps", 7)] = [Vn(lambda e: e.tensor_tensor(X[:, t, :], X[:, t, :], PS[:, 7, 0:256], ALU.add), p)]

            for i in range(NT + 2):
                if i < NT:
                    sa(i)
                    bg(7)
                if 1 <= i <= NT:
                    sb(i - 1)
                    bg(7)
                if i >= 2:
                    p = sd(i - 2)
                if 1 <= i <= NT:
                    sc(i - 1)
                    bg(7)
                if i >= 2:
                    se(i - 2, p)
                    bg(7)

        def xattn_heads(L, H, hd, scale, masked, bo, bg=None):
            phase()
            g = K.group("gx" + L)
            WK = ar.get(2, H * hd, parts=96)
            WV = ar.get(2, H * hd, parts=96)
            WQ = ar.get(H, D, parts=hd)
            WO = ar.get(H, D, parts=hd)
            g.load(WK, d[L + "Wk"].rearrange("(c p) n -> p c n", p=96))
            g.load(WV, d[L + "Wv"].rearrange("(c p) n -> p c n", p=96))
            g.load(WQ, d[L + "WqT"].rearrange("(h p) n -> p h n", p=hd))
            g.load(WO, d[L + "Wo"].rearrange("(h p) n -> p h n", p=hd))
            bor = None
            if bo:
                bor = ar.get(D, parts=1)
                g.load(bor, d[L + "bo"])
            w = g.tok()
            KT = ar.get(H, 2 * S2, parts=hd)
            VT = ar.get(H, 2 * S2, parts=hd)
            M = ar.get(2, 2, H * S2)
            Zp = ar.get(len(chunks(H)), 2, D)
            mrow, t_mrow = mask_row() if masked else (None, None)
            step = bg(ar) if bg else None
            ln_stats(X, (L0,))
            kt = small_proj(KT, WK, hd, H, w)
            vt = small_proj(VT, WV, hd, H, w)
            at = ar.at
            Zs = ar.get(H, 2, D, parts=S2)
            zt = []
            for h in range(H):
                k = ("ps", h % 4)
                for b in range(2):
                    p = mm(PS[0:S2, h % 4, b * 256:(b + 1) * 256], VT[:, h, b * S2:(b + 1) * S2], WO[:, h, :],
                           True, True, vt[h], w, *fr(k), sig=(b == 1))
                e = evac(Zs[:, h, :, :], PS[0:S2, h % 4, :].rearrange("p (b n) -> p b n", b=2), p)
                free[k] = [e]
                zt.append(e)
            zp = pack_rows(K.group("gz" + L), Zp, Zs, H, zt)
            mt = build_M(M, WQ, KT, hd, H, 1, kt, w)
            Hb = ar.get(4, D)
            ht = []
            for t in range(NT):
                a = ln_tile(Hb[:, t % 4, :], X, t, *fr(("hb", t % 4)))
                p, e = transpose_tile(Hb[:, t % 4, :], t, a, 4 + t % 4)
                free[("hb", t % 4)] = [p]
                ht.append(e)
            ar.at = at
            attention(H, M, mt[-2:], mrow, t_mrow, scale, Zp, [zp], bor, w, ht, early=[zp, ht[-1], ht[-2], p], bg=step)
            if step:
                step(10 ** 6)

        def s4d(ar, bank, early):
            gk = K.group("gk")
            PI2 = 2 * math.pi
            C1 = 6.28125
            C2 = float(np.float32(PI2 - C1))
            C3 = PI2 - C1 - C2
            l32 = ar.get(2, 32)
            KC = [ar.get(D) for _ in range(4)]
            dre, dim, cr, ci = KC
            s2 = ar.at
            dta = ar.get(D)
            Are = ar.get(D)
            Aim = ar.get(D)
            Cre = ar.get(D)
            Cim = ar.get(D)
            for n_, o_ in (("A_re", Are), ("A_im", Aim), ("C_re", Cre), ("C_im", Cim)):
                gk.load(o_[0:64], d["L2_" + n_ + "T"], *early)
                gk.load(o_[64:128], d["L2_" + n_ + "T"])
            gk.load(dta, d["L2_log_dt"].partition_broadcast(128).rearrange("p a n -> p (a n)"))
            gk.load(l32, d["c_l32"].partition_broadcast(128).rearrange("p a (c n) -> p (a c) n", c=2))
            wk = gk.tok()
            dt_ = ar.get(D)
            ei = ar.get(D, dt=I32)
            tmp = [ar.get(D) for _ in range(6)]
            e1 = ar.at
            ar.at = s2
            ND = 8
            R = ar.get(2, ND, 32)
            Q = ar.get(2, ND, 32)
            C_ = ar.get(2, ND, 32)
            EXP = ar.get(2, ND, 32)
            S_ = ar.get(ND, 32)
            UV = ar.get(2, 2, ND, 32)
            Kt = ar.get(32, 4 * ND, parts=32)
            ar.at = max(ar.at, e1)
            SH = 0.9999995
            fk = {}

            def ts(o, i, s0, s1=None, op0=ALU.mult, op1=None, *after):
                if s1 is None:
                    return V(lambda e: e.tensor_scalar(o, i, s0, None, op0), *after)
                return V(lambda e: e.tensor_scalar(o, i, s0, s1, op0, op1), *after)

            def tt(o, a_, b_, op, *after):
                return V(lambda e: e.tensor_tensor(o, a_, b_, op), *after)

            def gg(o, a_, b_, op, *after):
                return G(lambda e: e.tensor_tensor(o, a_, b_, op), *after)

            def stt(o, a_, s_, b_, op0, op1, *after):
                return V(lambda e: e.scalar_tensor_tensor(o, a_, s_, b_, op0, op1), *after)

            def pexp(o, x_, kf, r, *after):
                ts(kf, x_, 1.4426950408889634, MAGIC, ALU.mult, ALU.add, *after)
                ts(kf, kf, -MAGIC, None, ALU.add)
                stt(r, kf, -0.693359375, x_, ALU.mult, ALU.add)
                stt(r, kf, 2.12194440e-4, r, ALU.mult, ALU.add)
                yield
                ts(kf, kf, 127.0, None, ALU.add)
                ts(kf, kf, 0.0, 254.0, ALU.max, ALU.min)
                V(lambda e: e.tensor_copy(ei, kf))
                V(lambda e: e.tensor_scalar(ei, ei, 23, None, ALU.logical_shift_left))
                yield
                ts(o, r, 1.0 / 5040)
                for c in (1 / 720, 1 / 120, 1 / 24, 1 / 6, 0.5, 1.0):
                    stt(o, o, c, r, ALU.add, ALU.mult)
                    yield
                ts(o, o, 1.0, None, ALU.add)
                tt(o, o, ei.bitcast(F32), ALU.mult)
                yield

            def reduce2pi(r, kf, x_, *after):
                ts(kf, x_, 1.0 / PI2, MAGIC, ALU.mult, ALU.add, *after)
                ts(kf, kf, -MAGIC, None, ALU.add)
                yield
                stt(r, kf, -C1, x_, ALU.mult, ALU.add)
                yield
                stt(r, kf, -C2, r, ALU.mult, ALU.add)
                yield
                stt(r, kf, -C3, r, ALU.mult, ALU.add)
                yield

            def wrap(y, m, r, c_, pc, *after):
                ts(m, r, pc, -PI2, ALU.is_gt, ALU.mult, *after)
                return stt(y, r, c_, m, ALU.add, ALU.add)

            def work():
                yield from pexp(dt_, dta, tmp[0], tmp[1], wk, *early)
                tt(dre, dt_, Are, ALU.mult)
                tt(dim, dt_, Aim, ALU.mult)
                er = tmp[4]
                yield from pexp(er, dre, tmp[0], tmp[1])
                yield from reduce2pi(tmp[5], tmp[0], dim)
                v = wrap(tmp[2], tmp[0], tmp[5], math.pi / 2, math.pi / 2)
                A(lambda e: e.activation(tmp[3], tmp[5], ACT.Sin, scale=SH), v)
                a = A(lambda e: e.activation(tmp[2], tmp[2], ACT.Sin, scale=SH), v)
                yield
                ec, es, t4, t5 = tmp[2], tmp[3], tmp[0], tmp[1]
                tt(ec, ec, er, ALU.mult, a)
                ts(ec, ec, -1.0, None, ALU.add)
                tt(es, es, er, ALU.mult)
                yield
                tt(cr, ec, Cre, ALU.mult)
                tt(t4, es, Cim, ALU.mult)
                tt(cr, cr, t4, ALU.subtract)
                yield
                tt(ci, ec, Cim, ALU.mult)
                tt(t4, es, Cre, ALU.mult)
                tt(ci, ci, t4, ALU.add)
                yield
                tt(t4, Are, Are, ALU.mult)
                tt(t5, Aim, Aim, ALU.mult)
                tt(t4, t4, t5, ALU.add)
                V(lambda e: e.reciprocal(t4, t4))
                ts(t4, t4, 2.0)
                yield
                tt(t5, cr, Are, ALU.mult)
                tt(ec, ci, Aim, ALU.mult)
                tt(t5, t5, ec, ALU.add)
                yield
                tt(ci, ci, Are, ALU.mult)
                tt(ec, cr, Aim, ALU.mult)
                tt(ci, ci, ec, ALU.subtract)
                yield
                tt(ci, ci, t4, ALU.mult)
                st = tt(cr, t5, t4, ALU.mult)
                yield
                sh4 = [128, 2, ND, 32]
                lb = l32.unsqueeze(2).to_broadcast(sh4)
                sh3 = (128, ND, 32)
                pend = None

                def products(blk, v):
                    u, q = blk % 2, blk % 4
                    bk = bank()
                    k = ("ps", bk)
                    for j in range(ND):
                        p = mm(PS[0:32, bk, j * 32:(j + 1) * 32], UV[:, u, 1, j, :], UV[:, u, 0, j, :], True, True, v,
                               *fr(k), sig=(j == ND - 1))
                    e_ = A(lambda e: e.activation(Kt[:, :, q * ND:(q + 1) * ND].rearrange("p a d -> p d a"),
                                                  PS[0:32, bk, 0:ND * 32].rearrange("p (d a) -> p d a", d=ND), ACT.Copy),
                           p, *(fk.get("kt", ()) if q == 0 else ()))
                    free[k] = [e_]
                    fk[("uv", u)] = [p]
                    if q == 3:
                        c0 = (blk - 3) * ND
                        fk["kt"] = [gkt.load(scr["K"].rearrange("(a b) n -> b a n", b=32)[:, :, c0:c0 + 4 * ND], Kt, e_)]

                for blk in range(D // ND):
                    u = blk % 2
                    ds = slice(blk * ND, (blk + 1) * ND)
                    dimb = dim[:, ds].unsqueeze(1).unsqueeze(3).to_broadcast(sh4)
                    dreb = dre[:, ds].unsqueeze(1).unsqueeze(3).to_broadcast(sh4)
                    g_ = gg(EXP, dreb, lb, ALU.mult, st, *fk.get("exp", ()))
                    tt(R, dimb, lb, ALU.mult)
                    yield
                    yield from reduce2pi(C_, Q, R, *fk.get("c", ()))
                    v = wrap(S_, Q[:, 0], C_[:, 0], colc[:, 0:1], colc[:, 1:2], *fk.get("s", ()))
                    yield
                    wrap(C_[:, 0], Q[:, 0], C_[:, 0], colc[:, 2:3], colc[:, 3:4])
                    yield
                    v = wrap(C_[:, 1], Q[:, 1], C_[:, 1], colc[:, 4:5], colc[:, 5:6])
                    yield
                    A(lambda e: e.activation(S_, S_, ACT.Sin, scale=SH), v)
                    a1 = A(lambda e: e.activation(C_, C_, ACT.Sin, scale=SH), v)
                    a2 = A(lambda e: e.activation(EXP, EXP, ACT.Exp), g_)
                    if pend:
                        products(*pend)
                    yield
                    q1 = gg(UV[:, u, 1], C_[:, 1], EXP[:, 1], ALU.mult, a2, *fk.get(("uv", u), ()))
                    q2 = gg(C_[:, 0], C_[:, 0], bc(cr[:, ds], 2, sh3), ALU.mult, a1)
                    q3 = gg(S_, S_, bc(ci[:, ds], 2, sh3), ALU.mult, a1)
                    yield
                    q4 = gg(S_, C_[:, 0], S_, ALU.subtract, q3)
                    yield
                    q5 = gg(UV[:, u, 0], S_, EXP[:, 0], ALU.mult, q4)
                    fk["exp"] = fk["s"] = [q5]
                    fk["c"] = [q4]
                    pend = (blk, q5)
                    yield
                yield
                products(*pend)

            gkt = K.group("gkt")
            it = work()

            def step(n):
                for _ in range(n):
                    if next(it, "end") == "end":
                        if not scr_done:
                            scr_done.append(gkt.tok())
                        return
            return step

        scr_done = []

        xattn_heads("L0_xattn_", 8, 64, 0.125, False, True)

        def moe():
            phase()
            NU = 41
            g = K.group("gmw")
            gm = K.group("gmm")
            WGU = ar.get(2, 2, NU, 128)
            WD = ar.get(NU, D)
            GW = ar.get(2, 32)
            gb = ar.get(32)
            gm.load(GW, d["gwT"].rearrange("(c p) n -> p c n", p=128))
            gm.load(gb, d["gate_bias"].partition_broadcast(128).rearrange("p a n -> p (a n)"))
            wl = []
            for s0, s1 in ((0, 4), (4, 16), (16, 28), (28, 41)):
                gg = K.group(f"gmw{s0}")
                gg.load(WGU[:, 0, :, s0:s1, :], d["moe_g"].rearrange("p (c e n) -> p c e n", c=2, e=NU)[:, :, s0:s1, :])
                gg.load(WGU[:, 1, :, s0:s1, :], d["moe_u"].rearrange("p (c e n) -> p c e n", c=2, e=NU)[:, :, s0:s1, :])
                gg.load(WD[:, s0:s1, :], d["moe_d"].rearrange("p (e n) -> p e n", e=NU)[:, s0:s1, :])
                wl += [gg.tok()] * (s1 - s0)
            ht = layernorm_T(X)
            s0 = ar.at
            sc = ar.get(NT, 32)
            sb_ = ar.get(NT, 32)
            gs = ar.get(NT, 8)
            tops = ar.get(NT, 4, 8)
            t8 = ar.get(NT, 8)
            sel = ar.get(NT, 32)
            cw = ar.get(NT, 48)
            wsum = ar.get(NT)
            for t in range(NT):
                for c in range(2):
                    p = mm(PS[:, 0, t * 32:(t + 1) * 32], HT[:, c, t * 128:(t + 1) * 128], GW[:, c, :],
                           c == 0, c == 1, ht[t], gm.tok(), sig=(c == 1))
            a = A(lambda e: e.activation(sc, PS[:, 0, :].rearrange("p (t n) -> p t n", t=NT), ACT.Sigmoid), p)
            V(lambda e: e.tensor_tensor(sb_, sc, bc(gb, 1, (128, NT, 32)), ALU.add), a)
            for t in range(NT):
                for q in range(4):
                    V(lambda e, t=t, q=q: e.max(tops[:, t, q, :], sb_[:, t, q * 8:(q + 1) * 8]))
            V(lambda e: e.memset(gs, NEG))
            V(lambda e: e.tensor_tensor(gs[:, :, 0:4], tops[:, :, :, 0], tops[:, :, :, 1], ALU.add))
            for t in range(NT):
                V(lambda e, t=t: e.max(t8[:, t, :], gs[:, t, :]))
            V(lambda e: e.tensor_tensor(gs[:, :, 0:4], gs[:, :, 0:4], bc(t8[:, :, 1], 2, (128, NT, 4)), ALU.is_ge))
            V(lambda e: e.tensor_scalar(gs[:, :, 0:4], gs[:, :, 0:4], -1.0, -NEG, ALU.add, ALU.mult))
            for q in range(4):
                V(lambda e, q=q: e.tensor_tensor(sb_[:, :, q * 8:(q + 1) * 8], sb_[:, :, q * 8:(q + 1) * 8],
                                                 bc(gs[:, :, q], 2, (128, NT, 8)), ALU.add))
            for t in range(NT):
                V(lambda e, t=t: e.max(t8[:, t, :], sb_[:, t, :]))
            V(lambda e: e.tensor_tensor(sel, sb_, bc(t8[:, :, 5], 2, (128, NT, 32)), ALU.is_ge))
            V(lambda e: e.tensor_tensor(sel, sel, sc, ALU.mult))
            V(lambda e: e.tensor_reduce(wsum, sel, AX.X, ALU.add))
            V(lambda e: e.tensor_scalar(wsum, wsum, 1e-20, None, ALU.add))
            V(lambda e: e.reciprocal(wsum, wsum))
            V(lambda e: e.tensor_scalar(wsum, wsum, 0.2, None, ALU.mult))
            V(lambda e: e.tensor_tensor(cw[:, :, 0:32], sel, bc(wsum, 2, (128, NT, 32)), ALU.mult))
            V(lambda e: e.tensor_tensor(sel, sb_, bc(t8[:, :, 0], 2, (128, NT, 32)), ALU.is_ge))
            s4 = sel.rearrange("p t (l r) -> p t l r", r=2)
            V(lambda e: e.tensor_tensor(cw[:, :, 32:48], s4[:, :, :, 0], s4[:, :, :, 1], ALU.max))
            a = V(lambda e: e.tensor_scalar(cw[:, :, 32:48], cw[:, :, 32:48], 0.1, None, ALU.mult))
            cwT = ar.get(T, parts=48)
            gc = K.group("gcw")
            for i in range(4):
                for j in range(4):
                    t = 4 * i + j
                    p = tr(PS[0:48, 1 + i % 2, j * 128:(j + 1) * 128], cw[:, t, :], ident, a,
                           *fr(("cwt", i % 2)), sig=(j == 3))
                e = A(lambda e, i=i: e.activation(cwT[:, i * 512:(i + 1) * 512], PS[0:48, 1 + i % 2, :], ACT.Copy), p)
                free[("cwt", i % 2)] = [e]
            gc.load(scr["cw"], cwT, e)
            wrote = gc.tok()
            pend = [(K.sem["dve"], K.n["dve"]), (K.sem["pe"], K.n["pe"]), wrote, (K.sem["act"], K.n["act"])]
            ar.at = s0
            NB_ = 4
            CB = ar.get(NB_, 512)
            SG = ar.get(2, 512)
            UU = ar.get(2, 512)
            AC = ar.get(2, 512)
            gcb = [K.group(f"gcb{i}") for i in range(NB_)]
            free_cb = {}
            bgstep = s4d(ar, lambda: 4 + 2 * ((now[0] + 1) % 2), pend)
            now = [0]
            free[("ps", 0)] = pend
            units = [(e, g4) for g4 in range(4) for e in range(NU)]
            actt = {}

            def up(i):
                e_, g4 = units[i]
                tk = slice(g4 * 512, (g4 + 1) * 512)
                u = i % 2
                if e_ < 40:
                    slot = i % NB_
                    G_ = gcb[slot]
                    deps = pend if i < NB_ else [wrote]
                    if e_ < 32:
                        G_.load(CB[:, slot, :], scr["cw"][e_:e_ + 1, tk].partition_broadcast(128)
                                .rearrange("p a n -> p (a n)"), *deps, *free_cb.get(slot, ()))
                    else:
                        l = 32 + 2 * (e_ - 32)
                        G_.load(CB[0:64, slot, :], scr["cw"][l:l + 1, tk].partition_broadcast(64)
                                .rearrange("p a n -> p (a n)"), *deps, *free_cb.get(slot, ()))
                        G_.load(CB[64:128, slot, :], scr["cw"][l + 1:l + 2, tk].partition_broadcast(64)
                                .rearrange("p a n -> p (a n)"))
                    ct = G_.tok()
                for m in range(2):
                    bk = 2 * u + m
                    for c in range(2):
                        p = mm(PS[:, bk, :], WGU[:, m, c, e_, :], HT[:, c, tk], c == 0, c == 1, wl[e_],
                               *(pend if i < 2 else ()), *ht[4 * g4:4 * g4 + 4], *fr(("ps", bk)), sig=(c == 1))
                    if m == 0:
                        s = A(lambda e, bk=bk, u=u: e.activation(SG[:, u, :], PS[:, bk, :], ACT.Silu), p,
                              *fr(("SG", u)), *(pend if i < 2 else ()))
                        free[("ps", bk)] = [s]
                if e_ < 40:
                    v1 = V(lambda e, bk=bk, u=u, slot=slot: e.tensor_tensor(UU[:, u, :], PS[:, bk, :], CB[:, slot, :], ALU.mult),
                           p, ct, *fr(("UU", u)))
                    free[("ps", bk)] = [v1]
                    free_cb[slot] = [v1]
                    a_ = G(lambda e, u=u: e.tensor_tensor(AC[:, u, :], UU[:, u, :], SG[:, u, :], ALU.mult), v1, s,
                           *fr(("AC", u)))
                    free[("UU", u)] = [a_]
                else:
                    a_ = V(lambda e, bk=bk, u=u: e.tensor_tensor(AC[:, u, :], PS[:, bk, :], SG[:, u, :], ALU.mult),
                           p, s, *fr(("AC", u)))
                    free[("ps", bk)] = [a_]
                free[("SG", u)] = [a_]
                actt[i] = a_

            def down(i):
                e_, g4 = units[i]
                u = i % 2
                for j in range(4):
                    bk = 4 + 2 * (g4 % 2) + j // 2
                    p = mm(PS[:, bk, (j % 2) * 256:(j % 2) * 256 + 256], AC[:, u, j * 128:(j + 1) * 128], WD[:, e_, :],
                           e_ == 0 and j % 2 == 0, e_ == NU - 1, actt[i], *fr(("ps", bk)), sig=(j == 3))
                free[("AC", u)] = [p]
                if e_ == NU - 1:
                    for q in range(2):
                        bk = 4 + 2 * (g4 % 2) + q
                        t = 4 * g4 + 2 * q
                        v = V(lambda e, bk=bk, t=t: e.tensor_tensor(
                            X[:, t:t + 2, :], X[:, t:t + 2, :],
                            PS[:, bk, :].rearrange("p (a n) -> p a n", a=2), ALU.add), p)
                        free[("ps", bk)] = [v]

            for i in range(len(units) + 1):
                if i < len(units):
                    up(i)
                if i:
                    down(i - 1)
                if i < len(units):
                    now[0] = units[i][1]
                    bgstep(4)
            bgstep(10 ** 6)

        if True:
            moe()
        if True:
            xattn_heads("L1_xattn_", 16, 16, 0.25, True, False)

        def peer():
            phase()
            H = 8
            RW = ar.get(16, 64, parts=1)
            Mk = ar.get(2, 1024)
            s1 = ar.at
            Hn = ar.get(NT, D)
            gw = K.group("gpw")
            Wq = ar.get(2, 2048)
            WqT = ar.get(16, D)
            KY = ar.get(16, 64)
            gam = ar.get(16)
            bet = ar.get(16)
            gw.load(Wq, d["peer_wq"].rearrange("(c p) n -> p c n", p=128))
            gw.load(WqT, d["peer_wqT"].rearrange("(s p) n -> p s n", p=128))
            gw.load(KY, d["peer_keysT"])
            gw.load(gam, d["bn_gamma"])
            gw.load(bet, d["bn_beta"])
            w = gw.tok()
            ln_stats(X)
            ht = []
            for t in range(NT):
                a = ln_tile(Hn[:, t, :], X, t)
                ht.append(transpose_tile(Hn[:, t, :], t, a, 4 + t % 4)[1])
                for kc in range(2):
                    mm(PS[:, kc, 0:256], Hn[:, t, kc * 128:(kc + 1) * 128], Hn[:, t, :], t == 0, False)
                p = mm(PS[0:1, 2, 0:256], ones[:, 0:1], Hn[:, t, :], t == 0, t == NT - 1, t_ones, sig=True)
                for kc in range(2):
                    p = mm(PS[:, 3, 8 * kc:8 * kc + 1], Hn[:, t, kc * 128:(kc + 1) * 128], ones[:, 0:1],
                           t == 0 and kc == 0, t == NT - 1, sig=True)
            srow = ar.get(2, D, parts=1)
            mcol = ar.get(2)
            V(lambda e: e.tensor_copy(srow[:, 0, :], PS[0:1, 2, 0:256]), p)
            V(lambda e: e.tensor_scalar(srow[:, 1, :], PS[0:1, 2, 0:256], -1.0 / T, None, ALU.mult))
            a = V(lambda e: e.tensor_scalar(mcol, PS[:, 3, 0:16].rearrange("p (c n) -> p c n", c=2)[:, :, 0], 1.0 / T, None, ALU.mult))
            for kc in range(2):
                p = mm(PS[:, kc, 0:256], srow[:, 1, kc * 128:(kc + 1) * 128], srow[:, 0, :], False, True, a, sig=True)
            C = ar.get(2, D)
            a = A(lambda e: e.activation(C, PS[:, 0:2, 0:256], ACT.Copy), p)
            Gm = ar.get(2, 2048)
            for kc in range(2):
                for q in range(4):
                    bk = (kc * 4 + q) % 4
                    sl = slice(q * 512, (q + 1) * 512)
                    for c in range(2):
                        p = mm(PS[:, bk, :], C[:, c, kc * 128:(kc + 1) * 128], Wq[:, c, sl], c == 0, c == 1,
                               a, w, *fr(("ps", bk)), sig=(c == 1))
                    v = V(lambda e, kc=kc, sl=sl, bk=bk: e.tensor_tensor(Gm[:, kc, sl], PS[:, bk, :], Wq[:, kc, sl], ALU.mult), p)
                    free[("ps", bk)] = [v]
            for s in range(16):
                for c in range(2):
                    mm(PS[:, 4, s:s + 1], Gm[:, c, s * 128:(s + 1) * 128], ones[:, 0:1], s == 0 and c == 0,
                       c == 1, v, *fr(("ps", 4)))
            for s in range(16):
                for c in range(2):
                    p = mm(PS[:, 5, s:s + 1], Wq[:, c, s * 128:(s + 1) * 128], mcol[:, c:c + 1],
                           s == 0 and c == 0, c == 1, *fr(("ps", 5)), sig=(s == 15 and c == 1))
            av = ar.get(16)
            bv = ar.get(16)
            a = V(lambda e: e.tensor_scalar(av, PS[:, 4, 0:16], 1.0 / T, 1e-5, ALU.mult, ALU.add), p)
            a = A(lambda e: e.activation(av, av, ACT.Sqrt), a)
            V(lambda e: e.reciprocal(av, av), a)
            V(lambda e: e.tensor_tensor(av, av, gam, ALU.mult), w)
            V(lambda e: e.tensor_tensor(bv, PS[:, 5, 0:16], av, ALU.mult))
            V(lambda e: e.tensor_tensor(bv, bet, bv, ALU.subtract))
            KA = ar.get(16, 64)
            a = V(lambda e: e.tensor_tensor(KA, KY, bc(av, 2, (128, 16, 64)), ALU.mult))
            for kc in range(2):
                for s in range(16):
                    bk = 2 * kc + s // 8
                    p = mm(PS[:, bk, (s % 8) * 64:(s % 8) * 64 + 64], WqT[:, s, kc * 128:(kc + 1) * 128], KA[:, s, :],
                           True, True, a, *fr(("ps", bk)), sig=(s == 15))
                A(lambda e, kc=kc: e.activation(Mk[:, kc, :].rearrange("p (a n) -> p a n", a=2),
                                                PS[:, 2 * kc:2 * kc + 2, :], ACT.Copy), p)
            for s in range(16):
                p = mm(PS[0:1, 4 + s // 8, (s % 8) * 64:(s % 8) * 64 + 64], bv[:, s:s + 1], KY[:, s, :], True, True,
                       sig=(s == 15))
            A(lambda e: e.activation(RW.rearrange("p (a s) n -> p a (s n)", a=2), PS[0:1, 4:6, :], ACT.Copy), p)
            for key in K.q:
                K.q[key].append(([(K.sem[k], K.n[k]) for k in K.sem], lambda e: None, None))
            free.clear()
            ar.at = s1
            gd = K.group("gpd")
            DT_ = ar.get(2, 4096)
            UP = ar.get(32, D)
            gd.load(DT_, d["downT"].rearrange("(c p) n -> p c n", p=128))
            gd.load(UP, d["up_embed"].rearrange("(c p) n -> p c n", p=128))
            wd = gd.tok()
            iota = ar.get(128)
            gd.load(iota, d["c_iota"].partition_broadcast(128).rearrange("p a n -> p (a n)"))
            ti = wd = gd.tok()
            U32 = mybir.dt.uint32
            SXY = ar.get(2, 16, 64)
            GG = ar.get(2, 32, 256)
            OR = 2
            O = ar.get(OR, 128, 16, dt=F16)
            R = ar.get(OR, 32, 16, dt=F16)
            IDX = ar.get(4, 3, 128, dt=F16)
            IR = ar.get(128, 16, dt=F16)
            w1h = ar.get(64, dt=F16)
            tir = V(lambda e: e.tensor_copy(IR, bc(iota, 2, (128, 128, 16))), ti)
            sm_ = ar.get(16, 8)
            ixu = ar.get(16, 8, dt=I32).bitcast(U32)
            cand = ar.get(8, 64)
            top = ar.get(8, 8)
            pku = ar.get(8, 8, dt=I32).bitcast(U32)
            abu = ar.get(2, 64, dt=I32).bitcast(U32)
            EQ = cand.rearrange("p h (a b) -> p h a b", a=8)
            ij = ar.get(2, 64)
            w12 = ij[:, 0, :]
            rz = ar.get(8)
            e8 = ar.get(8, 8)
            TRS = ar.get(3, 2, 64)

            def sims(t):
                u = t % 2
                for q in range(2):
                    for c in range(2):
                        mm(PS[:, 0, :], HT[:, c, t * 128:(t + 1) * 128], Mk[:, c, q * 512:(q + 1) * 512], c == 0,
                           False, ht[t], *fr(("ps", 0)))
                    p = mm(PS[:, 0, :], ones[0:1, :], RW.rearrange("p (a s) n -> p a (s n)", a=2)[:, q, :],
                           False, True, sig=True)
                    e = A(lambda e, q=q: e.activation(
                        SXY[:, u, :, :].rearrange("p (a s) n -> p a (s n)", a=2)[:, q, :], PS[:, 0, :], ACT.Copy),
                        p, *fr(("SXY", u)))
                    free[("ps", 0)] = [e]
                return e

            def prep(t, st):
                u = t % 2
                for s in range(16):
                    (Vn if s else V)(lambda e, s=s: e.max(sm_[:, s, :], SXY[:, u, s, :]), st)
                for s in range(16):
                    v = (Vn if s else V)(lambda e, s=s: e.max_index(ixu[:, s, :], sm_[:, s, :], SXY[:, u, s, :]))
                free[("SXY", u)] = [v]
                V(lambda e: e.tensor_tensor(cand.rearrange("p h (a b) -> p h a b", a=8),
                                            sm_[:, 0:8, :].unsqueeze(3).to_broadcast([128, 8, 8, 8]),
                                            sm_[:, 8:16, :].unsqueeze(2).to_broadcast([128, 8, 8, 8]), ALU.add))
                for h in range(8):
                    (Vn if h else V)(lambda e, h=h: e.max(top[:, h, :], cand[:, h, :]))
                for h in range(8):
                    (Vn if h else V)(lambda e, h=h: e.max_index(pku[:, h, :], top[:, h, :], cand[:, h, :]))
                a = V(lambda e: e.tensor_tensor(e8, top, bc(top[:, :, 0], 2, (128, 8, 8)), ALU.subtract))
                a = A(lambda e: e.activation(e8, e8, ACT.Exp), a)
                pf = pku.rearrange("p h k -> p (h k)")
                V(lambda e: e.tensor_scalar(abu[:, 0, :], pf, 3, None, ALU.logical_shift_right))
                V(lambda e: e.tensor_scalar(abu[:, 1, :], pf, 7, None, ALU.bitwise_and))
                for m in range(2):
                    V(lambda e, m=m: e.tensor_tensor(
                        EQ, abu[:, m, :].rearrange("p (h k) -> p h k", h=8).unsqueeze(3).to_broadcast([128, 8, 8, 8]),
                        iota[:, 0:8].unsqueeze(1).unsqueeze(1).to_broadcast([128, 8, 8, 8]), ALU.is_equal), ti)
                    V(lambda e, m=m: e.tensor_tensor(
                        EQ, EQ, ixu[:, 8 * m:8 * m + 8, :].unsqueeze(2).to_broadcast([128, 8, 8, 8]), ALU.mult))
                    V(lambda e, m=m: e.tensor_reduce(ij[:, m, :].rearrange("p (h k) -> p h k", h=8), EQ, AX.X, ALU.add))
                V(lambda e: e.scalar_tensor_tensor(abu[:, 0, :], ij[:, 0, :], 64.0, ij[:, 1, :], ALU.mult, ALU.add))
                V(lambda e: e.tensor_scalar(abu[:, 1, :], abu[:, 0, :], 7, None, ALU.logical_shift_right))
                V(lambda e: e.tensor_scalar(abu[:, 0, :], abu[:, 0, :], 127, None, ALU.bitwise_and))
                V(lambda e: e.tensor_copy(TRS[:, 0:2, :, :], abu.unsqueeze(2).to_broadcast([128, 2, 2, 64])),
                  *fr("TRS"))
                V(lambda e: e.tensor_reduce(rz, e8, AX.X, ALU.add), a)
                V(lambda e: e.reciprocal(rz, rz))
                V(lambda e: e.tensor_scalar(rz, rz, WS, None, ALU.mult))
                V(lambda e: e.tensor_tensor(w12.rearrange("p (h k) -> p h k", h=8), e8, bc(rz, 2, (128, 8, 8)), ALU.mult))
                V(lambda e: e.tensor_copy(w1h, w12))
                V(lambda e: e.tensor_copy(TRS[:, 2, 0, :], w1h))
                return V(lambda e: e.tensor_tensor(TRS[:, 2, 1, :], w12, w1h, ALU.subtract))

            def turn(t, v):
                for m in range(3):
                    p = tr(PS[:, 0, m * 128:(m + 1) * 128], TRS[:, m, :, :].rearrange("p a b -> p (a b)"), ident, v,
                           *fr(("ps", 0)), sig=(m == 2))
                free["TRS"] = [p]
                e = A(lambda e: e.activation(IDX[:, t % 4, :, :], PS[:, 0, 0:384].rearrange("p (m n) -> p m n", m=3),
                                             ACT.Copy), p, *fr(("IDX", t % 4)))
                free[("ps", 0)] = [e]
                return e

            def scatter(t, it, gt, between, n_between=1):
                g2 = GG[:, (t // 2) % 2, :, :]
                ix = IDX[:, t % 4, :, :]
                for q in range(8):
                    r_ = q % OR
                    ts_ = slice(q * 16, q * 16 + 16)
                    ov = Vn(lambda e, r_=r_, ts_=ts_: e.tensor_tensor(O[:, r_, :, :], bc(ix[:, 0, ts_], 1, (128, 128, 16)),
                                                                IR, ALU.is_equal), it, tir, *fr(("O", r_)))
                    rv = Vn(lambda e, r_=r_, ts_=ts_: e.tensor_tensor(R[:, r_, :, :], bc(ix[:, 1, ts_], 1, (128, 32, 16)),
                                                                IR[:, 0:32, :], ALU.is_equal), it, tir, *fr(("O", r_)))
                    v = G(lambda e, r_=r_, ts_=ts_: e.tensor_tensor(R[:, r_, :, :], R[:, r_, :, :],
                                                                    bc(ix[:, 2, ts_], 1, (128, 32, 16)), ALU.mult), rv)
                    bk = 4 + q % 4
                    for i in range(16):
                        p = mm(PS[:, bk, i * 32:(i + 1) * 32], O[:, r_, :, i], R[:, r_, :, i], True, True, v, ov,
                               *fr(("ps", bk)), sig=(i == 15))
                    free[("O", r_)] = [p]
                    k = (t % 2) * 128 + q * 16
                    pv.append((g2[:, :, k:k + 16].rearrange("p c n -> p n c"), bk, p, gt))
                    for f in range(n_between):
                        if between:
                            between.pop(0)()
                    if len(pv) > 1:
                        apply_()
                free[("IDX", t % 4)] = [v, ov]

            pv = []
            last = {}

            def apply_():
                gv, bk, p, gt = pv.pop(0)
                w_ = Vn(lambda e: e.tensor_tensor(gv, gv, PS[:, bk, :].rearrange("p (n c) -> p n c", n=16),
                                                 ALU.mult), p, gt)
                free[("ps", bk)] = [w_]
                last["v"] = w_

            ghid = {}

            def hidden_steps(g_):
                u = g_ % 2

                def step(c2):
                    bk = 2 + c2 % 2
                    for h in range(2):
                        c = 2 * c2 + h
                        for kc in range(2):
                            p = mm(PS[:, bk, h * 256:(h + 1) * 256], DT_[:, kc, c * 128:(c + 1) * 128],
                                   HT[:, kc, g_ * 256:(g_ + 1) * 256], kc == 0, kc == 1, wd, ht[2 * g_], ht[2 * g_ + 1],
                                   *fr(("ps", bk)), sig=(h == 1 and kc == 1))
                    a = A(lambda e, bk=bk, c2=c2, u=u: e.activation(
                        GG[:, u, 2 * c2:2 * c2 + 2, :].rearrange("p a n -> p (a n)"), PS[:, bk, :],
                        ACT.Gelu_apprx_tanh), p, *fr(("GG", u)))
                    free[("ps", bk)] = [a]
                    ghid[g_] = a
                return [lambda c2=c2: step(c2) for c2 in range(16)]

            def outp(g_):
                u = g_ % 2
                for tl in range(2):
                    for c in range(32):
                        p = mm(PS[:, 1, tl * 256:(tl + 1) * 256], GG[:, u, c, tl * 128:(tl + 1) * 128], UP[:, c, :],
                               c == 0, c == 31, last["v"], *fr(("ps", 1)), sig=(c == 31))
                free[("GG", u)] = [p]
                return p

            def addx(g_, p):
                free[("ps", 1)] = [V(lambda e: e.scalar_tensor_tensor(
                    X[:, 2 * g_:2 * g_ + 2, :], PS[:, 1, :].rearrange("p (a n) -> p a n", a=2), 1.0 / WS,
                    X[:, 2 * g_:2 * g_ + 2, :], ALU.mult, ALU.add), p)]

            st = [sims(0), sims(1)]
            it = {}
            v0 = prep(0, st[0])
            for f in hidden_steps(0):
                f()
            it[0] = turn(0, v0)
            it[1] = turn(1, prep(1, st[1]))
            for g_ in range(8):
                nx = g_ + 1 < 8
                steps = hidden_steps(g_ + 1) if nx else []
                if nx:
                    st = [sims(2 * g_ + 2), sims(2 * g_ + 3)]
                for t in (2 * g_, 2 * g_ + 1):
                    scatter(t, it[t], ghid[g_], steps)
                apply_()
                for f in steps:
                    f()
                po = outp(g_)
                if nx:
                    for t in (2 * g_ + 2, 2 * g_ + 3):
                        it[t] = turn(t, prep(t, st[t % 2]))
                addx(g_, po)

        if True:
            peer()

        def l2x():
            phase()
            gw = K.group("gl2")
            XT0 = ar.get(NT, D)
            X1 = ar.get(NT, D)
            AT = ar.get(T, parts=S2)
            ZF = ar.get(2, 1024, parts=S2)
            FB = ar.get(1024, parts=1)
            gin = ar.get(D)
            bin_ = ar.get(D)
            dsk = ar.get(D)
            mg = ar.get(1)
            K128 = ar.get(8, D)
            kt128 = K.group("gkm").load(K128, scr["K"].rearrange("(l p) n -> p l n", p=128), *scr_done)
            for o_, n_ in ((gin, "g_norm_in"), (bin_, "b_norm_in"), (dsk, "D_skip"), (mg, "mod_gate")):
                gw.load(o_, d["L2_" + n_].partition_broadcast(128).rearrange("p a n -> p (a n)"))
            gw.load(FB[:, 0:512], d["L2_b_film_in"])
            gw.load(FB[:, 512:1024], d["L2_b_film_out"])
            s1 = ar.at
            WK = ar.get(2, 128, parts=96)
            WV = ar.get(2, 256, parts=96)
            WQ = ar.get(4, D, parts=32)
            WF = ar.get(2, 1024)
            tm8 = ar.get(NT, dt=U8)
            tmf = ar.get(NT)
            gw.load(WK, d["L2_Wk"].rearrange("(c p) n -> p c n", p=96))
            gw.load(WV, d["L2_Wv"].rearrange("(c p) n -> p c n", p=96))
            gw.load(WQ, d["L2_WqT"].rearrange("(h p) n -> p h n", p=32))
            gw.load(WF[:, :, 0:512], d["L2_W_film_in"].rearrange("(c p) n -> p c n", p=128))
            gw.load(WF[:, :, 512:1024], d["L2_W_film_out"].rearrange("(c p) n -> p c n", p=128))
            gw.load(tm8, d["mask1T"])
            w = gw.tok()
            V(lambda e: e.tensor_copy(tmf, tm8), w)
            V(lambda e: e.tensor_scalar(tmf, tmf, 0.25, None, ALU.mult))
            ln_stats(X)
            ht = []
            for t in range(NT):
                a = ln_tile(XT0[:, t, :], X, t)
                ht.append(transpose_tile(XT0[:, t, :], t, a, 4 + t % 4)[1])
            KT = ar.get(4, 2 * S2, parts=32)
            VT = ar.get(2, 2 * S2)
            M = ar.get(2, 2, 4 * S2)
            kt = small_proj(KT, WK, 32, 4, w)
            vt = small_proj(VT, WV, 128, 2, w)
            mt = build_M(M, WQ, KT, 32, 4, 1, kt, w)
            for b in range(2):
                for q in range(2):
                    bk = 2 * b + q
                    for c in range(2):
                        p = mm(PS[0:S2, bk, :], VT[:, c, b * S2:(b + 1) * S2], WF[:, c, q * 512:(q + 1) * 512], c == 0,
                               c == 1, *vt, *fr(("ps", bk)), sig=(c == 1))
                    v = V(lambda e, b=b, q=q, bk=bk: e.tensor_scalar(ZF[:, b, q * 512:(q + 1) * 512], PS[0:S2, bk, :],
                                                                     mg[0:S2, 0:1], None, ALU.mult), p)
                    free[("ps", bk)] = [v]
            V(lambda e: e.tensor_scalar(FB, FB, mg[0:1, 0:1], None, ALU.mult))
            for o_ in (0, 512):
                zt = V(lambda e, o_=o_: e.tensor_scalar(FB[:, o_:o_ + 256], FB[:, o_:o_ + 256], 1.0, None, ALU.add))
            W = 4 * S2
            mrow, t_mrow = mask_row()
            SS = ar.get(2, W)
            SR = ar.get(W)
            EE = ar.get(2, W)
            mx = ar.get(2, 4, 8)
            t8 = ar.get(4, 8)
            sm = ar.get(4)
            AM = ar.get(2, S2)
            for t in range(NT):
                b, u = t // 8, t % 2
                k = ("ps", u)
                o = PS[:, u, 0:W]
                for c in range(2):
                    mm(o, HT[:, c, t * 128:(t + 1) * 128], M[:, c, b, :], c == 0, False, ht[t], *mt[-2:], *fr(k))
                p = mm(o, ones[0:1, :], mrow[:, b, 0:W], False, True, t_mrow, sig=True)
                a = A(lambda e, u=u, o=o: e.activation(SS[:, u, :], o, ACT.Copy), p, *fr(("SS", u)))
                free[k] = [a]
                for h in range(4):
                    hs = slice(h * S2, (h + 1) * S2)
                    V(lambda e, h=h, u=u, hs=hs: e.max(mx[:, u, h, :], SS[:, u, hs]), a)
                    V(lambda e, h=h, u=u, hs=hs: e.match_replace(SR[:, hs], mx[:, u, h, :], SS[:, u, hs], -3.0e38))
                    V(lambda e, h=h, hs=hs: e.max(t8[:, h, :], SR[:, hs]))
                    for r in range(2):
                        V(lambda e, h=h, hs=hs: e.match_replace(SR[:, hs], t8[:, h, :], SR[:, hs], -3.0e38))
                        V(lambda e, h=h, hs=hs: e.max(t8[:, h, :], SR[:, hs]))
                v = V(lambda e, u=u: e.tensor_tensor(
                    EE[:, u, :].rearrange("p (h j) -> p h j", h=4), SS[:, u, :].rearrange("p (h j) -> p h j", h=4),
                    bc(mx[:, u, :, 0], 2, (128, 4, S2)), ALU.subtract))
                a = A(lambda e, u=u: e.activation(EE[:, u, :], EE[:, u, :], ACT.Exp, scale=32.0 ** -0.5), v)
                for h in range(4):
                    hs = slice(h * S2, (h + 1) * S2)
                    v = V(lambda e, h=h, u=u, hs=hs: e.scalar_tensor_tensor(
                        EE[:, u, hs], SS[:, u, hs], t8[:, h, 7:8], EE[:, u, hs], ALU.is_ge, ALU.mult), a)
                free[("SS", u)] = [v]
                V(lambda e, u=u: e.tensor_reduce(sm, EE[:, u, :].rearrange("p (h j) -> p h j", h=4), AX.X, ALU.add))
                V(lambda e: e.reciprocal(sm, sm))
                V(lambda e, t=t: e.tensor_scalar(sm, sm, tmf[:, t:t + 1], None, ALU.mult))
                V(lambda e, u=u: e.tensor_scalar(AM[:, u, :], EE[:, u, 0:S2], sm[:, 0:1], None, ALU.mult), *fr(("AM", u)))
                for h in range(1, 4):
                    hs = slice(h * S2, (h + 1) * S2)
                    v = V(lambda e, h=h, u=u, hs=hs: e.scalar_tensor_tensor(
                        AM[:, u, :], EE[:, u, hs], sm[:, h:h + 1], AM[:, u, :], ALU.mult, ALU.add))
                p = tr(PS[0:S2, 2 + u, 0:128], AM[:, u, :], ident, v, *fr(("ps", 2 + u)), sig=True)
                free[("AM", u)] = [p]
                e_ = A(lambda e, t=t, u=u: e.activation(AT[:, t * 128:(t + 1) * 128], PS[0:S2, 2 + u, 0:128], ACT.Copy), p)
                free[("ps", 2 + u)] = [e_]
            ln_stats(XT0)
            for t in range(NT):
                b, u = t // 8, t % 2
                ln_tile(X1[:, t, :], XT0, t)
                V(lambda e, t=t: e.tensor_tensor(X1[:, t, :], X1[:, t, :], gin, ALU.mult))
                V(lambda e, t=t: e.tensor_tensor(X1[:, t, :], X1[:, t, :], bin_, ALU.add))
                k = ("ps", 4 + u)
                mm(PS[:, 4 + u, :], AT[:, t * 128:(t + 1) * 128], ZF[:, b, 0:512], True, False, e_, zt, *fr(k))
                p = mm(PS[:, 4 + u, :], ones[0:1, :], FB[:, 0:512], False, True, sig=True)
                V(lambda e, t=t, u=u: e.tensor_tensor(X1[:, t, :], X1[:, t, :], PS[:, 4 + u, 0:256], ALU.mult), p)
                v = V(lambda e, t=t, u=u: e.tensor_tensor(X1[:, t, :], X1[:, t, :], PS[:, 4 + u, 256:512], ALU.add))
                free[k] = [v]
            x1t = v
            all_ = [(K.sem[k], K.n[k]) for k in K.sem if K.n[k]]
            for key in K.q:
                K.q[key].append((list(all_), lambda e: None, None))
            free.clear()
            ar.at = s1
            s2 = s1

            def tt(o, a_, b_, op, *after):
                return V(lambda e: e.tensor_tensor(o, a_, b_, op), *after)

            Y = ar.get(8, 2, 512)
            FF = ar.get(2, 8, 2, 128)
            KF = ar.get(2, 2, D)
            TP = ar.get(4, 512)
            gf = [K.group("gf0"), K.group("gf1")]
            bcx = lambda a_: a_.unsqueeze(1).to_broadcast([128, 2, D])
            r2 = lambda a_: a_.rearrange("p (b n) -> p b n", b=2)
            for j in range(8):
                u = j % 2
                gf[u].load(FF[:, u, :, :, :], d["c_fwd"][j].rearrange("p (l r n) -> p l r n", l=8, r=2), *fr(("FF", u)))
                ff = gf[u].tok()
                for r in range(2):
                    k = ("ps", 2 * u + r)
                    for lt in range(8):
                        p = mm(PS[:, 2 * u + r, :], FF[:, u, lt, r, :],
                               X1.rearrange("p (b l) n -> p b l n", b=2)[:, :, lt, :],
                               lt == 0, lt == 7, ff, x1t, *fr(k), sig=(lt == 7))
                for r in range(2):
                    for lt in range(8):
                        p = mm(PS[:, 4 + u, r * 256:(r + 1) * 256], FF[:, u, lt, r, :], K128[:, lt, :],
                               lt == 0, lt == 7, kt128, *fr(("ps", 4 + u)), sig=(lt == 7))
                free[("FF", u)] = [p]
                a = A(lambda e, u=u: e.activation(KF[:, u, :, :], r2(PS[:, 4 + u, :]), ACT.Copy), p, *fr(("KF", u)))
                free[("ps", 4 + u)] = [a]
                xr, xi = r2(PS[:, 2 * u, :]), r2(PS[:, 2 * u + 1, :])
                kr, ki = bcx(KF[:, u, 0, :]), bcx(KF[:, u, 1, :])
                tt(r2(TP[:, 0, :]), xr, kr, ALU.mult, a, *fr("TP"))
                tt(r2(TP[:, 1, :]), xi, ki, ALU.mult)
                tt(r2(TP[:, 2, :]), xr, ki, ALU.mult)
                v = tt(r2(TP[:, 3, :]), xi, kr, ALU.mult)
                free[("ps", 2 * u)] = [v]
                free[("ps", 2 * u + 1)] = [v]
                free[("KF", u)] = [v]
                G(lambda e, j=j: e.tensor_tensor(Y[:, j, 0, :], TP[:, 0, :], TP[:, 1, :], ALU.subtract), v)
                g_ = G(lambda e, j=j: e.tensor_tensor(Y[:, j, 1, :], TP[:, 2, :], TP[:, 3, :], ALU.add))
                free["TP"] = [g_]
            yt = g_
            tmpb = ar.get(2, D)
            gi = [K.group("gi0"), K.group("gi1")]
            for lt in range(8):
                u = lt % 2
                FI = FF[:, u, :, :, :]
                gi[u].load(FI, d["c_inv"][lt].rearrange("p (l r n) -> p l r n", l=8, r=2), *fr(("FF", u)))
                k = ("ps", u)
                for j in range(8):
                    for r in range(2):
                        p = mm(PS[:, u, :], FI[:, j, r, :], Y[:, j, r, :], j == 0 and r == 0, j == 7 and r == 1,
                               gi[u].tok(), yt, *fr(k), sig=(j == 7 and r == 1))
                free[("FF", u)] = [p]
                pc = p
                for b in range(2):
                    t = b * 8 + lt
                    k2 = ("ps", 4 + b)
                    mm(PS[:, 4 + b, :], AT[:, t * 128:(t + 1) * 128], ZF[:, b, 512:1024], True, False, *fr(k2))
                    p = mm(PS[:, 4 + b, :], ones[0:1, :], FB[:, 512:1024], False, True, sig=True)
                    tb = tmpb[:, b, :]
                    tt(tb, X1[:, t, :], dsk, ALU.mult, pc)
                    v0 = tt(tb, tb, PS[:, u, b * 256:(b + 1) * 256], ALU.add)
                    tt(tb, tb, PS[:, 4 + b, 0:256], ALU.mult, p)
                    v1 = tt(tb, tb, PS[:, 4 + b, 256:512], ALU.add)
                    free[k2] = [v1]
                    tt(XT0[:, t, :], XT0[:, t, :], tb, ALU.add)
                free[k] = [v0]
            for key in K.q:
                K.q[key].append(([(K.sem[k], K.n[k]) for k in K.sem], lambda e: None, None))
            free.clear()
            ar.at = s1
            gn = K.group("gn")
            vec = ar.get(4, D)
            W1 = ar.get(2, 1024)
            b1c = ar.get(8)
            W2 = ar.get(8, D)
            b2r = ar.get(D, parts=1)
            for i, n_ in enumerate(("g_ffn", "b_ffn", "g_norm_out", "b_norm_out")):
                gn.load(vec[:, i, :], d["L2_" + n_].partition_broadcast(128).rearrange("p a n -> p (a n)"))
            gn.load(W1, d["L2_W1"].rearrange("(c p) n -> p c n", p=128))
            gn.load(W2, d["L2_W2"].rearrange("(c p) n -> p c n", p=128))
            gn.load(b1c, d["L2_b1"])
            gn.load(b2r, d["L2_b2"])
            wn = gn.tok()
            ln_stats(XT0)
            Hb = ar.get(4, D)
            ht = []
            for t in range(NT):
                u = t % 4
                ln_tile(Hb[:, u, :], XT0, t, *fr(("hb", u)))
                tt(Hb[:, u, :], Hb[:, u, :], vec[:, 0, :], ALU.mult, wn)
                a = tt(Hb[:, u, :], Hb[:, u, :], vec[:, 1, :], ALU.add)
                p, e = transpose_tile(Hb[:, u, :], t, a, 4 + t % 4)
                free[("hb", u)] = [p]
                ht.append(e)
            ffn(W1, b1c, W2, b2r, wn, ht, ACT.Gelu,
                lambda t, n, ps, p: tt(XT0[:, t:t + n, :], XT0[:, t:t + n, :], ps, ALU.add, p))
            ln_stats(XT0)
            for t in range(NT):
                u = t % 4
                ln_tile(Hb[:, u, :], XT0, t, *fr(("hb", u)))
                tt(Hb[:, u, :], Hb[:, u, :], vec[:, 2, :], ALU.mult)
                tt(Hb[:, u, :], Hb[:, u, :], vec[:, 3, :], ALU.add)
                free[("hb", u)] = [tt(X[:, t, :], X[:, t, :], Hb[:, u, :], ALU.add)]

        def ffn(W1, b1c, W2, b2r, ready, ht, func, add):
            AT_ = ar.get(2, 8, 512)
            at = {}

            def up(g4):
                u = g4 % 2
                for f in range(8):
                    bk = f % 4
                    for c in range(2):
                        p = mm(PS[:, bk, :], W1[:, c, f * 128:(f + 1) * 128], HT[:, c, g4 * 512:(g4 + 1) * 512], c == 0,
                               c == 1, ready, *ht[4 * g4:4 * g4 + 4], *fr(("ps", bk)), sig=(c == 1))
                    a = A(lambda e, f=f, bk=bk, u=u: e.activation(AT_[:, u, f, :], PS[:, bk, :], func, bias=b1c[:, f:f + 1]),
                          p, *fr(("AT_", u)))
                    free[("ps", bk)] = [a]
                at[g4] = a

            def down(g4):
                u = g4 % 2
                for q in range(2):
                    bk = 4 + 2 * u + q
                    for j in range(2):
                        tl = 2 * q + j
                        o = PS[:, bk, j * 256:(j + 1) * 256]
                        for f in range(8):
                            mm(o, AT_[:, u, f, tl * 128:(tl + 1) * 128], W2[:, f, :], f == 0, False, at[g4],
                               *fr(("ps", bk)))
                        p = mm(o, ones[0:1, :], b2r, False, True, sig=True)
                    t = 4 * g4 + 2 * q
                    v = add(t, 2, PS[:, bk, :].rearrange("p (a n) -> p a n", a=2), p)
                    free[("ps", bk)] = [v]
                free[("AT_", u)] = [p]

            for i in range(5):
                if i < 4:
                    up(i)
                if i:
                    down(i - 1)

        if True:
            l2x()

        def bitffn():
            phase()
            g = K.group("gbf")
            Wf = [ar.get(2, 1024), ar.get(8, D)]
            Wq = [ar.get(2, 1024, dt=BF16), ar.get(8, D, dt=BF16)]
            b1b = ar.get(1024)
            b2b = ar.get(D)
            idb = ar.get(128, dt=BF16)
            g.load(Wf[0], d["L2f_W1T"].rearrange("(c p) n -> p c n", p=128))
            g.load(Wf[1], d["L2f_W2T"].rearrange("(c p) n -> p c n", p=128))
            g.load(b1b, d["L2f_b1"].partition_broadcast(128).rearrange("p a n -> p (a n)"))
            g.load(b2b, d["L2f_b2"].partition_broadcast(128).rearrange("p a n -> p (a n)"))
            w = g.tok()
            V(lambda e: e.tensor_copy(idb, ident))
            red = ar.get(2)
            ws = ar.get(2)
            wi = ar.get(2)
            for i in range(2):
                a = V(lambda e, i=i: e.tensor_reduce(red[:, i:i + 1], Wf[i].rearrange("p a b -> p (a b)"), AX.X, ALU.add,
                                                     apply_absolute_value=True), w)
            onesq = ones
            p = mm(PS[:, 0, 0:2], onesq, red, True, True, a, sig=True)
            V(lambda e: e.tensor_scalar(ws, PS[:, 0, 0:2], 1.0 / (D * 1024), 1e-5, ALU.mult, ALU.max), p)
            V(lambda e: e.reciprocal(wi, ws))
            V(lambda e: e.tensor_scalar(ws, ws, 1.0 / 127.0, None, ALU.mult))
            for i in range(2):
                fl = Wf[i].rearrange("p a b -> p (a b)")
                V(lambda e, i=i, fl=fl: e.tensor_scalar(fl, fl, wi[:, i:i + 1], MAGIC, ALU.mult, ALU.add))
                V(lambda e, fl=fl: e.tensor_scalar(fl, fl, -MAGIC, 1.0, ALU.add, ALU.min))
                wq = V(lambda e, i=i, fl=fl: e.tensor_scalar(Wq[i].rearrange("p a b -> p (a b)"), fl, -1.0, None, ALU.max))
            ln_stats(X)
            Hb = ar.get(2, D)
            am = ar.get(2, 4)
            Qb = ar.get(2, D, dt=BF16)
            QT = ar.get(2, 2, 128, dt=BF16)
            G1 = ar.get(2, 1024)
            am2 = ar.get(2, 4)
            Q2 = ar.get(2, 1024, dt=BF16)
            QT2 = ar.get(2, 8, 128, dt=BF16)
            tq = {}

            def quant(dst, src, m, n):
                V(lambda e: e.tensor_reduce(m[:, 0:1], src, AX.X, ALU.max, apply_absolute_value=True))
                V(lambda e: e.tensor_scalar(m[:, 2:3], m[:, 0:1], 1e-5, None, ALU.max))
                V(lambda e: e.reciprocal(m[:, 3:4], m[:, 2:3]))
                V(lambda e: e.tensor_scalar(m[:, 3:4], m[:, 3:4], 127.0, None, ALU.mult))
                V(lambda e: e.tensor_scalar(src, src, m[:, 3:4], MAGIC, ALU.mult, ALU.add))
                return V(lambda e: e.tensor_scalar(dst, src, -MAGIC, None, ALU.add))

            def first(t):
                u = t % 2
                ln_tile(Hb[:, u, :], X, t, *fr(("hb", u)))
                a = quant(Qb[:, u, :], Hb[:, u, :], am[:, u, :], D)
                k = ("ps", 4 + u)
                pb_ = PS[:, 4 + u, 0:128].bitcast(BF16)
                for c in range(2):
                    p = tr(pb_[:, c * 128:(c + 1) * 128], Qb[:, u, c * 128:(c + 1) * 128], idb, a, *fr(k), sig=(c == 1))
                e = A(lambda e, u=u, pb_=pb_: e.activation(QT[:, u, :, :].rearrange("p c n -> p (c n)"), pb_, ACT.Copy), p,
                      *fr(("QT", u)))
                free[k] = [e]
                a = V(lambda e, u=u: e.tensor_tensor(am[:, u, 1:2], am[:, u, 2:3], ws[:, 0:1], ALU.mult))
                for q in range(2):
                    k = ("ps", 2 * u + q)
                    for c in range(2):
                        p = mm(PS[:, 2 * u + q, :], QT[:, u, c, :], Wq[0][:, c, q * 512:(q + 1) * 512], c == 0, c == 1,
                               e, wq, *fr(k), sig=(c == 1))
                    v = V(lambda e, u=u, q=q: e.scalar_tensor_tensor(
                        G1[:, u, q * 512:(q + 1) * 512], PS[:, 2 * u + q, :], am[:, u, 1:2],
                        b1b[:, q * 512:(q + 1) * 512], ALU.mult, ALU.add), p, w)
                    free[k] = [v]
                free[("QT", u)] = [p]
                tq[t] = A(lambda e, u=u: e.activation(G1[:, u, :], G1[:, u, :], ACT.Gelu), v)

            def second(t):
                u = t % 2
                V(lambda e: e.tensor_copy(am2[:, u, 0:1], am[:, u, 0:1]), tq[t])
                a = quant(Q2[:, u, :], G1[:, u, :], am2[:, u, :], 1024)
                V(lambda e: e.tensor_tensor(am2[:, u, 1:2], am2[:, u, 2:3], ws[:, 1:2], ALU.mult))
                k = ("ps", 6)
                pb_ = PS[:, 6, :].bitcast(BF16)
                for f in range(8):
                    p = tr(pb_[:, f * 128:(f + 1) * 128], Q2[:, u, f * 128:(f + 1) * 128], idb, a, *fr(k), sig=(f == 7))
                e = A(lambda e, u=u, pb_=pb_: e.activation(QT2[:, u, :, :].rearrange("p c n -> p (c n)"), pb_, ACT.Copy), p,
                      *fr(("QT2", u)))
                free[k] = [e]
                k = ("ps", 7)
                for f in range(8):
                    p = mm(PS[:, 7, 0:256], QT2[:, u, f, :], Wq[1][:, f, :], f == 0, f == 7, e, *fr(k), sig=(f == 7))
                free[("QT2", u)] = [p]
                v = V(lambda e, u=u: e.scalar_tensor_tensor(Hb[:, u, :], PS[:, 7, 0:256], am2[:, u, 1:2], b2b,
                                                            ALU.mult, ALU.add), p)
                free[k] = [v]
                free[("hb", u)] = [V(lambda e, t=t, u=u: e.tensor_tensor(X[:, t, :], X[:, t, :], Hb[:, u, :], ALU.add))]

            for i in range(NT + 1):
                if i < NT:
                    first(i)
                if i:
                    second(i - 1)

        if True:
            bitffn()

        def l3x():
            phase()
            g = K.group("gl3")
            WK = ar.get(2, D, parts=96)
            WV = ar.get(2, D, parts=96)
            WQ = ar.get(2, D)
            bkc = ar.get(2)
            bqc = ar.get(2)
            bvr = ar.get(D, parts=1)
            g.load(WK, d["L3_Wk"].rearrange("(c p) n -> p c n", p=96))
            g.load(WV, d["L3_Wv"].rearrange("(c p) n -> p c n", p=96))
            g.load(WQ, d["L3_WqT"].rearrange("(h p) n -> p h n", p=128))
            g.load(bkc, d["L3_bk"])
            g.load(bqc, d["L3_bq"])
            g.load(bvr, d["L3_bv"])
            w = g.tok()
            KT = ar.get(2, 2 * S2)
            M = ar.get(2, 2, S2)
            Z = ar.get(1, 2, D)
            rb = ar.get(2, S2, parts=1)
            ht = layernorm_T(X)
            V(lambda e: e.memset(rb, 0.0), w)
            kt = small_proj(KT, WK, 128, 2, w, bias=bkc)
            mt = build_M(M, WQ, KT, 128, 1, 2, kt, w)
            for c in range(2):
                p = mm(PS[0:1, 2, 0:2 * S2], bqc[:, c:c + 1], KT[:, c, :], c == 0, c == 1, *kt, *fr(("ps", 2)), sig=(c == 1))
            rt = V(lambda e: e.tensor_copy(rb.rearrange("p b n -> p (b n)"), PS[0:1, 2, 0:2 * S2]), p)
            free[("ps", 2)] = [rt]
            for b in range(2):
                o = PS[0:S2, 3, b * 256:(b + 1) * 256]
                for c in range(2):
                    mm(o, ctxT[:, c, b * S2:(b + 1) * S2], WV[:, c, :], c == 0, False, w, *fr(("ps", 3)))
                p = mm(o, ones[0:1, 0:S2], bvr, False, True, sig=True)
            zt = V(lambda e: e.tensor_copy(Z[0:S2, 0, :, :], PS[0:S2, 3, :].rearrange("p (b n) -> p b n", b=2)), p)
            free[("ps", 3)] = [zt]
            attention(1, M, mt, rb, rt, 1.0, Z, [zt], None, None, ht)

        if True:
            l3x()

        def l3f():
            phase()
            g = K.group("gl3f")
            q1 = ar.get(2, 1024, dt=I32)
            q2 = ar.get(8, D, dt=I32)
            sc1 = ar.get(2, 1024)
            sc2 = ar.get(8, D)
            W1 = ar.get(2, 1024)
            W2 = ar.get(8, D)
            b1c = ar.get(8)
            b2r = ar.get(D, parts=1)
            vec = ar.get(2, D)
            R = ar.get(NT, D)
            g.load(q1, d["fc1_q"].rearrange("(c p) n -> p c n", p=128))
            g.load(q2, d["fc2_q"].rearrange("(c p) n -> p c n", p=128))
            for c in range(2):
                g.load(sc1[:, c, :], d["fc1_scales"][c:c + 1, :].partition_broadcast(128).rearrange("p a n -> p (a n)"))
            for c in range(8):
                g.load(sc2[:, c, :], d["fc2_scales"][c:c + 1, :].partition_broadcast(128).rearrange("p a n -> p (a n)"))
            g.load(b1c, d["fc1_bias"])
            g.load(b2r, d["fc2_bias"])
            g.load(vec[:, 0, :], d["ln_gamma"].partition_broadcast(128).rearrange("p a n -> p (a n)"))
            g.load(vec[:, 1, :], d["ln_beta"].partition_broadcast(128).rearrange("p a n -> p (a n)"))
            w = g.tok()
            f2 = lambda a_: a_.rearrange("p a b -> p (a b)")
            V(lambda e: e.scalar_tensor_tensor(f2(W1), f2(q1), -128.0, f2(sc1), ALU.add, ALU.mult), w)
            V(lambda e: e.scalar_tensor_tensor(f2(W2), f2(q2), -128.0, f2(sc2), ALU.add, ALU.mult))
            wt = (K.sem["dve"], K.n["dve"])
            ln_stats(X)
            for t in range(NT):
                ln_tile(R[:, t, :], X, t)
            ln_stats(R)
            Hb = ar.get(4, D)
            ht = []
            for t in range(NT):
                u = t % 4
                ln_tile(Hb[:, u, :], R, t, *fr(("hb", u)))
                V(lambda e, u=u: e.tensor_tensor(Hb[:, u, :], Hb[:, u, :], vec[:, 0, :], ALU.mult))
                a = V(lambda e, u=u: e.tensor_tensor(Hb[:, u, :], Hb[:, u, :], vec[:, 1, :], ALU.add))
                p, e = transpose_tile(Hb[:, u, :], t, a, 4 + t % 4)
                free[("hb", u)] = [p]
                ht.append(e)
            gb_out = K.group("gout")

            def add(t, n, ps, p):
                v0 = V(lambda e: e.scalar_tensor_tensor(R[:, t:t + n, :], ps, 0.5, R[:, t:t + n, :], ALU.mult, ALU.add), p)
                v = V(lambda e: e.tensor_tensor(X[:, t:t + n, :], X[:, t:t + n, :], R[:, t:t + n, :], ALU.add))
                gb_out.load(out.rearrange("b (t p) c -> p (b t) c", p=128)[:, t:t + n, :], X[:, t:t + n, :], v)
                return v0

            ffn(W1, b1c, W2, b2r, wt, ht, ACT.Silu, add)

        if True:
            l3f()
        else:
            phase()
            go = K.group("gout")
            go.load(out.rearrange("b (t p) c -> p (b t) c", p=128), X)
        K.emit()


def constants():
    f = np.arange(1024)
    l = np.arange(1024)
    th = 2 * np.pi * ((2 * f[None, :] + 1) * l[:, None] % 4096) / 4096.0
    co, si = np.cos(th), np.sin(th)
    fw = np.stack([co, -si], 0).reshape(2, 8, 128, 8, 128)
    iv = np.stack([co, -si], 0).transpose(0, 2, 1).reshape(2, 8, 128, 8, 128) * (2.0 / 2048)
    c = {}
    c["c_fwd"] = fw.transpose(3, 2, 1, 0, 4).reshape(8, 128, 2048).astype(np.float32)
    c["c_inv"] = iv.transpose(3, 2, 1, 0, 4).reshape(8, 128, 2048).astype(np.float32)
    c["c_iota"] = np.arange(128, dtype=np.float32)[None, :]
    c["c_ident"] = np.eye(128, dtype=np.float32)
    o = np.where(np.arange(128) < 64, 0.0, np.pi / 2)
    c["c_col"] = np.stack([o, np.pi - o, o + np.pi / 2, np.pi / 2 - o, np.pi / 2 - o, np.pi / 2 + o], 1).astype(np.float32)
    c["c_l32"] = np.concatenate([32.0 * np.arange(32), np.arange(32)])[None, :].astype(np.float32)
    return c


def layout(i):
    a = {}
    row = lambda v: v.reshape(1, -1)
    col = lambda v: np.ascontiguousarray(v.reshape(-1, 128).T)
    a["x"] = i["x"]
    a["ctxT"] = i["ctx_768"].transpose(2, 0, 1).reshape(192, 154)
    a["mask2"] = i["mask_BxS2_bf1"].view(np.uint8)
    a["mask1T"] = i["mask_BxS_bf1"].view(np.uint8).reshape(16, 128).T
    for L in ("L0_xattn_", "L1_xattn_"):
        a[L + "Wk"] = i[L + "Wk"]
        a[L + "Wv"] = i[L + "Wv"]
        a[L + "WqT"] = i[L + "Wq"].T
        a[L + "Wo"] = i[L + "Wo"]
    a["L0_xattn_bo"] = row(i["L0_xattn_bo"])
    a["gwT"] = i["L0_ffn_gate_weight"].T
    a["gate_bias"] = row(i["L0_ffn_gate_bias"])

    def up(w, s, n):
        w = w.transpose(1, 0, 2).reshape(256, 32, 128)
        n = n.transpose(1, 0, 2).reshape(256, 8, 128)
        w = np.concatenate([w, n, s.reshape(256, 1, 128)], 1)
        return w.reshape(2, 128, 41 * 128).transpose(1, 0, 2).reshape(128, -1)

    a["moe_g"] = up(i["L0_ffn_w_gate"], i["L0_ffn_shared_w_gate"], i["L0_ffn_anchor_w_gate"])
    a["moe_u"] = up(i["L0_ffn_w_up"], i["L0_ffn_shared_w_up"], i["L0_ffn_anchor_w_up"])
    dn = np.concatenate([i["L0_ffn_w_down"], i["L0_ffn_anchor_w_down"].reshape(8, 128, 256),
                         i["L0_ffn_shared_w_down"][None]], 0)
    a["moe_d"] = dn.transpose(1, 0, 2).reshape(128, -1)
    a["peer_wq"] = i["L1_ffn_w_q"]
    a["peer_wqT"] = i["L1_ffn_w_q"].T
    k = i["L1_ffn_keys"]
    a["peer_keysT"] = k.transpose(3, 2, 0, 1).reshape(128, 16, 64)
    a["bn_gamma"] = col(i["L1_ffn_bn_gamma"])
    a["bn_beta"] = col(i["L1_ffn_bn_beta"])
    a["downT"] = i["L1_ffn_down_embed"].T
    a["up_embed"] = i["L1_ffn_up_embed"]
    X = "L2_xattn_"
    for n in ("Wk", "Wv", "W_film_in", "W_film_out", "W1", "W2"):
        a["L2_" + n] = i[X + n]
    a["L2_WqT"] = i[X + "Wq"].T
    for n in ("g_norm_in", "b_norm_in", "D_skip", "mod_gate", "b_film_in", "b_film_out", "g_norm_out", "b_norm_out",
              "g_ffn", "b_ffn", "log_dt", "b2"):
        a["L2_" + n] = row(i[X + n])
    a["L2_b1"] = col(i[X + "b1"])
    for n in ("A_re", "A_im", "C_re", "C_im"):
        a["L2_" + n + "T"] = i[X + n].T
    a["L2f_W1T"] = i["L2_ffn_W1"].T
    a["L2f_W2T"] = i["L2_ffn_W2"].T
    a["L2f_b1"] = row(i["L2_ffn_b1"])
    a["L2f_b2"] = row(i["L2_ffn_b2"])
    X = "L3_xattn_"
    a["L3_Wk"] = i[X + "Wk"]
    a["L3_Wv"] = i[X + "Wv"]
    a["L3_WqT"] = i[X + "Wq"].T
    a["L3_bk"] = col(i[X + "bk"])
    a["L3_bq"] = col(i[X + "bq"])
    a["L3_bv"] = row(i[X + "bv"])
    X = "L3_ffn_"
    for n in ("fc1_q", "fc2_q", "fc1_scales", "fc2_scales"):
        a[n] = i[X + n]
    a["fc1_bias"] = col(i[X + "fc1_bias"])
    a["fc2_bias"] = row(i[X + "fc2_bias"])
    a["ln_gamma"] = row(i[X + "ln_gamma"])
    a["ln_beta"] = row(i[X + "ln_beta"])
    return a


def kernel(**inputs):
    import concourse.bacc as _bacc
    from concourse import mybir as _mybir
    from concourse.bass_utils import run_bass_kernel_spmd as _run

    nc = _bacc.Bacc("TRN2", target_bir_lowering=False, num_devices=1)
    arrays, aps = {}, {}
    data = layout({k: np.asarray(v) for k, v in inputs.items()})
    data.update(constants())
    for name, a in data.items():
        a = np.ascontiguousarray(a)
        arrays["in_" + name] = a
        aps[name] = nc.dram_tensor("in_" + name, a.shape, _mybir.dt.from_np(a.dtype), kind="ExternalInput").ap()
    o = nc.dram_tensor("out_0_dram", (2, 1024, 256), _mybir.dt.float32, kind="ExternalOutput").ap()
    program(nc, aps, o)
    r = _run(nc, [arrays], core_ids=[0])
    return r.results[0]["out_0_dram"]
```

```python
import numpy as np
import math
from contextlib import ExitStack

import concourse.bass as bass
from concourse import mybir

ALU = mybir.AluOpType
ACT = mybir.ActivationFunctionType
AX = mybir.AxisListType
F32 = mybir.dt.float32
BF16 = mybir.dt.bfloat16
I32 = mybir.dt.int32
U8 = mybir.dt.uint8
F16 = mybir.dt.float16

T = 2048
NT = 16
B = 2
D = 256
S2 = 77
MAGIC = 12582912.0
NEG = -1.0e30
WS = 4096.0


class Queues:

    def __init__(self, nc, ctx):
        self.nc, self.ctx = nc, ctx
        self.q = {k: [] for k in ("pe", "act", "dve", "pool", "sp")}
        self.sem = {k: ctx.enter_context(nc.semaphore("s_" + k)) for k in ("pe", "act", "dve", "pool")}
        self.n = {k: 0 for k in self.sem}
        self.groups = []

    def op(self, eng, fn, after, sig=True, chain=False):
        waits = [t for t in after if t is not None]
        if chain and self.n[eng]:
            waits.append((self.sem[eng], self.n[eng]))
        if sig:
            self.n[eng] += 1
        self.q[eng].append((waits, fn, (self.sem[eng], 1) if sig else None))
        return (self.sem[eng], self.n[eng]) if sig else None

    def V(self, fn, *after):
        return self.op("dve", fn, after, chain=True)

    def Vn(self, fn, *after):
        return self.op("dve", fn, after)

    def A(self, fn, *after):
        return self.op("act", fn, after)

    def G(self, fn, *after):
        return self.op("pool", fn, after)

    def mm(self, out, lhsT, rhs, start, stop, *after, sig=False):
        return self.op("pe", lambda e: e.matmul(out, lhsT, rhs, start=start, stop=stop,
                                                skip_group_check=True), after, sig)

    def tr(self, out, in_, ident, *after, sig=False):
        return self.op("pe", lambda e: e.transpose(out, in_, ident), after, sig)

    def group(self, name):
        g = Group(self, self.ctx.enter_context(self.nc.semaphore(name)))
        self.groups.append(g)
        return g

    def emit(self):
        done = {}

        def run(key, eng):
            seen = {}
            for waits, fn, inc in self.q[key]:
                for s, v in waits:
                    if seen.get(s.name, 0) < v:
                        eng.wait_ge(s, v)
                        seen[s.name] = v
                ins = fn(eng)
                if inc is not None:
                    ins.then_inc(*inc)
            done[key] = True

        block = self.ctx.enter_context(self.nc.Block())

        @block.sync
        def _(eng):
            run("sp", eng)
            for g in self.groups:
                if g.n:
                    eng.wait_ge(g.sem, 16 * g.n)

        @block.gpsimd
        def _(eng):
            run("pool", eng)

        @block.scalar
        def _(eng):
            run("act", eng)

        @block.tensor
        def _(eng):
            run("pe", eng)

        @block.vector
        def _(eng):
            run("dve", eng)


class Group:

    def __init__(self, K, sem):
        self.K, self.sem, self.n = K, sem, 0

    def load(self, out, in_, *after, eng="sp"):
        self.n += 1
        self.K.q[eng].append(([t for t in after if t is not None], lambda e: e.dma_start(out, in_), (self.sem, 16)))
        return (self.sem, 16 * self.n)

    def tok(self):
        return (self.sem, 16 * self.n)


class Arena:

    def __init__(self, mem, size):
        self.mem, self.size, self.at, self.peak = mem, size, 0, 0

    def get(self, *shape, dt=F32, parts=128):
        n = 1
        for s in shape:
            n *= s
        w = n if dt in (F32, I32) else (n + 1) // 2 if dt in (BF16, F16) else (n + 3) // 4
        w = (w + 7) // 8 * 8
        a = self.mem[0:parts, self.at:self.at + w]
        self.at += w
        self.peak = max(self.peak, self.at)
        assert self.at <= self.size, (self.at, self.size)
        if dt != F32:
            a = a.bitcast(dt)
        a = a[:, 0:n]
        if len(shape) > 1:
            names = "abcdef"[:len(shape)]
            a = a.rearrange(f"p ({' '.join(names)}) -> p {' '.join(names)}",
                            **{c: s for c, s in zip(names, shape)})
        return a


def bc(ap, axis, shape):
    return ap.unsqueeze(axis).to_broadcast(list(shape))


def program(nc, d, out):
    ctx = ExitStack()
    with ctx:
        K = Queues(nc, ctx)
        V, Vn, A, G, mm, tr = K.V, K.Vn, K.A, K.G, K.mm, K.tr
        SIZE = 53208
        mem = ctx.enter_context(nc.sbuf_tensor("mem", [128, SIZE], F32))
        PS = ctx.enter_context(nc.psum_tensor("PS", [128, 8, 512], F32))
        ar = Arena(mem, SIZE)
        free = {}
        scr = {n: nc.dram_tensor("scr_" + n, s, F32, kind="Internal").ap() for n, s in {"cw": (48, T), "K": (1024, D)}.items()}

        def fr(*keys):
            return [t for k in keys for t in free.get(k, ())]

        X = ar.get(NT, D)
        HT = ar.get(2, T)
        ident = ar.get(128)
        ones = ar.get(128)
        ctxT = ar.get(2, 2 * S2, parts=96)
        st6 = ar.get(NT, 6)
        mv = ar.get(NT, 2)
        rstd = ar.get(NT)
        colc = ar.get(6)
        m8 = ar.get(B * S2, dt=U8, parts=1)
        g0 = K.group("g0")
        tok4 = lambda a_: a_.rearrange("(h p s) c -> h p s c", p=128, s=4)
        tile4 = lambda a_, h: a_.rearrange("p (s h) c -> p s h c", h=2)[:, :, h, :]
        for b in range(B):
            for h in range(2):
                g0.load(tile4(X[:, b * 8:b * 8 + 8, :], h), tok4(d["x"][b])[h])
        g0.load(ident, d["c_ident"])
        g0.load(ctxT, d["ctxT"].rearrange("(c p) n -> p c n", p=96))
        g0.load(colc, d["c_col"])
        g0.load(m8, d["mask2"].rearrange("(a b) k -> a (b k)", a=1))
        L0 = g0.tok()
        t_ones = V(lambda e: e.memset(ones, 1.0))

        def mask_row():
            mrow = ar.get(B, 4 * S2, parts=1)
            V(lambda e: e.tensor_copy(mrow[:, :, 0:S2], m8.rearrange("p (b k) -> p b k", b=B)), L0)
            V(lambda e: e.tensor_scalar(mrow[:, :, 0:S2], mrow[:, :, 0:S2], -1.0, -NEG, ALU.add, ALU.mult))
            for h in range(1, 4):
                t = V(lambda e, h=h: e.tensor_copy(mrow[:, :, h * S2:(h + 1) * S2], mrow[:, :, 0:S2]))
            return mrow, t

        BASE = ar.at
        barrier_tokens = []

        def phase():
            toks = [(K.sem[k], K.n[k]) for k in K.sem if K.n[k]]
            for key in K.q:
                K.q[key].append((list(toks), lambda e: None, None))
            free.clear()
            ar.at = BASE

        def ln_stats(src, after=(), tiles=range(16)):
            for i, t in enumerate(tiles):
                (Vn if i else V)(lambda e, t=t: e.bn_stats(st6[:, t, :], src[:, t, :]), *after)
            for i, t in enumerate(tiles):
                (Vn if i else V)(lambda e, t=t: e.bn_aggr(mv[:, t, :], st6[:, t, :]))
            rs, var = rstd[:, tiles[0]:tiles[-1] + 1], mv[:, tiles[0]:tiles[-1] + 1, 1]
            a = V(lambda e: e.tensor_scalar(rs, var, 1e-5, None, ALU.add))
            a = A(lambda e: e.activation(rs, rs, ACT.Sqrt), a)
            r = V(lambda e: e.reciprocal(rs, rs), a)
            free["rstd"] = [r]
            return r

        QT4 = [range(4 * q, 4 * q + 4) for q in range(4)]

        def ln_tile(dst, src, t, *after):
            return Vn(lambda e: e.tensor_scalar(dst, src[:, t, :], mv[:, t, 0:1], rstd[:, t:t + 1],
                                               ALU.subtract, ALU.mult), *after, *fr("rstd"))

        evn = [0]

        def evac(out_ap, in_ap, *after):
            evn[0] += 1
            if evn[0] % 2:
                return A(lambda e: e.activation(out_ap, in_ap, ACT.Copy), *after)
            return Vn(lambda e: e.tensor_copy(out_ap, in_ap), *after)

        def transpose_tile(Hs, t, ready, bank, dst=None):
            dst = HT if dst is None else dst
            k = ("ps", bank)
            tr(PS[:, bank, 0:128], Hs[:, 0:128], ident, ready, *fr(k))
            p = tr(PS[:, bank, 128:256], Hs[:, 128:256], ident, sig=True)
            e = evac(dst[:, :, t * 128:(t + 1) * 128],
                     PS[:, bank, 0:256].rearrange("p (c n) -> p c n", c=2), p)
            free[k] = [e]
            return p, e

        def layernorm_T(src, after=(), known=False):
            if not known:
                ln_stats(src, after, QT4[0])
            Hb = ar.get(4, D)
            done = []
            for t in range(NT):
                if not known and t % 4 == 2 and t < 12:
                    ln_stats(src, after, QT4[t // 4 + 1])
                a = ln_tile(Hb[:, t % 4, :], src, t, *fr(("hb", t % 4)))
                p, e = transpose_tile(Hb[:, t % 4, :], t, a, 4 + t % 4)
                free[("hb", t % 4)] = [p]
                done.append(e)
            return done

        def affine_T(Hb, src, vec, ready, pre):
            ht = []
            pre(0)
            for q in range(4):
                u = q % 2
                if q < 3:
                    pre(q + 1)
                hb = Hb[:, u, :, :]
                for t in range(4 * q, 4 * q + 4):
                    ln_tile(Hb[:, u, t % 4, :], src, t, *fr(("hb", u)))
                V(lambda e, hb=hb: e.tensor_tensor(hb, hb, bc(vec[:, 0, :], 1, (128, 4, D)), ALU.mult), ready)
                a = V(lambda e, hb=hb: e.tensor_tensor(hb, hb, bc(vec[:, 1, :], 1, (128, 4, D)), ALU.add))
                for t in range(4 * q, 4 * q + 4):
                    p, e = transpose_tile(Hb[:, u, t % 4, :], t, a, 4 + t % 4)
                    ht.append(e)
                free[("hb", u)] = [p]
            return ht

        def small_proj(dst, W, hd, ns, ready, bias=None):
            toks = []
            for s in range(ns):
                k = ("ps", s % 4)
                o = PS[0:hd, s % 4, 0:2 * S2]
                mm(o, W[:, 0, s * hd:(s + 1) * hd], ctxT[:, 0, :], True, False, ready, L0, *fr(k))
                p = mm(o, W[:, 1, s * hd:(s + 1) * hd], ctxT[:, 1, :], False, True, sig=True)
                if bias is None:
                    e = evac(dst[:, s, :], o, p)
                else:
                    e = V(lambda e, s=s, o=o: e.tensor_scalar(dst[:, s, :], o, bias[:, s:s + 1], None, ALU.add), p)
                free[k] = [e]
                toks.append(e)
            return toks

        def build_M(M, WqT, KT, hd, H, nch, kt, ready):
            toks = []
            i = 0
            for h in range(H):
                for kc in range(2):
                    bk = i % 4
                    i += 1
                    k = ("ps", bk)
                    o = PS[:, bk, 0:2 * S2]
                    for c in range(nch):
                        s = h * nch + c
                        p = mm(o, WqT[:, s, kc * 128:(kc + 1) * 128], KT[:, s, :], c == 0, c == nch - 1,
                               ready, kt[s], *fr(k), sig=(c == nch - 1))
                    e = evac(M[:, kc, :, h * S2:(h + 1) * S2], o.rearrange("p (b j) -> p b j", b=2), p)
                    free[k] = [e]
                    toks.append(e)
            return toks

        def chunks(H):
            W = H * S2
            return [(c, min(128, W - 128 * c)) for c in range((W + 127) // 128)]

        def pack_rows(g, Zp, Zs, H, ready):
            for h in range(H):
                a = 0
                while a < S2:
                    r = h * S2 + a
                    n = min(S2 - a, 128 - r % 128)
                    g.load(Zp[r % 128:r % 128 + n, r // 128, :, :], Zs[a:a + n, h, :, :], ready[h])
                    a += n
            return g.tok()

        def attention(H, M, mtoks, rowb, rowt, scale, Z, ztoks, borow, bot, htoks, early=(), bg=None):
            W = H * S2
            NG = (H + 3) // 4
            CH = chunks(H)
            E = ar.get(2, W)
            ET = ar.get(2, len(CH), 128)
            mx = ar.get(2, H)
            sm = ar.get(2, H)
            free[("E", 0)] = free[("E", 1)] = free[("ET", 0)] = free[("ET", 1)] = list(early)
            tokE, tokT, tokN = {}, {}, {}
            bg = bg or (lambda n: None)

            def sa(t):
                b, u = t // 8, t % 2
                ps_ = []
                for g in range(NG):
                    n = min(4, H - 4 * g)
                    k = ("ps", g)
                    o = PS[:, g, 0:n * S2]
                    for c in range(2):
                        p = mm(o, HT[:, c, t * 128:(t + 1) * 128], M[:, c, b, g * 4 * S2:g * 4 * S2 + n * S2],
                               c == 0, c == 1 and rowb is None, htoks[t], *mtoks, *fr(k),
                               sig=(c == 1 and rowb is None))
                    if rowb is not None:
                        p = mm(o, ones[0:1, :], rowb[:, b, 0:n * S2], False, True,
                               rowt, t_ones, sig=True)
                    ps_.append((g, n, o.rearrange("p (h j) -> p h j", h=n), p))
                for g, n, o3, p in ps_:
                    (Vn if g else V)(lambda e, g=g, n=n, o3=o3: e.tensor_reduce(
                        mx[:, u, 4 * g:4 * g + n], o3, AX.X, ALU.max), p, *(early if t < 2 else ()))
                for g, n, o3, p in ps_:
                    v = (Vn if g else V)(lambda e, g=g, n=n, o3=o3: e.tensor_tensor(
                        E[:, u, g * 4 * S2:g * 4 * S2 + n * S2].rearrange("p (h j) -> p h j", h=n), o3,
                        bc(mx[:, u, 4 * g:4 * g + n], 2, (128, n, S2)), ALU.subtract), *fr(("E", u)))
                    free[("ps", g)] = [v]
                tokE[t] = A(lambda e: e.activation(E[:, u, :], E[:, u, :], ACT.Exp, scale=scale), v)

            def sb(t):
                u = t % 2
                E3 = E[:, u, :].rearrange("p (h j) -> p h j", h=H)
                V(lambda e: e.tensor_reduce(sm[:, u, :], E3, AX.X, ALU.add), tokE[t])
                V(lambda e: e.reciprocal(sm[:, u, :], sm[:, u, :]))
                tokN[t] = V(lambda e: e.tensor_tensor(E3, E3, bc(sm[:, u, :], 2, (128, H, S2)), ALU.mult))

            def sc(t):
                u = t % 2
                tt = []
                for q in range(0, len(CH), 4):
                    part = CH[q:q + 4]
                    bk = 4 + (q // 4) % 2
                    k = ("ps", bk)
                    for c, n in part:
                        p = tr(PS[0:n, bk, (c - q) * 128:(c - q + 1) * 128], E[:, u, c * 128:c * 128 + n], ident,
                               tokN[t], *fr(k), sig=(c == part[-1][0]))
                    free[k] = []
                    for n in sorted({n for _, n in part}, reverse=True):
                        cs = [c for c, m in part if m == n]
                        e = A(lambda e, cs=cs, n=n, q=q, bk=bk: e.activation(
                            ET[0:n, u, cs[0]:cs[-1] + 1, :],
                            PS[0:n, bk, (cs[0] - q) * 128:(cs[-1] - q + 1) * 128].rearrange("p (h j) -> p h j", h=len(cs)),
                            ACT.Copy), p, *fr(("ET", u)))
                        free[k] = [e]
                    tt.append(e)
                free[("E", u)] = [p]
                tokT[t] = tt

            def sd(t):
                b, u = t // 8, t % 2
                k = ("ps", 7)
                o = PS[:, 7, 0:256]
                for c, n in CH:
                    last = c == CH[-1][0] and borow is None
                    p = mm(o, ET[0:n, u, c, :], Z[0:n, c, b, :], c == 0, last, *tokT[t], *ztoks, *fr(k), sig=last)
                if borow is not None:
                    p = mm(o, ones[0:1, :], borow, False, True, bot, t_ones, sig=True)
                free[("ET", u)] = [p]
                return p

            def se(t, p):
                free[("ps", 7)] = [Vn(lambda e: e.tensor_tensor(X[:, t, :], X[:, t, :], PS[:, 7, 0:256], ALU.add), p)]

            for i in range(NT + 2):
                if i < NT:
                    sa(i)
                    bg(7)
                if 1 <= i <= NT:
                    sb(i - 1)
                    bg(7)
                if i >= 2:
                    p = sd(i - 2)
                if 1 <= i <= NT:
                    sc(i - 1)
                    bg(7)
                if i >= 2:
                    se(i - 2, p)
                    bg(7)

        def xattn_heads(L, H, hd, scale, masked, bo, bg=None):
            phase()
            g = K.group("gx" + L)
            WK = ar.get(2, H * hd, parts=96)
            WV = ar.get(2, H * hd, parts=96)
            WQ = ar.get(H, D, parts=hd)
            WO = ar.get(H, D, parts=hd)
            g.load(WK, d[L + "Wk"].rearrange("(c p) n -> p c n", p=96))
            g.load(WV, d[L + "Wv"].rearrange("(c p) n -> p c n", p=96))
            g.load(WQ, d[L + "WqT"].rearrange("(h p) n -> p h n", p=hd))
            g.load(WO, d[L + "Wo"].rearrange("(h p) n -> p h n", p=hd))
            bor = None
            if bo:
                bor = ar.get(D, parts=1)
                g.load(bor, d[L + "bo"])
            w = g.tok()
            KT = ar.get(H, 2 * S2, parts=hd)
            VT = ar.get(H, 2 * S2, parts=hd)
            M = ar.get(2, 2, H * S2)
            Zp = ar.get(len(chunks(H)), 2, D)
            mrow, t_mrow = mask_row() if masked else (None, None)
            step = bg(ar) if bg else None
            ln_stats(X, (L0,))
            kt = small_proj(KT, WK, hd, H, w)
            vt = small_proj(VT, WV, hd, H, w)
            at = ar.at
            Zs = ar.get(H, 2, D, parts=S2)
            zt = []
            for h in range(H):
                k = ("ps", h % 4)
                for b in range(2):
                    p = mm(PS[0:S2, h % 4, b * 256:(b + 1) * 256], VT[:, h, b * S2:(b + 1) * S2], WO[:, h, :],
                           True, True, vt[h], w, *fr(k), sig=(b == 1))
                e = evac(Zs[:, h, :, :], PS[0:S2, h % 4, :].rearrange("p (b n) -> p b n", b=2), p)
                free[k] = [e]
                zt.append(e)
            zp = pack_rows(K.group("gz" + L), Zp, Zs, H, zt)
            mt = build_M(M, WQ, KT, hd, H, 1, kt, w)
            Hb = ar.get(4, D)
            ht = []
            for t in range(NT):
                a = ln_tile(Hb[:, t % 4, :], X, t, *fr(("hb", t % 4)))
                p, e = transpose_tile(Hb[:, t % 4, :], t, a, 4 + t % 4)
                free[("hb", t % 4)] = [p]
                ht.append(e)
            ar.at = at
            attention(H, M, mt[-2:], mrow, t_mrow, scale, Zp, [zp], bor, w, ht, early=[zp, ht[-1], ht[-2], p], bg=step)
            if step:
                step(10 ** 6)

        def s4d(ar, bank, early):
            gk = K.group("gk")
            PI2 = 2 * math.pi
            C1 = 6.28125
            C2 = float(np.float32(PI2 - C1))
            C3 = PI2 - C1 - C2
            l32 = ar.get(2, 32)
            KC = [ar.get(D) for _ in range(4)]
            dre, dim, cr, ci = KC
            s2 = ar.at
            dta = ar.get(D)
            Are = ar.get(D)
            Aim = ar.get(D)
            Cre = ar.get(D)
            Cim = ar.get(D)
            for n_, o_ in (("A_re", Are), ("A_im", Aim), ("C_re", Cre), ("C_im", Cim)):
                gk.load(o_[0:64], d["L2_" + n_ + "T"], *early)
                gk.load(o_[64:128], d["L2_" + n_ + "T"])
            gk.load(dta, d["L2_log_dt"].partition_broadcast(128).rearrange("p a n -> p (a n)"))
            gk.load(l32, d["c_l32"].partition_broadcast(128).rearrange("p a (c n) -> p (a c) n", c=2))
            wk = gk.tok()
            dt_ = ar.get(D)
            ei = ar.get(D, dt=I32)
            tmp = [ar.get(D) for _ in range(6)]
            e1 = ar.at
            ar.at = s2
            ND = 8
            R = ar.get(2, ND, 32)
            Q = ar.get(2, ND, 32)
            C_ = ar.get(2, ND, 32)
            EXP = ar.get(2, ND, 32)
            S_ = ar.get(ND, 32)
            UV = ar.get(2, 2, ND, 32)
            Kt = ar.get(32, 4 * ND, parts=32)
            ar.at = max(ar.at, e1)
            SH = 0.9999995
            fk = {}

            def ts(o, i, s0, s1=None, op0=ALU.mult, op1=None, *after):
                if s1 is None:
                    return V(lambda e: e.tensor_scalar(o, i, s0, None, op0), *after)
                return V(lambda e: e.tensor_scalar(o, i, s0, s1, op0, op1), *after)

            def tt(o, a_, b_, op, *after):
                return V(lambda e: e.tensor_tensor(o, a_, b_, op), *after)

            def gg(o, a_, b_, op, *after):
                return G(lambda e: e.tensor_tensor(o, a_, b_, op), *after)

            def stt(o, a_, s_, b_, op0, op1, *after):
                return V(lambda e: e.scalar_tensor_tensor(o, a_, s_, b_, op0, op1), *after)

            def pexp(o, x_, kf, r, *after):
                ts(kf, x_, 1.4426950408889634, MAGIC, ALU.mult, ALU.add, *after)
                ts(kf, kf, -MAGIC, None, ALU.add)
                stt(r, kf, -0.693359375, x_, ALU.mult, ALU.add)
                stt(r, kf, 2.12194440e-4, r, ALU.mult, ALU.add)
                yield
                ts(kf, kf, 127.0, None, ALU.add)
                ts(kf, kf, 0.0, 254.0, ALU.max, ALU.min)
                V(lambda e: e.tensor_copy(ei, kf))
                V(lambda e: e.tensor_scalar(ei, ei, 23, None, ALU.logical_shift_left))
                yield
                ts(o, r, 1.0 / 5040)
                for c in (1 / 720, 1 / 120, 1 / 24, 1 / 6, 0.5, 1.0):
                    stt(o, o, c, r, ALU.add, ALU.mult)
                    yield
                ts(o, o, 1.0, None, ALU.add)
                tt(o, o, ei.bitcast(F32), ALU.mult)
                yield

            def reduce2pi(r, kf, x_, *after):
                ts(kf, x_, 1.0 / PI2, MAGIC, ALU.mult, ALU.add, *after)
                ts(kf, kf, -MAGIC, None, ALU.add)
                yield
                stt(r, kf, -C1, x_, ALU.mult, ALU.add)
                yield
                stt(r, kf, -C2, r, ALU.mult, ALU.add)
                yield
                stt(r, kf, -C3, r, ALU.mult, ALU.add)
                yield

            def wrap(y, m, r, c_, pc, *after):
                ts(m, r, pc, -PI2, ALU.is_gt, ALU.mult, *after)
                return stt(y, r, c_, m, ALU.add, ALU.add)

            def work():
                yield from pexp(dt_, dta, tmp[0], tmp[1], wk, *early)
                tt(dre, dt_, Are, ALU.mult)
                tt(dim, dt_, Aim, ALU.mult)
                er = tmp[4]
                yield from pexp(er, dre, tmp[0], tmp[1])
                yield from reduce2pi(tmp[5], tmp[0], dim)
                v = wrap(tmp[2], tmp[0], tmp[5], math.pi / 2, math.pi / 2)
                A(lambda e: e.activation(tmp[3], tmp[5], ACT.Sin, scale=SH), v)
                a = A(lambda e: e.activation(tmp[2], tmp[2], ACT.Sin, scale=SH), v)
                yield
                ec, es, t4, t5 = tmp[2], tmp[3], tmp[0], tmp[1]
                tt(ec, ec, er, ALU.mult, a)
                ts(ec, ec, -1.0, None, ALU.add)
                tt(es, es, er, ALU.mult)
                yield
                tt(cr, ec, Cre, ALU.mult)
                tt(t4, es, Cim, ALU.mult)
                tt(cr, cr, t4, ALU.subtract)
                yield
                tt(ci, ec, Cim, ALU.mult)
                tt(t4, es, Cre, ALU.mult)
                tt(ci, ci, t4, ALU.add)
                yield
                tt(t4, Are, Are, ALU.mult)
                tt(t5, Aim, Aim, ALU.mult)
                tt(t4, t4, t5, ALU.add)
                V(lambda e: e.reciprocal(t4, t4))
                ts(t4, t4, 2.0)
                yield
                tt(t5, cr, Are, ALU.mult)
                tt(ec, ci, Aim, ALU.mult)
                tt(t5, t5, ec, ALU.add)
                yield
                tt(ci, ci, Are, ALU.mult)
                tt(ec, cr, Aim, ALU.mult)
                tt(ci, ci, ec, ALU.subtract)
                yield
                tt(ci, ci, t4, ALU.mult)
                st = tt(cr, t5, t4, ALU.mult)
                yield
                sh4 = [128, 2, ND, 32]
                lb = l32.unsqueeze(2).to_broadcast(sh4)
                sh3 = (128, ND, 32)
                pend = None

                def products(blk, v):
                    u, q = blk % 2, blk % 4
                    bk = bank()
                    k = ("ps", bk)
                    for j in range(ND):
                        p = mm(PS[0:32, bk, j * 32:(j + 1) * 32], UV[:, u, 1, j, :], UV[:, u, 0, j, :], True, True, v,
                               *fr(k), sig=(j == ND - 1))
                    e_ = A(lambda e: e.activation(Kt[:, :, q * ND:(q + 1) * ND].rearrange("p a d -> p d a"),
                                                  PS[0:32, bk, 0:ND * 32].rearrange("p (d a) -> p d a", d=ND), ACT.Copy),
                           p, *(fk.get("kt", ()) if q == 0 else ()))
                    free[k] = [e_]
                    fk[("uv", u)] = [p]
                    if q == 3:
                        c0 = (blk - 3) * ND
                        fk["kt"] = [gkt.load(scr["K"].rearrange("(a b) n -> b a n", b=32)[:, :, c0:c0 + 4 * ND], Kt, e_)]

                for blk in range(D // ND):
                    u = blk % 2
                    ds = slice(blk * ND, (blk + 1) * ND)
                    dimb = dim[:, ds].unsqueeze(1).unsqueeze(3).to_broadcast(sh4)
                    dreb = dre[:, ds].unsqueeze(1).unsqueeze(3).to_broadcast(sh4)
                    g_ = gg(EXP, dreb, lb, ALU.mult, st, *fk.get("exp", ()))
                    tt(R, dimb, lb, ALU.mult)
                    yield
                    yield from reduce2pi(C_, Q, R, *fk.get("c", ()))
                    v = wrap(S_, Q[:, 0], C_[:, 0], colc[:, 0:1], colc[:, 1:2], *fk.get("s", ()))
                    yield
                    wrap(C_[:, 0], Q[:, 0], C_[:, 0], colc[:, 2:3], colc[:, 3:4])
                    yield
                    v = wrap(C_[:, 1], Q[:, 1], C_[:, 1], colc[:, 4:5], colc[:, 5:6])
                    yield
                    A(lambda e: e.activation(S_, S_, ACT.Sin, scale=SH), v)
                    a1 = A(lambda e: e.activation(C_, C_, ACT.Sin, scale=SH), v)
                    a2 = A(lambda e: e.activation(EXP, EXP, ACT.Exp), g_)
                    if pend:
                        products(*pend)
                    yield
                    q1 = gg(UV[:, u, 1], C_[:, 1], EXP[:, 1], ALU.mult, a2, *fk.get(("uv", u), ()))
                    q2 = gg(C_[:, 0], C_[:, 0], bc(cr[:, ds], 2, sh3), ALU.mult, a1)
                    q3 = gg(S_, S_, bc(ci[:, ds], 2, sh3), ALU.mult, a1)
                    yield
                    q4 = gg(S_, C_[:, 0], S_, ALU.subtract, q3)
                    yield
                    q5 = gg(UV[:, u, 0], S_, EXP[:, 0], ALU.mult, q4)
                    fk["exp"] = fk["s"] = [q5]
                    fk["c"] = [q4]
                    pend = (blk, q5)
                    yield
                yield
                products(*pend)

            gkt = K.group("gkt")
            it = work()

            def step(n):
                for _ in range(n):
                    if next(it, "end") == "end":
                        if not scr_done:
                            scr_done.append(gkt.tok())
                        return
            return step

        scr_done = []

        xattn_heads("L0_xattn_", 8, 64, 0.125, False, True)

        def moe():
            phase()
            NU = 41
            g = K.group("gmw")
            gm = K.group("gmm")
            WGU = ar.get(2, 2, NU, 128)
            WD = ar.get(NU, D)
            GW = ar.get(2, 32)
            gb = ar.get(32)
            gm.load(GW, d["gwT"].rearrange("(c p) n -> p c n", p=128))
            gm.load(gb, d["gate_bias"].partition_broadcast(128).rearrange("p a n -> p (a n)"))
            wl = []

            def load_units(s0, s1):
                gg = K.group(f"gmw{s0}")
                gg.load(WGU[:, 0, :, s0:s1, :], d["moe_g"].rearrange("p (c e n) -> p c e n", c=2, e=NU)[:, :, s0:s1, :])
                gg.load(WGU[:, 1, :, s0:s1, :], d["moe_u"].rearrange("p (c e n) -> p c e n", c=2, e=NU)[:, :, s0:s1, :])
                gg.load(WD[:, s0:s1, :], d["moe_d"].rearrange("p (e n) -> p e n", e=NU)[:, s0:s1, :])
                wl.extend([gg.tok()] * (s1 - s0))

            load_units(0, 4)
            load_units(4, 12)
            ht = layernorm_T(X)
            s0 = ar.at
            sc = ar.get(NT, 32)
            sb_ = ar.get(NT, 32)
            gs = ar.get(NT, 8)
            tops = ar.get(NT, 4, 8)
            t8 = ar.get(NT, 8)
            sel = ar.get(NT, 32)
            cw = ar.get(NT, 48)
            wsum = ar.get(NT)
            for t in range(NT):
                for c in range(2):
                    p = mm(PS[:, 0, t * 32:(t + 1) * 32], HT[:, c, t * 128:(t + 1) * 128], GW[:, c, :],
                           c == 0, c == 1, ht[t], gm.tok(), sig=(c == 1))
            a = A(lambda e: e.activation(sc, PS[:, 0, :].rearrange("p (t n) -> p t n", t=NT), ACT.Sigmoid), p)
            V(lambda e: e.tensor_tensor(sb_, sc, bc(gb, 1, (128, NT, 32)), ALU.add), a)
            for t in range(NT):
                for q in range(4):
                    (Vn if t + q else V)(lambda e, t=t, q=q: e.max(tops[:, t, q, :], sb_[:, t, q * 8:(q + 1) * 8]))
            V(lambda e: e.memset(gs, NEG))
            V(lambda e: e.tensor_tensor(gs[:, :, 0:4], tops[:, :, :, 0], tops[:, :, :, 1], ALU.add))
            for t in range(NT):
                (Vn if t else V)(lambda e, t=t: e.max(t8[:, t, :], gs[:, t, :]))
            V(lambda e: e.tensor_tensor(gs[:, :, 0:4], gs[:, :, 0:4], bc(t8[:, :, 1], 2, (128, NT, 4)), ALU.is_ge))
            V(lambda e: e.tensor_scalar(gs[:, :, 0:4], gs[:, :, 0:4], -1.0, -NEG, ALU.add, ALU.mult))
            for q in range(4):
                V(lambda e, q=q: e.tensor_tensor(sb_[:, :, q * 8:(q + 1) * 8], sb_[:, :, q * 8:(q + 1) * 8],
                                                 bc(gs[:, :, q], 2, (128, NT, 8)), ALU.add))
            for t in range(NT):
                (Vn if t else V)(lambda e, t=t: e.max(t8[:, t, :], sb_[:, t, :]))
            V(lambda e: e.tensor_tensor(sel, sb_, bc(t8[:, :, 5], 2, (128, NT, 32)), ALU.is_ge))
            V(lambda e: e.tensor_tensor(sel, sel, sc, ALU.mult))
            V(lambda e: e.tensor_reduce(wsum, sel, AX.X, ALU.add))
            V(lambda e: e.tensor_scalar(wsum, wsum, 1e-20, None, ALU.add))
            V(lambda e: e.reciprocal(wsum, wsum))
            V(lambda e: e.tensor_scalar(wsum, wsum, 0.2, None, ALU.mult))
            V(lambda e: e.tensor_tensor(cw[:, :, 0:32], sel, bc(wsum, 2, (128, NT, 32)), ALU.mult))
            V(lambda e: e.tensor_tensor(sel, sb_, bc(t8[:, :, 0], 2, (128, NT, 32)), ALU.is_ge))
            s4 = sel.rearrange("p t (l r) -> p t l r", r=2)
            V(lambda e: e.tensor_tensor(cw[:, :, 32:48], s4[:, :, :, 0], s4[:, :, :, 1], ALU.max))
            a = V(lambda e: e.tensor_scalar(cw[:, :, 32:48], cw[:, :, 32:48], 0.1, None, ALU.mult))
            cwT = ar.get(T, parts=48)
            gc = K.group("gcw")
            for i in range(4):
                for j in range(4):
                    t = 4 * i + j
                    p = tr(PS[0:48, 1 + i % 2, j * 128:(j + 1) * 128], cw[:, t, :], ident, a,
                           *fr(("cwt", i % 2)), sig=(j == 3))
                e = A(lambda e, i=i: e.activation(cwT[:, i * 512:(i + 1) * 512], PS[0:48, 1 + i % 2, :], ACT.Copy), p)
                free[("cwt", i % 2)] = [e]
            gc.load(scr["cw"], cwT, e)
            wrote = gc.tok()
            rest = [(u0, min(u0 + 3, NU)) for u0 in range(12, NU, 3)]
            pend = [(K.sem["dve"], K.n["dve"]), (K.sem["pe"], K.n["pe"]), wrote, (K.sem["act"], K.n["act"])]
            ar.at = s0
            NB_ = 4
            CB = ar.get(NB_, 512)
            SG = ar.get(2, 512)
            UU = ar.get(2, 512)
            AC = ar.get(2, 512)
            gcb = [K.group(f"gcb{i}") for i in range(NB_)]
            free_cb = {}
            bgstep = s4d(ar, lambda: 4 + 2 * ((now[0] + 1) % 2), pend)
            now = [0]
            free[("ps", 0)] = pend
            units = [(e, g4) for g4 in range(4) for e in range(NU)]
            actt = {}

            def up(i):
                e_, g4 = units[i]
                tk = slice(g4 * 512, (g4 + 1) * 512)
                u = i % 2
                if e_ < 40:
                    slot = i % NB_
                    G_ = gcb[slot]
                    deps = pend if i < NB_ else [wrote]
                    if e_ < 32:
                        G_.load(CB[:, slot, :], scr["cw"][e_:e_ + 1, tk].partition_broadcast(128)
                                .rearrange("p a n -> p (a n)"), *deps, *free_cb.get(slot, ()))
                    else:
                        l = 32 + 2 * (e_ - 32)
                        G_.load(CB[0:64, slot, :], scr["cw"][l:l + 1, tk].partition_broadcast(64)
                                .rearrange("p a n -> p (a n)"), *deps, *free_cb.get(slot, ()))
                        G_.load(CB[64:128, slot, :], scr["cw"][l + 1:l + 2, tk].partition_broadcast(64)
                                .rearrange("p a n -> p (a n)"))
                    ct = G_.tok()
                for m in range(2):
                    bk = 2 * u + m
                    for c in range(2):
                        p = mm(PS[:, bk, :], WGU[:, m, c, e_, :], HT[:, c, tk], c == 0, c == 1, wl[e_],
                               *(pend if i < 2 else ()), *ht[4 * g4:4 * g4 + 4], *fr(("ps", bk)), sig=(c == 1))
                    if m == 0:
                        s = A(lambda e, bk=bk, u=u: e.activation(SG[:, u, :], PS[:, bk, :], ACT.Silu), p,
                              *fr(("SG", u)), *(pend if i < 2 else ()))
                        free[("ps", bk)] = [s]
                if e_ < 40:
                    v1 = V(lambda e, bk=bk, u=u, slot=slot: e.tensor_tensor(UU[:, u, :], PS[:, bk, :], CB[:, slot, :], ALU.mult),
                           p, ct, *fr(("UU", u)))
                    free[("ps", bk)] = [v1]
                    free_cb[slot] = [v1]
                    a_ = G(lambda e, u=u: e.tensor_tensor(AC[:, u, :], UU[:, u, :], SG[:, u, :], ALU.mult), v1, s,
                           *fr(("AC", u)))
                    free[("UU", u)] = [a_]
                else:
                    a_ = V(lambda e, bk=bk, u=u: e.tensor_tensor(AC[:, u, :], PS[:, bk, :], SG[:, u, :], ALU.mult),
                           p, s, *fr(("AC", u)))
                    free[("ps", bk)] = [a_]
                free[("SG", u)] = [a_]
                actt[i] = a_

            def down(i):
                e_, g4 = units[i]
                u = i % 2
                for j in range(4):
                    bk = 4 + 2 * (g4 % 2) + j // 2
                    p = mm(PS[:, bk, (j % 2) * 256:(j % 2) * 256 + 256], AC[:, u, j * 128:(j + 1) * 128], WD[:, e_, :],
                           e_ == 0 and j % 2 == 0, e_ == NU - 1, actt[i], *fr(("ps", bk)), sig=(j == 3))
                free[("AC", u)] = [p]
                if e_ == NU - 1:
                    for q in range(2):
                        bk = 4 + 2 * (g4 % 2) + q
                        t = 4 * g4 + 2 * q
                        v = V(lambda e, bk=bk, t=t: e.tensor_tensor(
                            X[:, t:t + 2, :], X[:, t:t + 2, :],
                            PS[:, bk, :].rearrange("p (a n) -> p a n", a=2), ALU.add), p)
                        free[("ps", bk)] = [v]

            for i in range(len(units) + 1):
                if i and rest:
                    load_units(*rest.pop(0))
                if i < len(units):
                    up(i)
                if i:
                    down(i - 1)
                if i < len(units):
                    now[0] = units[i][1]
                    bgstep(4)
            bgstep(10 ** 6)

        if True:
            moe()
        if True:
            xattn_heads("L1_xattn_", 16, 16, 0.25, True, False)

        def peer():
            phase()
            H = 8
            RW = ar.get(16, 64, parts=1)
            Mk = ar.get(2, 1024)
            s1 = ar.at
            Hn = ar.get(NT, D)
            gw = K.group("gpw")
            Wq = ar.get(2, 2048)
            WqT = ar.get(16, D)
            KY = ar.get(16, 64)
            gam = ar.get(16)
            bet = ar.get(16)
            gw.load(Wq, d["peer_wq"].rearrange("(c p) n -> p c n", p=128))
            gw.load(WqT, d["peer_wqT"].rearrange("(s p) n -> p s n", p=128))
            gw.load(KY, d["peer_keysT"])
            gw.load(gam, d["bn_gamma"])
            gw.load(bet, d["bn_beta"])
            w = gw.tok()
            end = Arena(mem, SIZE)
            end.at = SIZE - 2 * 8192 - 128
            gd = K.group("gpd")
            DT_ = end.get(2, 4096)
            UP = end.get(32, D)
            iota = end.get(128)
            gd.load(DT_, d["downT"].rearrange("(c p) n -> p c n", p=128))
            gd.load(UP, d["up_embed"].rearrange("(c p) n -> p c n", p=128))
            gd.load(iota, d["c_iota"].partition_broadcast(128).rearrange("p a n -> p (a n)"))
            ti = wd = gd.tok()
            ln_stats(X, tiles=QT4[0])
            ht = []
            for t in range(NT):
                if t % 4 == 2 and t < 12:
                    ln_stats(X, tiles=QT4[t // 4 + 1])
                a = ln_tile(Hn[:, t, :], X, t)
                ht.append(transpose_tile(Hn[:, t, :], t, a, 4 + t % 4)[1])
                for kc in range(2):
                    mm(PS[:, kc, 0:256], Hn[:, t, kc * 128:(kc + 1) * 128], Hn[:, t, :], t == 0, False)
                p = mm(PS[0:1, 2, 0:256], ones[:, 0:1], Hn[:, t, :], t == 0, t == NT - 1, t_ones, sig=True)
                for kc in range(2):
                    p = mm(PS[:, 3, 8 * kc:8 * kc + 1], Hn[:, t, kc * 128:(kc + 1) * 128], ones[:, 0:1],
                           t == 0 and kc == 0, t == NT - 1, sig=True)
            srow = ar.get(2, D, parts=1)
            mcol = ar.get(2)
            V(lambda e: e.tensor_copy(srow[:, 0, :], PS[0:1, 2, 0:256]), p)
            V(lambda e: e.tensor_scalar(srow[:, 1, :], PS[0:1, 2, 0:256], -1.0 / T, None, ALU.mult))
            a = V(lambda e: e.tensor_scalar(mcol, PS[:, 3, 0:16].rearrange("p (c n) -> p c n", c=2)[:, :, 0], 1.0 / T, None, ALU.mult))
            for kc in range(2):
                p = mm(PS[:, kc, 0:256], srow[:, 1, kc * 128:(kc + 1) * 128], srow[:, 0, :], False, True, a, sig=True)
            C = ar.get(2, D)
            a = A(lambda e: e.activation(C, PS[:, 0:2, 0:256], ACT.Copy), p)
            Gm = ar.get(2, 2048)
            for kc in range(2):
                for q in range(4):
                    bk = (kc * 4 + q) % 4
                    sl = slice(q * 512, (q + 1) * 512)
                    for c in range(2):
                        p = mm(PS[:, bk, :], C[:, c, kc * 128:(kc + 1) * 128], Wq[:, c, sl], c == 0, c == 1,
                               a, w, *fr(("ps", bk)), sig=(c == 1))
                    v = V(lambda e, kc=kc, sl=sl, bk=bk: e.tensor_tensor(Gm[:, kc, sl], PS[:, bk, :], Wq[:, kc, sl], ALU.mult), p)
                    free[("ps", bk)] = [v]
            for s in range(16):
                for c in range(2):
                    mm(PS[:, 4, s:s + 1], Gm[:, c, s * 128:(s + 1) * 128], ones[:, 0:1], s == 0 and c == 0,
                       c == 1, v, *fr(("ps", 4)))
            for s in range(16):
                for c in range(2):
                    p = mm(PS[:, 5, s:s + 1], Wq[:, c, s * 128:(s + 1) * 128], mcol[:, c:c + 1],
                           s == 0 and c == 0, c == 1, *fr(("ps", 5)), sig=(s == 15 and c == 1))
            av = ar.get(16)
            bv = ar.get(16)
            a = V(lambda e: e.tensor_scalar(av, PS[:, 4, 0:16], 1.0 / T, 1e-5, ALU.mult, ALU.add), p)
            a = A(lambda e: e.activation(av, av, ACT.Sqrt), a)
            V(lambda e: e.reciprocal(av, av), a)
            V(lambda e: e.tensor_tensor(av, av, gam, ALU.mult), w)
            V(lambda e: e.tensor_tensor(bv, PS[:, 5, 0:16], av, ALU.mult))
            V(lambda e: e.tensor_tensor(bv, bet, bv, ALU.subtract))
            KA = ar.get(16, 64)
            a = V(lambda e: e.tensor_tensor(KA, KY, bc(av, 2, (128, 16, 64)), ALU.mult))
            for kc in range(2):
                for s in range(16):
                    bk = 2 * kc + s // 8
                    p = mm(PS[:, bk, (s % 8) * 64:(s % 8) * 64 + 64], WqT[:, s, kc * 128:(kc + 1) * 128], KA[:, s, :],
                           True, True, a, *fr(("ps", bk)), sig=(s == 15))
                A(lambda e, kc=kc: e.activation(Mk[:, kc, :].rearrange("p (a n) -> p a n", a=2),
                                                PS[:, 2 * kc:2 * kc + 2, :], ACT.Copy), p)
            for s in range(16):
                p = mm(PS[0:1, 4 + s // 8, (s % 8) * 64:(s % 8) * 64 + 64], bv[:, s:s + 1], KY[:, s, :], True, True,
                       sig=(s == 15))
            A(lambda e: e.activation(RW.rearrange("p (a s) n -> p a (s n)", a=2), PS[0:1, 4:6, :], ACT.Copy), p)
            for key in K.q:
                K.q[key].append(([(K.sem[k], K.n[k]) for k in K.sem], lambda e: None, None))
            free.clear()
            ar.at = s1
            U32 = mybir.dt.uint32
            SXY = ar.get(2, 16, 64)
            GG = ar.get(2, 32, 256)
            OR = 2
            O = ar.get(OR, 128, 16, dt=F16)
            R = ar.get(OR, 32, 16, dt=F16)
            IDX = ar.get(4, 3, 128, dt=F16)
            IR = ar.get(128, 16, dt=F16)
            w1h = ar.get(64, dt=F16)
            tir = V(lambda e: e.tensor_copy(IR, bc(iota, 2, (128, 128, 16))), ti)
            sm_ = ar.get(16, 8)
            ixu = ar.get(16, 8, dt=I32).bitcast(U32)
            cand = ar.get(8, 64)
            top = ar.get(8, 8)
            pku = ar.get(8, 8, dt=I32).bitcast(U32)
            abu = ar.get(2, 64, dt=I32).bitcast(U32)
            EQ = cand.rearrange("p h (a b) -> p h a b", a=8)
            ij = ar.get(2, 64)
            w12 = ij[:, 0, :]
            rz = ar.get(8)
            e8 = ar.get(8, 8)
            TRS = ar.get(3, 2, 64)

            def sims(t):
                u = t % 2
                for q in range(2):
                    for c in range(2):
                        mm(PS[:, 0, :], HT[:, c, t * 128:(t + 1) * 128], Mk[:, c, q * 512:(q + 1) * 512], c == 0,
                           False, ht[t], *fr(("ps", 0)))
                    p = mm(PS[:, 0, :], ones[0:1, :], RW.rearrange("p (a s) n -> p a (s n)", a=2)[:, q, :],
                           False, True, sig=True)
                    e = A(lambda e, q=q: e.activation(
                        SXY[:, u, :, :].rearrange("p (a s) n -> p a (s n)", a=2)[:, q, :], PS[:, 0, :], ACT.Copy),
                        p, *fr(("SXY", u)))
                    free[("ps", 0)] = [e]
                return e

            def prep(t, st):
                u = t % 2
                for s in range(16):
                    (Vn if s else V)(lambda e, s=s: e.max(sm_[:, s, :], SXY[:, u, s, :]), st)
                for s in range(16):
                    v = (Vn if s else V)(lambda e, s=s: e.max_index(ixu[:, s, :], sm_[:, s, :], SXY[:, u, s, :]))
                free[("SXY", u)] = [v]
                V(lambda e: e.tensor_tensor(cand.rearrange("p h (a b) -> p h a b", a=8),
                                            sm_[:, 0:8, :].unsqueeze(3).to_broadcast([128, 8, 8, 8]),
                                            sm_[:, 8:16, :].unsqueeze(2).to_broadcast([128, 8, 8, 8]), ALU.add))
                for h in range(8):
                    (Vn if h else V)(lambda e, h=h: e.max(top[:, h, :], cand[:, h, :]))
                for h in range(8):
                    (Vn if h else V)(lambda e, h=h: e.max_index(pku[:, h, :], top[:, h, :], cand[:, h, :]))
                a = V(lambda e: e.tensor_tensor(e8, top, bc(top[:, :, 0], 2, (128, 8, 8)), ALU.subtract))
                a = A(lambda e: e.activation(e8, e8, ACT.Exp), a)
                pf = pku.rearrange("p h k -> p (h k)")
                V(lambda e: e.tensor_scalar(abu[:, 0, :], pf, 3, None, ALU.logical_shift_right))
                V(lambda e: e.tensor_scalar(abu[:, 1, :], pf, 7, None, ALU.bitwise_and))
                for m in range(2):
                    V(lambda e, m=m: e.tensor_tensor(
                        EQ, abu[:, m, :].rearrange("p (h k) -> p h k", h=8).unsqueeze(3).to_broadcast([128, 8, 8, 8]),
                        iota[:, 0:8].unsqueeze(1).unsqueeze(1).to_broadcast([128, 8, 8, 8]), ALU.is_equal), ti)
                    V(lambda e, m=m: e.tensor_tensor(
                        EQ, EQ, ixu[:, 8 * m:8 * m + 8, :].unsqueeze(2).to_broadcast([128, 8, 8, 8]), ALU.mult))
                    V(lambda e, m=m: e.tensor_reduce(ij[:, m, :].rearrange("p (h k) -> p h k", h=8), EQ, AX.X, ALU.add))
                V(lambda e: e.scalar_tensor_tensor(abu[:, 0, :], ij[:, 0, :], 64.0, ij[:, 1, :], ALU.mult, ALU.add))
                V(lambda e: e.tensor_scalar(abu[:, 1, :], abu[:, 0, :], 7, None, ALU.logical_shift_right))
                V(lambda e: e.tensor_scalar(abu[:, 0, :], abu[:, 0, :], 127, None, ALU.bitwise_and))
                V(lambda e: e.tensor_copy(TRS[:, 0:2, :, :], abu.unsqueeze(2).to_broadcast([128, 2, 2, 64])),
                  *fr("TRS"))
                V(lambda e: e.tensor_reduce(rz, e8, AX.X, ALU.add), a)
                V(lambda e: e.reciprocal(rz, rz))
                V(lambda e: e.tensor_scalar(rz, rz, WS, None, ALU.mult))
                V(lambda e: e.tensor_tensor(w12.rearrange("p (h k) -> p h k", h=8), e8, bc(rz, 2, (128, 8, 8)), ALU.mult))
                V(lambda e: e.tensor_copy(w1h, w12))
                V(lambda e: e.tensor_copy(TRS[:, 2, 0, :], w1h))
                return V(lambda e: e.tensor_tensor(TRS[:, 2, 1, :], w12, w1h, ALU.subtract))

            def turn(t, v):
                for m in range(3):
                    p = tr(PS[:, 0, m * 128:(m + 1) * 128], TRS[:, m, :, :].rearrange("p a b -> p (a b)"), ident, v,
                           *fr(("ps", 0)), sig=(m == 2))
                free["TRS"] = [p]
                e = A(lambda e: e.activation(IDX[:, t % 4, :, :], PS[:, 0, 0:384].rearrange("p (m n) -> p m n", m=3),
                                             ACT.Copy), p, *fr(("IDX", t % 4)))
                free[("ps", 0)] = [e]
                return e

            def scatter(t, it, gt, between, n_between=1):
                g2 = GG[:, (t // 2) % 2, :, :]
                ix = IDX[:, t % 4, :, :]
                for q in range(8):
                    r_ = q % OR
                    ts_ = slice(q * 16, q * 16 + 16)
                    ov = Vn(lambda e, r_=r_, ts_=ts_: e.tensor_tensor(O[:, r_, :, :], bc(ix[:, 0, ts_], 1, (128, 128, 16)),
                                                                IR, ALU.is_equal), it, tir, *fr(("O", r_)))
                    rv = Vn(lambda e, r_=r_, ts_=ts_: e.tensor_tensor(R[:, r_, :, :], bc(ix[:, 1, ts_], 1, (128, 32, 16)),
                                                                IR[:, 0:32, :], ALU.is_equal), it, tir, *fr(("O", r_)))
                    v = G(lambda e, r_=r_, ts_=ts_: e.tensor_tensor(R[:, r_, :, :], R[:, r_, :, :],
                                                                    bc(ix[:, 2, ts_], 1, (128, 32, 16)), ALU.mult), rv)
                    bk = 4 + q % 4
                    for i in range(16):
                        p = mm(PS[:, bk, i * 32:(i + 1) * 32], O[:, r_, :, i], R[:, r_, :, i], True, True, v, ov,
                               *fr(("ps", bk)), sig=(i == 15))
                    free[("O", r_)] = [p]
                    k = (t % 2) * 128 + q * 16
                    pv.append((g2[:, :, k:k + 16].rearrange("p c n -> p n c"), bk, p, gt))
                    for f in range(n_between):
                        if between:
                            between.pop(0)()
                    if len(pv) > 1:
                        apply_()
                free[("IDX", t % 4)] = [v, ov]

            pv = []
            last = {}

            def apply_():
                gv, bk, p, gt = pv.pop(0)
                w_ = Vn(lambda e: e.tensor_tensor(gv, gv, PS[:, bk, :].rearrange("p (n c) -> p n c", n=16),
                                                 ALU.mult), p, gt)
                free[("ps", bk)] = [w_]
                last["v"] = w_

            ghid = {}

            def hidden_steps(g_):
                u = g_ % 2

                def step(c2):
                    bk = 2 + c2 % 2
                    for h in range(2):
                        c = 2 * c2 + h
                        for kc in range(2):
                            p = mm(PS[:, bk, h * 256:(h + 1) * 256], DT_[:, kc, c * 128:(c + 1) * 128],
                                   HT[:, kc, g_ * 256:(g_ + 1) * 256], kc == 0, kc == 1, wd, ht[2 * g_], ht[2 * g_ + 1],
                                   *fr(("ps", bk)), sig=(h == 1 and kc == 1))
                    a = A(lambda e, bk=bk, c2=c2, u=u: e.activation(
                        GG[:, u, 2 * c2:2 * c2 + 2, :].rearrange("p a n -> p (a n)"), PS[:, bk, :],
                        ACT.Gelu_apprx_tanh), p, *fr(("GG", u)))
                    free[("ps", bk)] = [a]
                    ghid[g_] = a
                return [lambda c2=c2: step(c2) for c2 in range(16)]

            def outp(g_):
                u = g_ % 2
                for tl in range(2):
                    for c in range(32):
                        p = mm(PS[:, 1, tl * 256:(tl + 1) * 256], GG[:, u, c, tl * 128:(tl + 1) * 128], UP[:, c, :],
                               c == 0, c == 31, last["v"], *fr(("ps", 1)), sig=(c == 31))
                free[("GG", u)] = [p]
                return p

            def addx(g_, p):
                free[("ps", 1)] = [V(lambda e: e.scalar_tensor_tensor(
                    X[:, 2 * g_:2 * g_ + 2, :], PS[:, 1, :].rearrange("p (a n) -> p a n", a=2), 1.0 / WS,
                    X[:, 2 * g_:2 * g_ + 2, :], ALU.mult, ALU.add), p)]

            st = [sims(0), sims(1)]
            it = {}
            v0 = prep(0, st[0])
            for f in hidden_steps(0):
                f()
            it[0] = turn(0, v0)
            it[1] = turn(1, prep(1, st[1]))
            for g_ in range(8):
                nx = g_ + 1 < 8
                steps = hidden_steps(g_ + 1) if nx else []
                if nx:
                    st = [sims(2 * g_ + 2), sims(2 * g_ + 3)]
                for t in (2 * g_, 2 * g_ + 1):
                    scatter(t, it[t], ghid[g_], steps)
                apply_()
                for f in steps:
                    f()
                po = outp(g_)
                if nx:
                    for t in (2 * g_ + 2, 2 * g_ + 3):
                        it[t] = turn(t, prep(t, st[t % 2]))
                else:
                    ln_stats(X, tiles=range(14))
                addx(g_, po)

        if True:
            peer()

        top = Arena(mem, SIZE)
        top.at = SIZE - 18400
        l2f, l3a, l3w = {}, {}, {}
        for n, shape in (("q1", (2, 1024)), ("q2", (8, D)), ("sc1", (2, 1024)), ("sc2", (8, D)), ("b1c", (8,)),
                         ("vec", (2, D))):
            l3w[n] = top.get(*shape)
        l3w["b2r"] = top.get(D, parts=1)

        def load_l2f():
            g = K.group("gbf")
            Wf = l2f["Wf"] = [top.get(2, 1024), top.get(8, D)]
            l2f["Wq"] = [top.get(2, 1024, dt=BF16), top.get(8, D, dt=BF16)]
            l2f["b1b"] = top.get(1024)
            l2f["b2b"] = top.get(D)
            l2f["idb"] = top.get(128, dt=BF16)
            g.load(Wf[0], d["L2f_W1T"].rearrange("(c p) n -> p c n", p=128))
            g.load(Wf[1], d["L2f_W2T"].rearrange("(c p) n -> p c n", p=128))
            g.load(l2f["b1b"], d["L2f_b1"].partition_broadcast(128).rearrange("p a n -> p (a n)"))
            g.load(l2f["b2b"], d["L2f_b2"].partition_broadcast(128).rearrange("p a n -> p (a n)"))
            l2f["w"] = g.tok()
            for n in ("red", "ws", "wi"):
                l2f[n] = top.get(2)

        def ternary_sums():
            Wf, red, ws, wi = (l2f[n] for n in ("Wf", "red", "ws", "wi"))
            V(lambda e: e.tensor_copy(l2f["idb"], ident))
            for i in range(2):
                a = V(lambda e, i=i: e.tensor_reduce(red[:, i:i + 1], Wf[i].rearrange("p a b -> p (a b)"), AX.X, ALU.add,
                                                     apply_absolute_value=True), l2f["w"])
            l2f["red_t"] = a

        def ternary_weights():
            Wf, Wq, red, ws, wi = (l2f[n] for n in ("Wf", "Wq", "red", "ws", "wi"))
            p = mm(PS[:, 0, 0:2], ones, red, True, True, l2f["red_t"], *fr(("ps", 0)), sig=True)
            free[("ps", 0)] = [V(lambda e: e.tensor_scalar(ws, PS[:, 0, 0:2], 1.0 / (D * 1024), 1e-5, ALU.mult, ALU.max), p)]
            V(lambda e: e.reciprocal(wi, ws))
            V(lambda e: e.tensor_scalar(ws, ws, 1.0 / 127.0, None, ALU.mult))
            for i in range(2):
                fl = Wf[i].rearrange("p a b -> p (a b)")
                V(lambda e, i=i, fl=fl: e.tensor_scalar(fl, fl, wi[:, i:i + 1], MAGIC, ALU.mult, ALU.add))
                V(lambda e, fl=fl: e.tensor_scalar(fl, fl, -MAGIC, 1.0, ALU.add, ALU.min))
                l2f["wq"] = V(lambda e, i=i, fl=fl: e.tensor_scalar(Wq[i].rearrange("p a b -> p (a b)"), fl, -1.0, None,
                                                                    ALU.max))

        def load_l3x():
            g = K.group("gl3")
            for n, a_ in (("WK", top.get(2, D, parts=96)), ("WV", top.get(2, D, parts=96)), ("WQ", top.get(2, D)),
                          ("bkc", top.get(2)), ("bqc", top.get(2)), ("bvr", top.get(D, parts=1))):
                l3a[n] = a_
            g.load(l3a["WK"], d["L3_Wk"].rearrange("(c p) n -> p c n", p=96))
            g.load(l3a["WV"], d["L3_Wv"].rearrange("(c p) n -> p c n", p=96))
            g.load(l3a["WQ"], d["L3_WqT"].rearrange("(h p) n -> p h n", p=128))
            g.load(l3a["bkc"], d["L3_bk"])
            g.load(l3a["bqc"], d["L3_bq"])
            g.load(l3a["bvr"], d["L3_bv"])
            l3a["w"] = g.tok()

        def load_l3f():
            g = K.group("gl3f")
            sc1, sc2, vec = l3w["sc1"], l3w["sc2"], l3w["vec"]
            g.load(l3w["q1"].bitcast(I32), d["fc1_q"].rearrange("(c p) n -> p c n", p=128))
            g.load(l3w["q2"].bitcast(I32), d["fc2_q"].rearrange("(c p) n -> p c n", p=128))
            for c in range(2):
                g.load(sc1[:, c, :], d["fc1_scales"][c:c + 1, :].partition_broadcast(128).rearrange("p a n -> p (a n)"))
            for c in range(8):
                g.load(sc2[:, c, :], d["fc2_scales"][c:c + 1, :].partition_broadcast(128).rearrange("p a n -> p (a n)"))
            g.load(l3w["b1c"], d["fc1_bias"])
            g.load(l3w["b2r"], d["fc2_bias"])
            g.load(vec[:, 0, :], d["ln_gamma"].partition_broadcast(128).rearrange("p a n -> p (a n)"))
            g.load(vec[:, 1, :], d["ln_beta"].partition_broadcast(128).rearrange("p a n -> p (a n)"))
            l3w["w"] = g.tok()

        def dequant():
            f2 = lambda a_: a_.rearrange("p a b -> p (a b)")
            for q, sc in (("q1", "sc1"), ("q2", "sc2")):
                V(lambda e, q=q, sc=sc: e.scalar_tensor_tensor(f2(l3w[sc]), f2(l3w[q].bitcast(I32)), -128.0, f2(l3w[sc]),
                                                               ALU.add, ALU.mult), l3w["w"])

        def l2x():
            phase()
            gw = K.group("gl2")
            XT0 = ar.get(NT, D)
            X1 = ar.get(NT, D)
            AT = ar.get(T, parts=S2)
            ZF = ar.get(2, 1024, parts=S2)
            FB = ar.get(1024, parts=1)
            gin = ar.get(D)
            bin_ = ar.get(D)
            dsk = ar.get(D)
            mg = ar.get(1)
            s0 = ar.at
            K128 = ar.get(8, D)
            FF = ar.get(2, 8, 2, 128)
            FI = ar.get(8, 2, 2, 128)
            for o_, n_ in ((gin, "g_norm_in"), (bin_, "b_norm_in"), (dsk, "D_skip"), (mg, "mod_gate")):
                gw.load(o_, d["L2_" + n_].partition_broadcast(128).rearrange("p a n -> p (a n)"))
            gw.load(FB[:, 0:512], d["L2_b_film_in"])
            gw.load(FB[:, 512:1024], d["L2_b_film_out"])
            s1 = ar.at
            WK = ar.get(2, 128, parts=96)
            WV = ar.get(2, 256, parts=96)
            WQ = ar.get(4, D, parts=32)
            WF = ar.get(2, 1024)
            tm8 = ar.get(NT, dt=U8)
            tmf = ar.get(NT)
            gw.load(WK, d["L2_Wk"].rearrange("(c p) n -> p c n", p=96))
            gw.load(WV, d["L2_Wv"].rearrange("(c p) n -> p c n", p=96))
            gw.load(WQ, d["L2_WqT"].rearrange("(h p) n -> p h n", p=32))
            gw.load(WF[:, :, 0:512], d["L2_W_film_in"].rearrange("(c p) n -> p c n", p=128))
            gw.load(WF[:, :, 512:1024], d["L2_W_film_out"].rearrange("(c p) n -> p c n", p=128))
            gw.load(tm8, d["mask1T"])
            w = gw.tok()
            gk = K.group("gkm")
            for h in range(2):
                gk.load(tile4(K128, h), tok4(scr["K"])[h], *scr_done)
            gk.load(FF.rearrange("p j l r n -> p (j l r n)"), d["c_fwd"])
            gk.load(FI.rearrange("p l j r n -> p (l j r n)"), d["c_inv"])
            kt128 = gk.tok()
            ln_stats(X, tiles=range(14, 16))
            ht = []
            for t in range(NT):
                a = ln_tile(XT0[:, t, :], X, t)
                ht.append(transpose_tile(XT0[:, t, :], t, a, 4 + t % 4)[1])
            V(lambda e: e.tensor_copy(tmf, tm8), w)
            V(lambda e: e.tensor_scalar(tmf, tmf, 0.25, None, ALU.mult))
            KT = ar.get(4, 2 * S2, parts=32)
            VT = ar.get(2, 2 * S2)
            M = ar.get(2, 2, 4 * S2)
            kt = small_proj(KT, WK, 32, 4, w)
            vt = small_proj(VT, WV, 128, 2, w)
            mt = build_M(M, WQ, KT, 32, 4, 1, kt, w)
            for b in range(2):
                for q in range(2):
                    bk = 2 * b + q
                    for c in range(2):
                        p = mm(PS[0:S2, bk, :], VT[:, c, b * S2:(b + 1) * S2], WF[:, c, q * 512:(q + 1) * 512], c == 0,
                               c == 1, *vt, *fr(("ps", bk)), sig=(c == 1))
                    v = V(lambda e, b=b, q=q, bk=bk: e.tensor_scalar(ZF[:, b, q * 512:(q + 1) * 512], PS[0:S2, bk, :],
                                                                     mg[0:S2, 0:1], None, ALU.mult), p)
                    free[("ps", bk)] = [v]
            V(lambda e: e.tensor_scalar(FB, FB, mg[0:1, 0:1], None, ALU.mult))
            for o_ in (0, 512):
                zt = V(lambda e, o_=o_: e.tensor_scalar(FB[:, o_:o_ + 256], FB[:, o_:o_ + 256], 1.0, None, ALU.add))
            W = 4 * S2
            mrow, t_mrow = mask_row()
            SS = ar.get(2, W)
            SR = ar.get(2, W)
            EE = ar.get(2, W)
            mx = ar.get(2, 4, 8)
            t8 = ar.get(4, 8)
            sm = ar.get(2, 4)
            AM = ar.get(2, S2)
            h3 = lambda a_: a_.rearrange("p (h j) -> p h j", h=4)

            def scores(t):
                b, u = t // 8, t % 2
                k = ("ps", u)
                o = PS[:, u, 0:W]
                for c in range(2):
                    mm(o, HT[:, c, t * 128:(t + 1) * 128], M[:, c, b, :], c == 0, False, ht[t], *mt[-2:], *fr(k))
                p = mm(o, ones[0:1, :], mrow[:, b, 0:W], False, True, t_mrow, sig=True)
                a = A(lambda e: e.activation(SS[:, u, :], o, ACT.Copy), p, *fr(("SS", u)))
                free[k] = [a]
                return a

            def each(fn, *after):
                for h in range(4):
                    v = (Vn if h else V)(lambda e, h=h: fn(e, h, slice(h * S2, (h + 1) * S2)), *after)
                return v

            def select(t, a):
                u = t % 2
                each(lambda e, h, hs: e.max(mx[:, u, h, :], SS[:, u, hs]), a)
                v = V(lambda e: e.tensor_tensor(h3(EE[:, u, :]), h3(SS[:, u, :]), bc(mx[:, u, :, 0], 2, (128, 4, S2)),
                                                ALU.subtract), *fr(("EE", u)))
                x_ = A(lambda e: e.activation(EE[:, u, :], EE[:, u, :], ACT.Exp, scale=32.0 ** -0.5), v)
                v = each(lambda e, h, hs: e.match_replace(SR[:, 0, hs], mx[:, u, h, :], SS[:, u, hs], -3.0e38))
                free[("SS", u)] = [v]
                for r in range(3):
                    each(lambda e, h, hs, r=r: e.max(t8[:, h, :], SR[:, r % 2, hs]))
                    each(lambda e, h, hs, r=r: e.match_replace(SR[:, (r + 1) % 2, hs], t8[:, h, :], SR[:, r % 2, hs],
                                                               -3.0e38))
                V(lambda e: e.scalar_tensor_tensor(EE[:, u, :], SR[:, 1, :], -2.9e38, EE[:, u, :], ALU.is_le, ALU.mult), x_)
                V(lambda e: e.tensor_reduce(sm[:, u, :], h3(EE[:, u, :]), AX.X, ALU.add))
                V(lambda e: e.reciprocal(sm[:, u, :], sm[:, u, :]))
                v = V(lambda e: e.tensor_scalar(sm[:, u, :], sm[:, u, :], tmf[:, t:t + 1], None, ALU.mult))
                own = lambda: (K.sem["pool"], K.n["pool"])
                E4 = h3(EE[:, u, :])
                G(lambda e: e.tensor_tensor(E4, E4, bc(sm[:, u, :], 2, (128, 4, S2)), ALU.mult), v)
                G(lambda e: e.tensor_tensor(E4[:, 0:2], E4[:, 0:2], E4[:, 2:4], ALU.add), own())
                g_ = G(lambda e: e.tensor_tensor(AM[:, u, :], E4[:, 0], E4[:, 1], ALU.add), own(), *fr(("AM", u)))
                free[("EE", u)] = [g_]
                return g_

            a = scores(0)
            for t in range(NT):
                b, u = t // 8, t % 2
                nxt = scores(t + 1) if t + 1 < NT else None
                v = select(t, a)
                a = nxt
                p = tr(PS[0:S2, 2 + u, 0:128], AM[:, u, :], ident, v, *fr(("ps", 2 + u)), sig=True)
                free[("AM", u)] = [p]
                e_ = A(lambda e, t=t, u=u: e.activation(AT[:, t * 128:(t + 1) * 128], PS[0:S2, 2 + u, 0:128], ACT.Copy), p)
                free[("ps", 2 + u)] = [e_]
            ln_stats(XT0)
            for q in range(4):
                b, bk = q // 2, 4 * (q % 2)
                xs = X1[:, 4 * q:4 * q + 4, :]
                k = ("ps4", q % 2)
                for t in range(4 * q, 4 * q + 4):
                    v = ln_tile(X1[:, t, :], XT0, t)
                    mm(PS[:, bk + t % 4, :], AT[:, t * 128:(t + 1) * 128], ZF[:, b, 0:512], True, False, e_, zt,
                       *fr(k, *[("ps", i) for i in range(8)]))
                    p = mm(PS[:, bk + t % 4, :], ones[0:1, :], FB[:, 0:512], False, True, sig=True)
                V(lambda e, xs=xs: e.tensor_tensor(xs, xs, bc(gin, 1, (128, 4, D)), ALU.mult))
                V(lambda e, xs=xs: e.tensor_tensor(xs, xs, bc(bin_, 1, (128, 4, D)), ALU.add))
                V(lambda e, xs=xs, bk=bk: e.tensor_tensor(xs, xs, PS[:, bk:bk + 4, 0:256], ALU.mult), p)
                v = V(lambda e, xs=xs, bk=bk: e.tensor_tensor(xs, xs, PS[:, bk:bk + 4, 256:512], ALU.add))
                free[k] = [v]
            x1t = v
            all_ = [(K.sem[k], K.n[k]) for k in K.sem if K.n[k]]
            for key in K.q:
                K.q[key].append((list(all_), lambda e: None, None))
            free.clear()
            ar.at = s1
            s2 = s1

            def tt(o, a_, b_, op, *after):
                return V(lambda e: e.tensor_tensor(o, a_, b_, op), *after)

            Q = ar.get(2, 4, 2, 512)
            FK = ar.get(2, 4, 256)
            FX = ar.get(2, 4, 256)
            SD = ar.get(2, 2, 2, 256)
            TC = ar.get(2, 2, 256)
            MM = [HT.rearrange("p c n -> p (c n)"), ar.get(4096)]
            MM = [m_.rearrange("p (k r f n) -> p k r f n", k=2, r=2, n=256) for m_ in MM]
            ri = lambda a_: a_.rearrange("p s (r n) -> p s r n", r=2)

            def gg(o, a_, b_, op, *after):
                return G(lambda e: e.tensor_tensor(o, a_, b_, op), (K.sem["pool"], K.n["pool"]), *after)

            def spectrum(F, i, jb, rows, *after):
                u = i % 2
                k = ("spec", u)
                for s in range(4):
                    for r in range(2):
                        for h in range(2):
                            p = mm(PS[:, 4 * u + s, r * 256:(r + 1) * 256], FF[:, jb, 2 * s + h, r, :], rows(2 * s + h),
                                   h == 0, h == 1, kt128, *after, *fr(k), sig=(h == 1))
                a = A(lambda e: e.activation(TC, ri(PS[:, 4 * u + 2:4 * u + 4, :]), ACT.Copy), p, *fr("TC"))
                lo, hi = ri(PS[:, 4 * u:4 * u + 2, :]), TC
                tt(SD[:, 0, :, :, :], lo, hi, ALU.add, a)
                v = tt(SD[:, 1, :, :, :], lo, hi, ALU.subtract)
                free[k] = [v]
                free["TC"] = [v]
                (A_, C_), (B_, D_) = [[SD[:, x, y, :, :] for y in range(2)] for x in range(2)]
                tt(F[:, :, 0, :], A_, C_, ALU.add)
                tt(F[:, :, 2, :], A_, C_, ALU.subtract)
                tt(F[:, 0, 1, :], B_[:, 0, :], D_[:, 1, :], ALU.add)
                tt(F[:, 0, 3, :], B_[:, 0, :], D_[:, 1, :], ALU.subtract)
                tt(F[:, 1, 1, :], B_[:, 1, :], D_[:, 0, :], ALU.subtract)
                return tt(F[:, 1, 3, :], B_[:, 1, :], D_[:, 0, :], ALU.add)

            i = 0
            yt = []
            for jb in range(2):
                spectrum(FK, i, jb, lambda lt: K128[:, lt, :])
                i += 1
                for b in range(B):
                    spectrum(FX, i, jb, lambda lt, b=b: X1[:, b * 8 + lt, :], x1t)
                    i += 1
                    m = MM[b]
                    tt(m[:, 0, 0], FX[:, 0], FK[:, 0], ALU.mult, *fr(("MM", b)))
                    tt(m[:, 1, 0], FX[:, 1], FK[:, 1], ALU.mult)
                    tt(m[:, 0, 1], FX[:, 0], FK[:, 1], ALU.mult)
                    v = tt(m[:, 1, 1], FX[:, 1], FK[:, 0], ALU.mult)
                    add_ = tt if jb == 1 and b == 1 else gg
                    add_(m[:, 0, 0], m[:, 0, 0], m[:, 1, 0], ALU.subtract, v)
                    add_(m[:, 0, 1], m[:, 0, 1], m[:, 1, 1], ALU.add)
                    add_(m[:, 1, :, 0:2], m[:, 0, :, 0:2], m[:, 0, :, 2:4], ALU.add)
                    add_(m[:, 1, :, 2:4], m[:, 0, :, 0:2], m[:, 0, :, 2:4], ALU.subtract)
                    S_, D_ = m[:, 1, :, 0:2], m[:, 1, :, 2:4]
                    q = Q[:, jb, :, :, b * 256:(b + 1) * 256]
                    add_(q[:, 0], S_[:, :, 0], S_[:, :, 1], ALU.add)
                    add_(q[:, 2], S_[:, :, 0], S_[:, :, 1], ALU.subtract)
                    add_(q[:, 1, 0], D_[:, 0, 0], D_[:, 1, 1], ALU.subtract)
                    add_(q[:, 3, 0], D_[:, 0, 0], D_[:, 1, 1], ALU.add)
                    add_(q[:, 1, 1], D_[:, 1, 0], D_[:, 0, 1], ALU.add)
                    g_ = add_(q[:, 3, 1], D_[:, 1, 0], D_[:, 0, 1], ALU.subtract)
                    yt += [g_]
                    free[("MM", b)] = [g_]
            tmpb = FX.rearrange("p r (a b) n -> p (r a) b n", b=2)[:, 0:2]
            free[("tb", 0)] = free[("tb", 1)] = [g_]
            r2 = lambda a_: a_.rearrange("p (b n) -> p b n", b=2)
            for lt in range(8):
                u = lt % 2
                k = ("ps", u)
                for jb in range(2):
                    for r in range(2):
                        p = mm(PS[:, u, :], FI[:, lt, jb, r, :], Q[:, jb, lt // 2, r, :], jb == 0 and r == 0,
                               jb == 1 and r == 1, *yt, *fr(k, ("spec", 0)), sig=(jb == 1 and r == 1))
                tb = tmpb[:, u, :, :]
                two = lambda a_: a_.rearrange("p (b l) n -> p b l n", b=2)[:, :, lt, :]
                g_ = G(lambda e, tb=tb, x_=two(X1): e.tensor_tensor(tb, x_, bc(dsk, 1, (128, 2, D)), ALU.mult), x1t,
                       *fr(("tb", u)))
                k2 = ("psf", u)
                for b in range(2):
                    t = b * 8 + lt
                    mm(PS[:, 4 + 2 * u + b, :], AT[:, t * 128:(t + 1) * 128], ZF[:, b, 512:1024], True, False, *fr(k2),
                       *fr(("spec", 1)))
                    p2 = mm(PS[:, 4 + 2 * u + b, :], ones[0:1, :], FB[:, 512:1024], False, True, sig=True)
                fb = 4 + 2 * u
                v0 = tt(tb, tb, r2(PS[:, u, :]), ALU.add, p, g_)
                tt(tb, tb, PS[:, fb:fb + 2, 0:256], ALU.mult, p2)
                v1 = tt(tb, tb, PS[:, fb:fb + 2, 256:512], ALU.add)
                free[k2] = [v1]
                free[k] = [v0]
                free[("tb", u)] = [tt(two(XT0), two(XT0), tb, ALU.add)]
            for key in K.q:
                K.q[key].append(([(K.sem[k], K.n[k]) for k in K.sem], lambda e: None, None))
            free.clear()
            ar.at = s0
            gn = K.group("gn")
            vec = ar.get(4, D)
            W1 = ar.get(2, 1024)
            b1c = ar.get(8)
            W2 = ar.get(8, D)
            b2r = ar.get(D, parts=1)
            for i, n_ in enumerate(("g_ffn", "b_ffn", "g_norm_out", "b_norm_out")):
                gn.load(vec[:, i, :], d["L2_" + n_].partition_broadcast(128).rearrange("p a n -> p (a n)"))
            gn.load(W1, d["L2_W1"].rearrange("(c p) n -> p c n", p=128))
            gn.load(W2, d["L2_W2"].rearrange("(c p) n -> p c n", p=128))
            gn.load(b1c, d["L2_b1"])
            gn.load(b2r, d["L2_b2"])
            wn = gn.tok()
            load_l2f()
            load_l3x()
            Hb = ar.get(2, 4, D)
            ht = affine_T(Hb, XT0, vec, wn, lambda q: ln_stats(XT0, tiles=QT4[q]))

            def add(t, n, ps, p):
                v = tt(XT0[:, t:t + n, :], XT0[:, t:t + n, :], ps, ALU.add, p)
                if t % 4 == 2:
                    q = t // 4
                    u = q % 2
                    hb = Hb[:, u, :, :]
                    ln_stats(XT0, tiles=QT4[q])
                    for t in QT4[q]:
                        ln_tile(Hb[:, u, t % 4, :], XT0, t, *fr(("hb", u)))
                    tt(hb, hb, bc(vec[:, 2, :], 1, (128, 4, D)), ALU.mult)
                    tt(hb, hb, bc(vec[:, 3, :], 1, (128, 4, D)), ALU.add)
                    xs = X[:, 4 * q:4 * q + 4, :]
                    free[("hb", u)] = [tt(xs, xs, hb, ALU.add)]
                    ln_stats(X, tiles=QT4[q])
                return v

            ffn(W1, b1c, W2, b2r, wn, ht, ACT.Gelu, add, [ternary_sums, ternary_weights])

        def ffn(W1, b1c, W2, b2r, ready, ht, func, add, between=()):
            AT_ = ar.get(2, 8, 512)
            at = {}

            def up(g4):
                u = g4 % 2
                for f in range(8):
                    bk = f % 4
                    for c in range(2):
                        p = mm(PS[:, bk, :], W1[:, c, f * 128:(f + 1) * 128], HT[:, c, g4 * 512:(g4 + 1) * 512], c == 0,
                               c == 1, ready, *ht[4 * g4:4 * g4 + 4], *fr(("ps", bk)), sig=(c == 1))
                    a = A(lambda e, f=f, bk=bk, u=u: e.activation(AT_[:, u, f, :], PS[:, bk, :], func, bias=b1c[:, f:f + 1]),
                          p, *fr(("AT_", u)))
                    free[("ps", bk)] = [a]
                at[g4] = a

            def down(g4):
                u = g4 % 2
                for q in range(2):
                    bk = 4 + 2 * u + q
                    for j in range(2):
                        tl = 2 * q + j
                        o = PS[:, bk, j * 256:(j + 1) * 256]
                        for f in range(8):
                            mm(o, AT_[:, u, f, tl * 128:(tl + 1) * 128], W2[:, f, :], f == 0, False, at[g4],
                               *fr(("ps", bk)))
                        p = mm(o, ones[0:1, :], b2r, False, True, sig=True)
                    t = 4 * g4 + 2 * q
                    v = add(t, 2, PS[:, bk, :].rearrange("p (a n) -> p a n", a=2), p)
                    free[("ps", bk)] = [v]
                free[("AT_", u)] = [p]

            for i in range(5):
                if i < 4:
                    up(i)
                if i < len(between):
                    between[i]()
                if i:
                    down(i - 1)

        if True:
            l2x()

        def bitffn():
            phase()
            load_l3f()
            Wq, b1b, b2b, idb, ws, w, wq = (l2f[n] for n in ("Wq", "b1b", "b2b", "idb", "ws", "w", "wq"))
            Hq = ar.get(2, 4, D)
            Qq = ar.get(2, 4, D, dt=BF16)
            QT = ar.get(4, 4, 2, 128, dt=BF16)
            G1 = ar.get(2, 2, 1024)
            Q2 = ar.get(2, 2, 1024, dt=BF16)
            QT2 = ar.get(2, 8, 128, dt=BF16)
            Yb = ar.get(2, D)
            mx1, inv1, sc1, mx2, inv2, sc2 = (ar.get(NT) for _ in range(6))
            tk = {}

            def absmax(src, mx, inv, sc, w1, *after):
                V(lambda e: e.tensor_reduce(mx, src, AX.X, ALU.max, apply_absolute_value=True), *after)
                V(lambda e: e.tensor_scalar(mx, mx, 1e-5, None, ALU.max))
                V(lambda e: e.reciprocal(inv, mx))
                v = V(lambda e: e.tensor_scalar(inv, inv, 127.0, None, ALU.mult))
                Vn(lambda e: e.tensor_scalar(sc, mx, w1, None, ALU.mult))
                return v

            def first(q):
                u, sl = q % 2, slice(4 * q, 4 * q + 4)
                for t in QT4[q]:
                    ln_tile(Hq[:, u, t % 4, :], X, t, *fr(("hq", u)))
                absmax(Hq[:, u, :, :], mx1[:, sl], inv1[:, sl], sc1[:, sl], ws[:, 0:1])
                for t in QT4[q]:
                    h_ = Hq[:, u, t % 4, :]
                    (Vn if t % 4 else V)(lambda e, h_=h_, t=t: e.tensor_scalar(h_, h_, inv1[:, t:t + 1], MAGIC, ALU.mult,
                                                                               ALU.add))
                v = V(lambda e: e.tensor_scalar(Qq[:, u, :, :], Hq[:, u, :, :], -MAGIC, None, ALU.add), *fr(("qq", u)))
                free[("hq", u)] = [v]
                pb_ = PS[:, 4, :].bitcast(BF16)
                for t in range(4):
                    for c in range(2):
                        p = tr(pb_[:, (2 * t + c) * 128:(2 * t + c + 1) * 128], Qq[:, u, t, c * 128:(c + 1) * 128], idb, v,
                               *fr(("ps", 4)), sig=(t == 3 and c == 1))
                free[("qq", u)] = [p]
                tk["QT", q] = A(lambda e: e.activation(QT[:, q, :, :, :].rearrange("p t c n -> p (t c n)"), pb_, ACT.Copy), p)
                free[("ps", 4)] = [tk["QT", q]]

            def up(j):
                for u in range(2):
                    t = 2 * j + u
                    k = ("ps", 2 * u)
                    for q in range(2):
                        for c in range(2):
                            p = mm(PS[:, 2 * u + q, :], QT[:, t // 4, t % 4, c, :], Wq[0][:, c, q * 512:(q + 1) * 512],
                                   c == 0, c == 1, tk["QT", t // 4], wq, *fr(k), sig=(c == 1))
                    tk["up", t] = p

            def evacuate(j):
                for u in range(2):
                    t = 2 * j + u
                    g1 = G1[:, j % 2, u, :]
                    v = V(lambda e, g1=g1, t=t, u=u: e.scalar_tensor_tensor(
                        g1.rearrange("p (a n) -> p a n", a=2), PS[:, 2 * u:2 * u + 2, :], sc1[:, t:t + 1],
                        b1b.rearrange("p (a n) -> p a n", a=2), ALU.mult, ALU.add), tk["up", t], w)
                    free[("ps", 2 * u)] = [v]
                    tk["g", t] = A(lambda e, g1=g1: e.activation(g1, g1, ACT.Gelu), v)

            def scale2(j):
                sl = slice(2 * j, 2 * j + 2)
                v = absmax(G1[:, j % 2, :, :], mx2[:, sl], inv2[:, sl], sc2[:, sl], ws[:, 1:2], tk["g", 2 * j],
                           tk["g", 2 * j + 1])
                for u in range(2):
                    g1 = G1[:, j % 2, u, :]
                    tk["r", j] = A(lambda e, g1=g1, t=2 * j + u: e.activation(g1, g1, ACT.Copy, scale=inv2[:, t:t + 1],
                                                                             bias=MAGIC), v)

            def round2(j):
                h = j % 2
                tk["q2", j] = V(lambda e: e.tensor_scalar(Q2[:, h, :, :], G1[:, h, :, :], -MAGIC, None, ALU.add),
                                tk["r", j], *fr(("q2", h)))

            def down(j):
                for u in range(2):
                    pb_ = PS[:, 5 + u, :].bitcast(BF16)
                    for f in range(8):
                        p = tr(pb_[:, f * 128:(f + 1) * 128], Q2[:, j % 2, u, f * 128:(f + 1) * 128], idb, tk["q2", j],
                               *fr(("ps", 5 + u)), sig=(f == 7))
                    a = A(lambda e, u=u, pb_=pb_: e.activation(QT2[:, u, :, :].rearrange("p c n -> p (c n)"), pb_, ACT.Copy),
                          p, *fr(("QT2", u)))
                    free[("ps", 5 + u)] = [a]
                    tk["a", u] = a
                free[("q2", j % 2)] = [p]
                for u in range(2):
                    for f in range(8):
                        p = mm(PS[:, 7, u * 256:(u + 1) * 256], QT2[:, u, f, :], Wq[1][:, f, :], f == 0, f == 7, tk["a", u],
                               *fr(("ps", 7)), sig=(f == 7))
                    free[("QT2", u)] = [p]
                tk["down", j] = p

            def out2(j):
                for u in range(2):
                    t = 2 * j + u
                    v = V(lambda e, t=t, u=u: e.scalar_tensor_tensor(Yb[:, u, :], PS[:, 7, u * 256:(u + 1) * 256],
                                                                     sc2[:, t:t + 1], b2b, ALU.mult, ALU.add),
                          tk["down", j], *fr(("yb", u)))
                    free[("yb", u)] = [G(lambda e, t=t, u=u: e.tensor_tensor(X[:, t, :], X[:, t, :], Yb[:, u, :], ALU.add), v)]
                free[("ps", 7)] = [v]

            first(0)
            up(0)
            evacuate(0)
            first(1)
            for j in range(8):
                if j < 7:
                    up(j + 1)
                scale2(j)
                if j < 7:
                    evacuate(j + 1)
                round2(j)
                if j:
                    out2(j - 1)
                down(j)
                if j % 2 == 1 and j < 5:
                    first(j // 2 + 2)
                if j == 4:
                    dequant()
            out2(7)

        if True:
            bitffn()

        def l3x():
            phase()
            WK, WV, WQ, bkc, bqc, bvr, w = (l3a[n] for n in ("WK", "WV", "WQ", "bkc", "bqc", "bvr", "w"))
            KT = ar.get(2, 2 * S2)
            M = ar.get(2, 2, S2)
            Z = ar.get(1, 2, D)
            rb = ar.get(2, S2, parts=1)
            ht = layernorm_T(X)
            V(lambda e: e.memset(rb, 0.0), w)
            kt = small_proj(KT, WK, 128, 2, w, bias=bkc)
            mt = build_M(M, WQ, KT, 128, 1, 2, kt, w)
            for c in range(2):
                p = mm(PS[0:1, 2, 0:2 * S2], bqc[:, c:c + 1], KT[:, c, :], c == 0, c == 1, *kt, *fr(("ps", 2)), sig=(c == 1))
            rt = V(lambda e: e.tensor_copy(rb.rearrange("p b n -> p (b n)"), PS[0:1, 2, 0:2 * S2]), p)
            free[("ps", 2)] = [rt]
            for b in range(2):
                o = PS[0:S2, 3, b * 256:(b + 1) * 256]
                for c in range(2):
                    mm(o, ctxT[:, c, b * S2:(b + 1) * S2], WV[:, c, :], c == 0, False, w, *fr(("ps", 3)))
                p = mm(o, ones[0:1, 0:S2], bvr, False, True, sig=True)
            zt = V(lambda e: e.tensor_copy(Z[0:S2, 0, :, :], PS[0:S2, 3, :].rearrange("p (b n) -> p b n", b=2)), p)
            free[("ps", 3)] = [zt]
            attention(1, M, mt, rb, rt, 1.0, Z, [zt], None, None, ht)

        if True:
            l3x()

        def l3f():
            phase()
            W1, W2, b1c, b2r, vec, w = (l3w[n] for n in ("sc1", "sc2", "b1c", "b2r", "vec", "w"))
            R = ar.get(NT, D)

            def pre(q):
                ln_stats(X, tiles=QT4[q])
                for t in QT4[q]:
                    ln_tile(R[:, t, :], X, t)
                ln_stats(R, tiles=QT4[q])

            Hb = ar.get(2, 4, D)
            ht = affine_T(Hb, R, vec, w, pre)
            gb_out = K.group("gout")

            def add(t, n, ps, p):
                v0 = V(lambda e: e.scalar_tensor_tensor(R[:, t:t + n, :], ps, 0.5, R[:, t:t + n, :], ALU.mult, ALU.add), p)
                v = V(lambda e: e.tensor_tensor(X[:, t:t + n, :], X[:, t:t + n, :], R[:, t:t + n, :], ALU.add))
                gb_out.load(out[t // 8].rearrange("(h p s) c -> s p h c", p=128, s=4)[t % 8 // 2], X[:, t:t + n, :], v)
                return v0

            ffn(W1, b1c, W2, b2r, w, ht, ACT.Silu, add)

        if True:
            l3f()
        else:
            phase()
            go = K.group("gout")
            for b in range(B):
                for h in range(2):
                    go.load(tok4(out[b])[h], tile4(X[:, b * 8:b * 8 + 8, :], h))
        K.emit()


def constants():
    f = np.arange(256)
    p, t = np.arange(128), np.arange(8)
    l = (512 * (t % 2)[:, None] + 4 * p[None, :] + (t // 2)[:, None]).reshape(-1)
    th = 2 * np.pi * ((2 * f[None, :] + 1) * l[:, None] % 4096) / 4096.0
    co, si = np.cos(th), np.sin(th)
    fw = np.stack([co, -si], 0).reshape(2, 8, 128, 2, 128)
    iv = np.stack([co, -si], 0).transpose(0, 2, 1).reshape(2, 2, 128, 8, 128) * (2.0 / 2048)
    c = {}
    c["c_fwd"] = fw.transpose(2, 3, 1, 0, 4).reshape(128, 4096).astype(np.float32)
    c["c_inv"] = iv.transpose(2, 3, 1, 0, 4).reshape(128, 4096).astype(np.float32)
    c["c_iota"] = np.arange(128, dtype=np.float32)[None, :]
    c["c_ident"] = np.eye(128, dtype=np.float32)
    o = np.where(np.arange(128) < 64, 0.0, np.pi / 2)
    c["c_col"] = np.stack([o, np.pi - o, o + np.pi / 2, np.pi / 2 - o, np.pi / 2 - o, np.pi / 2 + o], 1).astype(np.float32)
    c["c_l32"] = np.concatenate([32.0 * np.arange(32), np.arange(32)])[None, :].astype(np.float32)
    return c


def layout(i):
    a = {}
    row = lambda v: v.reshape(1, -1)
    col = lambda v: np.ascontiguousarray(v.reshape(-1, 128).T)
    a["x"] = i["x"]
    a["ctxT"] = i["ctx_768"].transpose(2, 0, 1).reshape(192, 154)
    a["mask2"] = i["mask_BxS2_bf1"].view(np.uint8)
    a["mask1T"] = i["mask_BxS_bf1"].view(np.uint8).reshape(2, 2, 128, 4).transpose(2, 0, 3, 1).reshape(128, 16)
    for L in ("L0_xattn_", "L1_xattn_"):
        a[L + "Wk"] = i[L + "Wk"]
        a[L + "Wv"] = i[L + "Wv"]
        a[L + "WqT"] = i[L + "Wq"].T
        a[L + "Wo"] = i[L + "Wo"]
    a["L0_xattn_bo"] = row(i["L0_xattn_bo"])
    a["gwT"] = i["L0_ffn_gate_weight"].T
    a["gate_bias"] = row(i["L0_ffn_gate_bias"])

    def up(w, s, n):
        w = w.transpose(1, 0, 2).reshape(256, 32, 128)
        n = n.transpose(1, 0, 2).reshape(256, 8, 128)
        w = np.concatenate([w, n, s.reshape(256, 1, 128)], 1)
        return w.reshape(2, 128, 41 * 128).transpose(1, 0, 2).reshape(128, -1)

    a["moe_g"] = up(i["L0_ffn_w_gate"], i["L0_ffn_shared_w_gate"], i["L0_ffn_anchor_w_gate"])
    a["moe_u"] = up(i["L0_ffn_w_up"], i["L0_ffn_shared_w_up"], i["L0_ffn_anchor_w_up"])
    dn = np.concatenate([i["L0_ffn_w_down"], i["L0_ffn_anchor_w_down"].reshape(8, 128, 256),
                         i["L0_ffn_shared_w_down"][None]], 0)
    a["moe_d"] = dn.transpose(1, 0, 2).reshape(128, -1)
    a["peer_wq"] = i["L1_ffn_w_q"]
    a["peer_wqT"] = i["L1_ffn_w_q"].T
    k = i["L1_ffn_keys"]
    a["peer_keysT"] = k.transpose(3, 2, 0, 1).reshape(128, 16, 64)
    a["bn_gamma"] = col(i["L1_ffn_bn_gamma"])
    a["bn_beta"] = col(i["L1_ffn_bn_beta"])
    a["downT"] = i["L1_ffn_down_embed"].T
    a["up_embed"] = i["L1_ffn_up_embed"]
    X = "L2_xattn_"
    for n in ("Wk", "Wv", "W_film_in", "W_film_out", "W1", "W2"):
        a["L2_" + n] = i[X + n]
    a["L2_WqT"] = i[X + "Wq"].T
    for n in ("g_norm_in", "b_norm_in", "D_skip", "mod_gate", "b_film_in", "b_film_out", "g_norm_out", "b_norm_out",
              "g_ffn", "b_ffn", "log_dt", "b2"):
        a["L2_" + n] = row(i[X + n])
    a["L2_b1"] = col(i[X + "b1"])
    for n in ("A_re", "A_im", "C_re", "C_im"):
        a["L2_" + n + "T"] = i[X + n].T
    a["L2f_W1T"] = i["L2_ffn_W1"].T
    a["L2f_W2T"] = i["L2_ffn_W2"].T
    a["L2f_b1"] = row(i["L2_ffn_b1"])
    a["L2f_b2"] = row(i["L2_ffn_b2"])
    X = "L3_xattn_"
    a["L3_Wk"] = i[X + "Wk"]
    a["L3_Wv"] = i[X + "Wv"]
    a["L3_WqT"] = i[X + "Wq"].T
    a["L3_bk"] = col(i[X + "bk"])
    a["L3_bq"] = col(i[X + "bq"])
    a["L3_bv"] = row(i[X + "bv"])
    X = "L3_ffn_"
    for n in ("fc1_q", "fc2_q", "fc1_scales", "fc2_scales"):
        a[n] = i[X + n]
    a["fc1_bias"] = col(i[X + "fc1_bias"])
    a["fc2_bias"] = row(i[X + "fc2_bias"])
    a["ln_gamma"] = row(i[X + "ln_gamma"])
    a["ln_beta"] = row(i[X + "ln_beta"])
    return a


def kernel(**inputs):
    import concourse.bacc as _bacc
    from concourse import mybir as _mybir
    from concourse.bass_utils import run_bass_kernel_spmd as _run

    nc = _bacc.Bacc("TRN2", target_bir_lowering=False, num_devices=1)
    arrays, aps = {}, {}
    data = layout({k: np.asarray(v) for k, v in inputs.items()})
    data.update(constants())
    for name, a in data.items():
        a = np.ascontiguousarray(a)
        arrays["in_" + name] = a
        aps[name] = nc.dram_tensor("in_" + name, a.shape, _mybir.dt.from_np(a.dtype), kind="ExternalInput").ap()
    o = nc.dram_tensor("out_0_dram", (2, 1024, 256), _mybir.dt.float32, kind="ExternalOutput").ap()
    program(nc, aps, o)
    r = _run(nc, [arrays], core_ids=[0])
    return r.results[0]["out_0_dram"]
```
